# Optimizing a Trainium2 kernel written in Bass

```python
import numpy as np
import jax
import jax.numpy as jnp

def _softmax(x, axis=-1):
    return jax.nn.softmax(x, axis=axis)

def _gelu(x):
    return jax.nn.gelu(x, approximate=True)

def _silu(x):
    return jax.nn.silu(x)

def _sigmoid(x):
    return jax.nn.sigmoid(x)

def _layernorm(x, axis=-1, eps=1e-05):
    m = jnp.mean(x, axis=axis, keepdims=True)
    v = jnp.var(x, axis=axis, keepdims=True)
    return (x - m) / jnp.sqrt(v + eps)

def _scatter_add(tgt, idx, src, axis=0):
    return tgt.at[idx].add(src)

def _segment_sum(src, seg, n):
    return jax.ops.segment_sum(src, seg, n)
kernel_name = 'mk_cond_seq_d4_seqx_r4_dba1d1'

def setup_inputs(seed: int=0):
    np.random.seed(seed)
    _w = jnp.asarray

    def _rec_inputs():
        import jax
        import jax.numpy as jnp
        _rk = jax.random.key(seed)
        x = -0.0003929 + 0.9999 * jax.random.normal(jax.random.fold_in(_rk, 1), (16, 256, 256), jnp.float32)
        _lenS = 256 - jax.random.randint(jax.random.fold_in(_rk, 7), (16,), 0, max(1, 256 // 4) + 1, jnp.int32)
        _lenS2 = 256 - jax.random.randint(jax.random.fold_in(_rk, 8), (16,), 0, max(1, 256 // 4) + 1, jnp.int32)
        cond_1024 = 0.00386106 + 1.00199 * jax.random.normal(jax.random.fold_in(_rk, 11), (16, 256), jnp.float32)
        return (x, cond_1024)
    x, cond_1024 = _rec_inputs()

    def _L0_cond_setup():
        import jax, jax.numpy as jnp
        import numpy as np
        FEAT = 256
        ADA = 256
        INTER = 256
        RANK = 8
        EPS = 1e-05

        def _layernorm(a, g, b):
            mu = jnp.mean(a, axis=-1, keepdims=True)
            var = jnp.mean(jnp.square(a - mu), axis=-1, keepdims=True)
            return (a - mu) * jax.lax.rsqrt(var + EPS) * g + b
        key = jax.random.key(seed)
        ks = jax.random.split(key, 6)
        B, T = (16, 256)
        x = jax.random.normal(ks[0], (B, T, FEAT), dtype=jnp.float32)
        ada_emb = jax.random.normal(ks[1], (B, ADA), dtype=jnp.float32)
        W1 = jax.random.normal(ks[2], (ADA, INTER), dtype=jnp.float32) / np.sqrt(ADA)
        b1 = jnp.zeros((INTER,), dtype=jnp.float32)
        W2 = jax.random.normal(ks[3], (INTER, FEAT * RANK * 4), dtype=jnp.float32) * (0.1 / np.sqrt(INTER))
        b2 = jnp.zeros((FEAT * RANK * 4,), dtype=jnp.float32)
        ln_g = jnp.ones((ADA,), dtype=jnp.float32)
        ln_b = jnp.zeros((ADA,), dtype=jnp.float32)
        return {'x': x, 'ada_emb': ada_emb, 'ln_g': ln_g, 'ln_b': ln_b, 'W1': W1, 'b1': b1, 'W2': W2, 'b2': b2}
    _L0_cond_all = _L0_cond_setup()
    _L0_cond_in = {k: v for k, v in _L0_cond_all.items() if k in ('ln_g', 'ln_b', 'W1', 'b1', 'W2', 'b2')}
    del _L0_cond_all

    def _L1_cond_setup():
        import jax, jax.numpy as jnp
        import numpy as np
        B, L, D_MODEL, COND = (2, 512, 256, 256)
        D_STATE, EXPAND = (64, 2)
        D_INNER = EXPAND * D_MODEL
        MLP_H = 2 * D_MODEL
        EPS = 1e-05

        def _adaln(x, c, w, b):
            mod = (c @ w + b)[:, None, :]
            shift, scale, gate = jnp.split(mod, 3, axis=-1)
            mu = jnp.mean(x, axis=-1, keepdims=True)
            var = jnp.var(x, axis=-1, keepdims=True)
            normed = (x - mu) * jax.lax.rsqrt(var + EPS) * (1.0 + scale) + shift
            return (normed, gate)

        def _ssm(h, in_w, xproj_w, dt_bias, A_log, Dskip, out_w):
            xz = h @ in_w
            xs, z = jnp.split(xz, 2, axis=-1)
            xs = jax.nn.silu(xs)
            proj = xs @ xproj_w
            dt = jax.nn.softplus(proj[..., :D_INNER] + dt_bias)
            Bm = proj[..., D_INNER:D_INNER + D_STATE]
            Cm = proj[..., D_INNER + D_STATE:]
            A = -jnp.exp(A_log)

            def step(hst, ins):
                dt_t, B_t, C_t, x_t = ins
                dA = jnp.exp(dt_t[:, :, None] * A)
                hst = hst * dA + (dt_t * x_t)[:, :, None] * B_t[:, None, :]
                y_t = jnp.einsum('bds,bs->bd', hst, C_t)
                return (hst, y_t)
            tm = lambda a: jnp.swapaxes(a, 0, 1)
            h0 = jnp.zeros((h.shape[0], D_INNER, D_STATE), h.dtype)
            _, ys = jax.lax.scan(step, h0, (tm(dt), tm(Bm), tm(Cm), tm(xs)))
            y = jnp.swapaxes(ys, 0, 1) + xs * Dskip
            return y * jax.nn.silu(z) @ out_w
        key = jax.random.key(seed)
        ks = jax.random.split(key, 24)
        p = lambda i, shape, s=0.02: jax.random.normal(ks[i], shape, jnp.float32) * s
        inp = {'x': jax.random.normal(ks[0], (B, L, D_MODEL), jnp.float32), 'c': jax.random.normal(ks[1], (B, COND), jnp.float32), 'adaln_mamba_w': p(2, (COND, 3 * D_MODEL)), 'adaln_mamba_b': jnp.zeros((3 * D_MODEL,), jnp.float32), 'adaln_mlp_w': p(3, (COND, 3 * D_MODEL)), 'adaln_mlp_b': jnp.zeros((3 * D_MODEL,), jnp.float32), 'mlp_w1': p(4, (D_MODEL, MLP_H)), 'mlp_w2': p(5, (D_MODEL, MLP_H)), 'mlp_w3': p(6, (MLP_H, D_MODEL))}
        a_init = jnp.log(jnp.tile(jnp.arange(1, D_STATE + 1, dtype=jnp.float32), (D_INNER, 1)))
        for j, pre in enumerate(['fwd', 'bwd']):
            o = 7 + 6 * j
            inp[f'{pre}_in_w'] = p(o, (D_MODEL, 2 * D_INNER))
            inp[f'{pre}_xproj_w'] = p(o + 1, (D_INNER, D_INNER + 2 * D_STATE))
            inp[f'{pre}_dt_bias'] = jnp.zeros((D_INNER,), jnp.float32)
            inp[f'{pre}_A_log'] = a_init
            inp[f'{pre}_D'] = jnp.ones((D_INNER,), jnp.float32)
            inp[f'{pre}_out_w'] = p(o + 2, (D_INNER, D_MODEL))
        return inp
    _L1_cond_all = _L1_cond_setup()
    _L1_cond_in = {k: v for k, v in _L1_cond_all.items() if k in ('adaln_mamba_w', 'adaln_mamba_b', 'adaln_mlp_w', 'adaln_mlp_b', 'mlp_w1', 'mlp_w2', 'mlp_w3', 'fwd_in_w', 'fwd_xproj_w', 'fwd_dt_bias', 'fwd_A_log', 'fwd_D', 'fwd_out_w', 'bwd_in_w', 'bwd_xproj_w', 'bwd_dt_bias', 'bwd_A_log', 'bwd_D', 'bwd_out_w')}
    del _L1_cond_all

    def _L2_cond_setup():
        import jax, jax.numpy as jnp
        import numpy as np
        B, T, DIM = (4, 256, 256)
        COND = 256
        HEADS, DH = (16, 64)
        INNER = HEADS * DH
        MLP = 1024
        EPS = 1e-05

        def _layernorm(x):
            mu = jnp.mean(x, axis=-1, keepdims=True)
            var = jnp.mean(jnp.square(x - mu), axis=-1, keepdims=True)
            return (x - mu) * jax.lax.rsqrt(var + EPS)

        def _modulate(x, shift, scale):
            return x * (1.0 + scale) + shift

        def _attention(x, W_qkv, W_out, b_out):
            Bq, Tq, _ = x.shape
            qkv = x @ W_qkv
            q, k, v = jnp.split(qkv, 3, axis=-1)
            q = q.reshape(Bq, Tq, HEADS, DH)
            k = k.reshape(Bq, Tq, HEADS, DH)
            v = v.reshape(Bq, Tq, HEADS, DH)
            scale = DH ** (-0.5)
            attn = jnp.einsum('bqhd,bkhd->bhqk', q, k) * scale
            attn = jax.nn.softmax(attn, axis=-1)
            out = jnp.einsum('bhqk,bkhd->bqhd', attn, v).reshape(Bq, Tq, INNER)
            return out @ W_out + b_out

        def _ff(x, W1, b1, W2, b2):
            return jax.nn.gelu(x @ W1 + b1, approximate=False) @ W2 + b2
        key = jax.random.key(seed)
        ks = jax.random.split(key, 12)
        s = 0.02
        return {'x': jax.random.normal(ks[0], (B, T, DIM), jnp.float32), 'c': jax.random.normal(ks[1], (B, 1, COND), jnp.float32), 'W_mod': jax.random.normal(ks[2], (COND, 6 * DIM), jnp.float32) * s, 'b_mod': jax.random.normal(ks[3], (6 * DIM,), jnp.float32) * s, 'W_qkv': jax.random.normal(ks[4], (DIM, 3 * INNER), jnp.float32) * s, 'W_out': jax.random.normal(ks[5], (INNER, DIM), jnp.float32) * s, 'b_out': jax.random.normal(ks[6], (DIM,), jnp.float32) * s, 'W1': jax.random.normal(ks[7], (DIM, MLP), jnp.float32) * s, 'b1': jax.random.normal(ks[8], (MLP,), jnp.float32) * s, 'W2': jax.random.normal(ks[9], (MLP, DIM), jnp.float32) * s, 'b2': jax.random.normal(ks[10], (DIM,), jnp.float32) * s}
    _L2_cond_all = _L2_cond_setup()
    _L2_cond_in = {k: v for k, v in _L2_cond_all.items() if k in ('W_mod', 'b_mod', 'W_qkv', 'W_out', 'b_out', 'W1', 'b1', 'W2', 'b2')}
    del _L2_cond_all

    def _L3_cond_setup():
        import jax, jax.numpy as jnp
        import numpy as np
        D = 256
        H = 16
        HD = D // H
        MLP = 4 * D

        def _lin(key, fin, fout):
            k1, k2 = jax.random.split(key)
            lim = 1.0 / np.sqrt(fin)
            W = jax.random.uniform(k1, (fin, fout), minval=-lim, maxval=lim, dtype=jnp.float32)
            b = jax.random.uniform(k2, (fout,), minval=-lim, maxval=lim, dtype=jnp.float32)
            return (W, b)

        def layernorm(x, g, b, eps=1e-05):
            mu = jnp.mean(x, axis=-1, keepdims=True)
            var = jnp.var(x, axis=-1, keepdims=True)
            return (x - mu) * jax.lax.rsqrt(var + eps) * g + b

        def attention(h, Wqkv, bqkv, Wproj, bproj):
            B, L, _ = h.shape
            qkv = (h @ Wqkv + bqkv).reshape(B, L, 3, H, HD)
            q, k, v = jnp.moveaxis(qkv, 2, 0)
            scale = HD ** (-0.5)
            attn = jnp.einsum('blhd,bmhd->bhlm', q, k) * scale
            attn = jax.nn.softmax(attn, axis=-1)
            out = jnp.einsum('bhlm,bmhd->blhd', attn, v).reshape(B, L, D)
            return out @ Wproj + bproj
        key = jax.random.key(seed)
        ks = jax.random.split(key, 10)
        x = jax.random.normal(ks[0], (4, 512, D), dtype=jnp.float32)
        time_emb = jax.random.normal(ks[1], (4, D), dtype=jnp.float32)
        Wqkv, bqkv = _lin(ks[2], D, 3 * D)
        Wproj, bproj = _lin(ks[3], D, D)
        W1, b1 = _lin(ks[4], D, MLP)
        W2, b2 = _lin(ks[5], MLP, D)
        Wt, bt = _lin(ks[6], D, 6 * D)
        g1 = jnp.ones((D,), jnp.float32)
        be1 = jnp.zeros((D,), jnp.float32)
        g2 = jnp.ones((D,), jnp.float32)
        be2 = jnp.zeros((D,), jnp.float32)
        return {'x': x, 'time_emb': time_emb, 'Wqkv': Wqkv, 'bqkv': bqkv, 'Wproj': Wproj, 'bproj': bproj, 'W1': W1, 'b1': b1, 'W2': W2, 'b2': b2, 'Wt': Wt, 'bt': bt, 'g1': g1, 'be1': be1, 'g2': g2, 'be2': be2}
    _L3_cond_all = _L3_cond_setup()
    _L3_cond_in = {k: v for k, v in _L3_cond_all.items() if k in ('Wqkv', 'bqkv', 'Wproj', 'bproj', 'W1', 'b1', 'W2', 'b2', 'Wt', 'bt', 'g1', 'be1', 'g2', 'be2')}
    del _L3_cond_all
    return {'x': x, 'cond_1024': cond_1024, 'L0_cond_ln_g': _L0_cond_in['ln_g'], 'L0_cond_ln_b': _L0_cond_in['ln_b'], 'L0_cond_W1': _L0_cond_in['W1'], 'L0_cond_b1': _L0_cond_in['b1'], 'L0_cond_W2': _L0_cond_in['W2'], 'L0_cond_b2': _L0_cond_in['b2'], 'L1_cond_adaln_mamba_w': _L1_cond_in['adaln_mamba_w'], 'L1_cond_adaln_mamba_b': _L1_cond_in['adaln_mamba_b'], 'L1_cond_adaln_mlp_w': _L1_cond_in['adaln_mlp_w'], 'L1_cond_adaln_mlp_b': _L1_cond_in['adaln_mlp_b'], 'L1_cond_mlp_w1': _L1_cond_in['mlp_w1'], 'L1_cond_mlp_w2': _L1_cond_in['mlp_w2'], 'L1_cond_mlp_w3': _L1_cond_in['mlp_w3'], 'L1_cond_fwd_in_w': _L1_cond_in['fwd_in_w'], 'L1_cond_fwd_xproj_w': _L1_cond_in['fwd_xproj_w'], 'L1_cond_fwd_dt_bias': _L1_cond_in['fwd_dt_bias'], 'L1_cond_fwd_A_log': _L1_cond_in['fwd_A_log'], 'L1_cond_fwd_D': _L1_cond_in['fwd_D'], 'L1_cond_fwd_out_w': _L1_cond_in['fwd_out_w'], 'L1_cond_bwd_in_w': _L1_cond_in['bwd_in_w'], 'L1_cond_bwd_xproj_w': _L1_cond_in['bwd_xproj_w'], 'L1_cond_bwd_dt_bias': _L1_cond_in['bwd_dt_bias'], 'L1_cond_bwd_A_log': _L1_cond_in['bwd_A_log'], 'L1_cond_bwd_D': _L1_cond_in['bwd_D'], 'L1_cond_bwd_out_w': _L1_cond_in['bwd_out_w'], 'L2_cond_W_mod': _L2_cond_in['W_mod'], 'L2_cond_b_mod': _L2_cond_in['b_mod'], 'L2_cond_W_qkv': _L2_cond_in['W_qkv'], 'L2_cond_W_out': _L2_cond_in['W_out'], 'L2_cond_b_out': _L2_cond_in['b_out'], 'L2_cond_W1': _L2_cond_in['W1'], 'L2_cond_b1': _L2_cond_in['b1'], 'L2_cond_W2': _L2_cond_in['W2'], 'L2_cond_b2': _L2_cond_in['b2'], 'L3_cond_Wqkv': _L3_cond_in['Wqkv'], 'L3_cond_bqkv': _L3_cond_in['bqkv'], 'L3_cond_Wproj': _L3_cond_in['Wproj'], 'L3_cond_bproj': _L3_cond_in['bproj'], 'L3_cond_W1': _L3_cond_in['W1'], 'L3_cond_b1': _L3_cond_in['b1'], 'L3_cond_W2': _L3_cond_in['W2'], 'L3_cond_b2': _L3_cond_in['b2'], 'L3_cond_Wt': _L3_cond_in['Wt'], 'L3_cond_bt': _L3_cond_in['bt'], 'L3_cond_g1': _L3_cond_in['g1'], 'L3_cond_be1': _L3_cond_in['be1'], 'L3_cond_g2': _L3_cond_in['g2'], 'L3_cond_be2': _L3_cond_in['be2']}

def reference(x, cond_1024, L0_cond_ln_g, L0_cond_ln_b, L0_cond_W1, L0_cond_b1, L0_cond_W2, L0_cond_b2, L1_cond_adaln_mamba_w, L1_cond_adaln_mamba_b, L1_cond_adaln_mlp_w, L1_cond_adaln_mlp_b, L1_cond_mlp_w1, L1_cond_mlp_w2, L1_cond_mlp_w3, L1_cond_fwd_in_w, L1_cond_fwd_xproj_w, L1_cond_fwd_dt_bias, L1_cond_fwd_A_log, L1_cond_fwd_D, L1_cond_fwd_out_w, L1_cond_bwd_in_w, L1_cond_bwd_xproj_w, L1_cond_bwd_dt_bias, L1_cond_bwd_A_log, L1_cond_bwd_D, L1_cond_bwd_out_w, L2_cond_W_mod, L2_cond_b_mod, L2_cond_W_qkv, L2_cond_W_out, L2_cond_b_out, L2_cond_W1, L2_cond_b1, L2_cond_W2, L2_cond_b2, L3_cond_Wqkv, L3_cond_bqkv, L3_cond_Wproj, L3_cond_bproj, L3_cond_W1, L3_cond_b1, L3_cond_W2, L3_cond_b2, L3_cond_Wt, L3_cond_bt, L3_cond_g1, L3_cond_be1, L3_cond_g2, L3_cond_be2):
    import jax
    import jax.numpy as jnp

    def _L0_cond_ref(x, ada_emb, ln_g, ln_b, W1, b1, W2, b2):
        import jax, jax.numpy as jnp
        import numpy as np
        FEAT = 256
        ADA = 256
        INTER = 256
        RANK = 8
        EPS = 1e-05

        def _layernorm(a, g, b):
            mu = jnp.mean(a, axis=-1, keepdims=True)
            var = jnp.mean(jnp.square(a - mu), axis=-1, keepdims=True)
            return (a - mu) * jax.lax.rsqrt(var + EPS) * g + b
        B, T, D = x.shape
        h = jax.nn.gelu(_layernorm(ada_emb, ln_g, ln_b) @ W1 + b1, approximate=False)
        w = h @ W2 + b2
        a1, bb1, a2, bb2 = jnp.split(w, 4, axis=-1)
        a1 = a1.reshape(B, D, RANK)
        bb1 = bb1.reshape(B, D, RANK)
        a2 = a2.reshape(B, D, RANK)
        bb2 = bb2.reshape(B, D, RANK)
        y = jnp.einsum('btd,bdr->btr', x, a1)
        y = jnp.einsum('btr,bdr->btd', y, bb1)
        y = jax.nn.gelu(y, approximate=False)
        y = jnp.einsum('btd,bdr->btr', y, a2)
        y = jnp.einsum('btr,bdr->btd', y, bb2)
        return y + x

    def _L1_cond_ref(x, c, adaln_mamba_w, adaln_mamba_b, adaln_mlp_w, adaln_mlp_b, mlp_w1, mlp_w2, mlp_w3, fwd_in_w, fwd_xproj_w, fwd_dt_bias, fwd_A_log, fwd_D, fwd_out_w, bwd_in_w, bwd_xproj_w, bwd_dt_bias, bwd_A_log, bwd_D, bwd_out_w):
        import jax, jax.numpy as jnp
        import numpy as np
        B, L, D_MODEL, COND = (2, 512, 256, 256)
        D_STATE, EXPAND = (64, 2)
        D_INNER = EXPAND * D_MODEL
        MLP_H = 2 * D_MODEL
        EPS = 1e-05

        def _adaln(x, c, w, b):
            mod = (c @ w + b)[:, None, :]
            shift, scale, gate = jnp.split(mod, 3, axis=-1)
            mu = jnp.mean(x, axis=-1, keepdims=True)
            var = jnp.var(x, axis=-1, keepdims=True)
            normed = (x - mu) * jax.lax.rsqrt(var + EPS) * (1.0 + scale) + shift
            return (normed, gate)

        def _ssm(h, in_w, xproj_w, dt_bias, A_log, Dskip, out_w):
            xz = h @ in_w
            xs, z = jnp.split(xz, 2, axis=-1)
            xs = jax.nn.silu(xs)
            proj = xs @ xproj_w
            dt = jax.nn.softplus(proj[..., :D_INNER] + dt_bias)
            Bm = proj[..., D_INNER:D_INNER + D_STATE]
            Cm = proj[..., D_INNER + D_STATE:]
            A = -jnp.exp(A_log)

            def step(hst, ins):
                dt_t, B_t, C_t, x_t = ins
                dA = jnp.exp(dt_t[:, :, None] * A)
                hst = hst * dA + (dt_t * x_t)[:, :, None] * B_t[:, None, :]
                y_t = jnp.einsum('bds,bs->bd', hst, C_t)
                return (hst, y_t)
            tm = lambda a: jnp.swapaxes(a, 0, 1)
            h0 = jnp.zeros((h.shape[0], D_INNER, D_STATE), h.dtype)
            _, ys = jax.lax.scan(step, h0, (tm(dt), tm(Bm), tm(Cm), tm(xs)))
            y = jnp.swapaxes(ys, 0, 1) + xs * Dskip
            return y * jax.nn.silu(z) @ out_w
        h, gate = _adaln(x, c, adaln_mamba_w, adaln_mamba_b)
        h_fwd = _ssm(h, fwd_in_w, fwd_xproj_w, fwd_dt_bias, fwd_A_log, fwd_D, fwd_out_w)
        h_bwd = jnp.flip(_ssm(jnp.flip(h, 1), bwd_in_w, bwd_xproj_w, bwd_dt_bias, bwd_A_log, bwd_D, bwd_out_w), 1)
        x = x + gate * (h_fwd + h_bwd)
        h, gate = _adaln(x, c, adaln_mlp_w, adaln_mlp_b)
        mlp_out = jax.nn.silu(h @ mlp_w1) * (h @ mlp_w2) @ mlp_w3
        return x + gate * mlp_out

    def _L2_cond_ref(x, c, W_mod, b_mod, W_qkv, W_out, b_out, W1, b1, W2, b2):
        import jax, jax.numpy as jnp
        import numpy as np
        B, T, DIM = (4, 256, 256)
        COND = 256
        HEADS, DH = (16, 64)
        INNER = HEADS * DH
        MLP = 1024
        EPS = 1e-05

        def _layernorm(x):
            mu = jnp.mean(x, axis=-1, keepdims=True)
            var = jnp.mean(jnp.square(x - mu), axis=-1, keepdims=True)
            return (x - mu) * jax.lax.rsqrt(var + EPS)

        def _modulate(x, shift, scale):
            return x * (1.0 + scale) + shift

        def _attention(x, W_qkv, W_out, b_out):
            Bq, Tq, _ = x.shape
            qkv = x @ W_qkv
            q, k, v = jnp.split(qkv, 3, axis=-1)
            q = q.reshape(Bq, Tq, HEADS, DH)
            k = k.reshape(Bq, Tq, HEADS, DH)
            v = v.reshape(Bq, Tq, HEADS, DH)
            scale = DH ** (-0.5)
            attn = jnp.einsum('bqhd,bkhd->bhqk', q, k) * scale
            attn = jax.nn.softmax(attn, axis=-1)
            out = jnp.einsum('bhqk,bkhd->bqhd', attn, v).reshape(Bq, Tq, INNER)
            return out @ W_out + b_out

        def _ff(x, W1, b1, W2, b2):
            return jax.nn.gelu(x @ W1 + b1, approximate=False) @ W2 + b2
        mod = jax.nn.silu(c) @ W_mod + b_mod
        sh_msa, sc_msa, g_msa, sh_mlp, sc_mlp, g_mlp = jnp.split(mod, 6, axis=-1)
        x = x + g_msa * _attention(_modulate(_layernorm(x), sh_msa, sc_msa), W_qkv, W_out, b_out)
        x = x + g_mlp * _ff(_modulate(_layernorm(x), sh_mlp, sc_mlp), W1, b1, W2, b2)
        return x

    def _L3_cond_ref(x, time_emb, Wqkv, bqkv, Wproj, bproj, W1, b1, W2, b2, Wt, bt, g1, be1, g2, be2):
        import jax, jax.numpy as jnp
        import numpy as np
        D = 256
        H = 16
        HD = D // H
        MLP = 4 * D

        def _lin(key, fin, fout):
            k1, k2 = jax.random.split(key)
            lim = 1.0 / np.sqrt(fin)
            W = jax.random.uniform(k1, (fin, fout), minval=-lim, maxval=lim, dtype=jnp.float32)
            b = jax.random.uniform(k2, (fout,), minval=-lim, maxval=lim, dtype=jnp.float32)
            return (W, b)

        def layernorm(x, g, b, eps=1e-05):
            mu = jnp.mean(x, axis=-1, keepdims=True)
            var = jnp.var(x, axis=-1, keepdims=True)
            return (x - mu) * jax.lax.rsqrt(var + eps) * g + b

        def attention(h, Wqkv, bqkv, Wproj, bproj):
            B, L, _ = h.shape
            qkv = (h @ Wqkv + bqkv).reshape(B, L, 3, H, HD)
            q, k, v = jnp.moveaxis(qkv, 2, 0)
            scale = HD ** (-0.5)
            attn = jnp.einsum('blhd,bmhd->bhlm', q, k) * scale
            attn = jax.nn.softmax(attn, axis=-1)
            out = jnp.einsum('bhlm,bmhd->blhd', attn, v).reshape(B, L, D)
            return out @ Wproj + bproj
        tp = (jax.nn.silu(time_emb) @ Wt + bt)[:, None, :]
        shift_msa, scale_msa, gate_msa, shift_mlp, scale_mlp, gate_mlp = jnp.split(tp, 6, axis=-1)
        h = layernorm(x, g1, be1)
        h = h * (1.0 + scale_msa) + shift_msa
        h = attention(h, Wqkv, bqkv, Wproj, bproj)
        x = x + gate_msa * h
        h = layernorm(x, g2, be2)
        h = h * (1.0 + scale_mlp) + shift_mlp
        h = jax.nn.gelu(h @ W1 + b1, approximate=False) @ W2 + b2
        x = x + gate_mlp * h
        return x
    x = _L0_cond_ref(x, cond_1024, L0_cond_ln_g, L0_cond_ln_b, L0_cond_W1, L0_cond_b1, L0_cond_W2, L0_cond_b2)
    x = _L1_cond_ref(x, cond_1024, L1_cond_adaln_mamba_w, L1_cond_adaln_mamba_b, L1_cond_adaln_mlp_w, L1_cond_adaln_mlp_b, L1_cond_mlp_w1, L1_cond_mlp_w2, L1_cond_mlp_w3, L1_cond_fwd_in_w, L1_cond_fwd_xproj_w, L1_cond_fwd_dt_bias, L1_cond_fwd_A_log, L1_cond_fwd_D, L1_cond_fwd_out_w, L1_cond_bwd_in_w, L1_cond_bwd_xproj_w, L1_cond_bwd_dt_bias, L1_cond_bwd_A_log, L1_cond_bwd_D, L1_cond_bwd_out_w)
    x = _L2_cond_ref(x, cond_1024[:, None, :], L2_cond_W_mod, L2_cond_b_mod, L2_cond_W_qkv, L2_cond_W_out, L2_cond_b_out, L2_cond_W1, L2_cond_b1, L2_cond_W2, L2_cond_b2)
    x = _L3_cond_ref(x, cond_1024, L3_cond_Wqkv, L3_cond_bqkv, L3_cond_Wproj, L3_cond_bproj, L3_cond_W1, L3_cond_b1, L3_cond_W2, L3_cond_b2, L3_cond_Wt, L3_cond_bt, L3_cond_g1, L3_cond_be1, L3_cond_g2, L3_cond_be2)
    return x

_drawn_inputs = setup_inputs


def setup_inputs(seed=0):
    import zlib

    import numpy as np

    out = dict(_drawn_inputs(seed))
    spreads = {'L0_cond_ln_g': (1.0, 0.2),
     'L0_cond_ln_b': (0.0, 0.1),
     'L0_cond_b1': (0.0, 0.1),
     'L0_cond_b2': (0.0, 0.1),
     'L1_cond_adaln_mamba_b': (0.0, 0.1),
     'L1_cond_adaln_mlp_b': (0.0, 0.1),
     'L1_cond_fwd_dt_bias': (0.0, 0.1),
     'L1_cond_fwd_D': (1.0, 0.2),
     'L1_cond_bwd_dt_bias': (0.0, 0.1),
     'L1_cond_bwd_D': (1.0, 0.2),
     'L3_cond_g1': (1.0, 0.2),
     'L3_cond_be1': (0.0, 0.1),
     'L3_cond_g2': (1.0, 0.2),
     'L3_cond_be2': (0.0, 0.1)}
    factors = {}
    for name, (base, spread) in spreads.items():
        noise = np.random.default_rng([zlib.crc32(name.encode()), seed]).standard_normal(out[name].shape)
        drawn = base * np.exp(spread * noise) if base else spread * noise
        out[name] = jnp.asarray(drawn.astype(out[name].dtype))
    for name, factor in factors.items():
        out[name] = (out[name] * factor).astype(out[name].dtype)
    return out
```

```python
import numpy as np
from contextlib import ExitStack

import concourse.bass as bass
from concourse import mybir

F32 = mybir.dt.float32
BF16 = mybir.dt.bfloat16
ALU = mybir.AluOpType
ACT = mybir.ActivationFunctionType
AX = mybir.AxisListType

P = 128
NB, T, D = 16, 256, 256
PAIR = 2
UNITS = NB // PAIR
N = PAIR * T
FC = D // P
RANK = 8
DI = 2 * D
IC = DI // P
S = 64
PARTS = 3
ROWS = PARTS * PARTS * PAIR
TC = T // P
Q = 4
QR = P // Q
EPS = 1e-5
H = 16
DH2, DH3 = 64, 16
PADH = 32
MLP = 1024

VEC = {}


def _columns():
    at = 0
    for name, n in (("ln_g", 2), ("ln_b", 2), ("l0b1", 2), ("l0b2a", 32), ("mod_b", 36),
                    ("g1", 2), ("be1", 2), ("g2", 2), ("be2", 2),
                    ("dtb0", 4), ("dtb1", 4), ("D0", 4), ("D1", 4),
                    ("bo2", 2), ("b12", 8), ("b22", 2),
                    ("bq3", 4), ("bk3", 4), ("bv3", 4), ("bo3", 2), ("b13", 8), ("b23", 2)):
        VEC[name] = (at, at + n)
        at += n
    return at


NVEC = _columns()

MOD = {n: 2 * k for k, n in enumerate(
    ("m_sh", "m_sc", "m_g", "p_sh", "p_sc", "p_g",
     "a2_sh", "a2_sc", "a2_g", "f2_sh", "f2_sc", "f2_g",
     "a3_sh", "a3_sc", "a3_g", "f3_sh", "f3_sc", "f3_g"))}
NMOD = 36


def wait(eng, sem, value):
    if isinstance(value, int) and value <= 0:
        return
    eng.wait_ge(sem, value)


def release(nc, sems):
    nc.clear_and_free_semaphores(sems)
    nc.all_engine_barrier()


def over_units(eng, body, count=UNITS):
    body(0)
    with eng.Fori(1, count) as i:
        body(i)


def conditioning(nc, ctx, io, keep, scratch):
    sems = []
    with ExitStack() as c:
        def sb(name, shape, dt=F32):
            return c.enter_context(nc.sbuf_tensor(name, shape, dt))

        def sem(name):
            sems.append(nc.alloc_semaphore(name="c_" + name))
            return sems[-1]

        vec, mod, wa = keep["vec"], keep["mod"], keep["wa"]
        cond = sb("cond", [P, FC, NB])
        ones = sb("c_ones", [P, P])
        w1 = sb("w1", [P, FC, D])
        w2a = sb("w2a", [P, FC, 4096])
        w2b = sb("w2b", [P, FC, 4096])
        b2b = sb("b2b", [NB, 4096])
        wm = sb("wm", [P, FC, NMOD * P])
        xc = sb("c_xc", [P, FC, NB])
        sq = sb("c_sq", [P, FC, NB])
        rstd = sb("c_rstd", [P, NB])
        xn = sb("c_xn", [P, FC, NB])
        hn = sb("c_hn", [P, FC, NB])
        hid = sb("c_hid", [P, FC, NB])
        sil = sb("c_sil", [P, FC, NB])
        wbb = sb("c_wbb", [NB, 4096])
        alog = sb("c_alog", [P, 2 * IC, S])
        aneg = sb("c_aneg", [P, 2 * IC, S])
        ares = sb("c_ares", [P, 2 * IC, S])
        az = sb("c_az", [P, 2 * IC, PARTS, PAIR, PAIR, S], BF16)
        gsc = sb("c_gsc", [P, 4, NB])
        ps = c.enter_context(nc.psum_tensor("c_ps", [P, 4, 512], F32))
        pw = c.enter_context(nc.psum_tensor("c_pw", [P, 4, 512], F32))

        small_in, w1_in, w2_in, wm_in, a_in = (sem(n) for n in ("small_in", "w1_in", "w2_in", "wm_in", "a_in"))
        ones_set, mean_mm, xc_done, sq_done, var_mm, rstd_done, xn_done, hn_done = (
            sem(n) for n in ("ones", "mean", "xc", "sq", "var", "rstd", "xn", "hn"))
        ln_done, hid_mm, hid_done, sil_done, wa_mm, bb_mm, bb_done, mod_mm, mod_done = (
            sem(n) for n in ("ln", "hidmm", "hid", "sil", "wamm", "bbmm", "bb", "modmm", "mod"))
        bb_out, a_out, exp_done, az_zero, split_v, split_a, one_done, fold, eps_set = (
            sem(n) for n in ("bbout", "aout", "exp", "azz", "splitv", "splita", "one", "fold", "eps"))

        with nc.Block() as block:
            @block.sync
            def _(sp):
                sp.dma_start(vec[:], io["vecs"]).then_inc(small_in, 16)
                sp.dma_start(cond[:], io["condT"]).then_inc(small_in, 16)
                sp.dma_start(b2b[:], io["l0b2b"].to_broadcast([NB, 4096])).then_inc(small_in, 16)
                sp.dma_start(w1[:], io["l0W1"].rearrange("(c p) m -> p c m", p=P)).then_inc(w1_in, 16)
                sp.dma_start(alog[:], io["A_log"].rearrange("(n p) s -> p n s", p=P)).then_inc(a_in, 16)
                at = 0
                for name in ("mamba_w", "mlp_w", "W_mod", "Wt"):
                    n = io[name].shape[1]
                    sp.dma_start(wm[:, :, at:at + n], io[name].rearrange("(c p) m -> p c m", p=P)).then_inc(wm_in, 16)
                    at += n
                sp.dma_start(w2a[:], io["l0W2a"].rearrange("(c p) m -> p c m", p=P)).then_inc(w2_in, 16)
                sp.dma_start(w2b[:], io["l0W2b"].rearrange("(c p) m -> p c m", p=P)).then_inc(w2_in, 16)
                sp.wait_ge(split_v, 4)
                sp.wait_ge(split_a, 4)
                sp.dma_start(scratch["A3"].rearrange("n i b d f -> d (n i b) f"),
                             az[:].rearrange("p n i b c s -> p (n i b) (c s)")).then_inc(a_out, 16)
                sp.wait_ge(bb_done, 8)
                sp.dma_start(scratch["BB"].rearrange("q r b d -> b (q r) d"),
                             wbb[:].rearrange("b (m d) -> b m d", d=D)).then_inc(bb_out, 16)
                sp.wait_ge(a_out, 16)
                sp.wait_ge(bb_out, 16)

            @block.tensor
            def _(pe):
                pe.wait_ge(ones_set, 1)
                pe.wait_ge(small_in, 48)
                for k in range(FC):
                    mm = pe.matmul(ps[:, 0, 0:NB], ones[:], cond[:, k, :], start=(k == 0), stop=(k == FC - 1))
                mm.then_inc(mean_mm, 1)
                pe.wait_ge(sq_done, 1)
                for k in range(FC):
                    mm = pe.matmul(ps[:, 1, 0:NB], ones[:], sq[:, k, :], start=(k == 0), stop=(k == FC - 1))
                mm.then_inc(var_mm, 1)
                pe.wait_ge(wm_in, 64)
                for m in range(NMOD):
                    if m == 12:
                        pe.wait_ge(sil_done, 1)
                    src = cond if m < 12 else sil
                    out = ps[:, 2, m * NB:(m + 1) * NB] if m < 12 else ps[:, 3, (m - 12) * NB:(m - 11) * NB]
                    for k in range(FC):
                        mm = pe.matmul(out, wm[:, k, m * P:(m + 1) * P], src[:, k, :],
                                       start=(k == 0), stop=(k == FC - 1))
                mm.then_inc(mod_mm, 1)
                pe.wait_ge(w1_in, 16)
                pe.wait_ge(hn_done, 2)
                for m in range(FC):
                    for k in range(FC):
                        mm = pe.matmul(ps[:, 0, 64 + m * NB:64 + (m + 1) * NB], w1[:, k, m * P:(m + 1) * P],
                                       hn[:, k, :], start=(k == 0), stop=(k == FC - 1))
                mm.then_inc(hid_mm, 1)
                pe.wait_ge(w2_in, 32)
                pe.wait_ge(hid_done, 2)
                for m in range(32):
                    for k in range(FC):
                        mm = pe.matmul(pw[:, 0, m * NB:(m + 1) * NB], w2a[:, k, m * P:(m + 1) * P],
                                       hid[:, k, :], start=(k == 0), stop=(k == FC - 1))
                mm.then_inc(wa_mm, 1)
                for m in range(8):
                    if m >= 3:
                        pe.wait_ge(bb_done, m - 2)
                    for k in range(FC):
                        mm = pe.matmul(pw[0:NB, 1 + m % 3, :], hid[:, k, :], w2b[:, k, m * 512:(m + 1) * 512],
                                       start=(k == 0), stop=(k == FC - 1))
                    mm.then_inc(bb_mm, 1)

            @block.scalar
            def _(act):
                act.wait_ge(xc_done, 1)
                act.activation(sq[:], xc[:], ACT.Square).then_inc(sq_done, 1)
                act.wait_ge(var_mm, 1)
                act.wait_ge(eps_set, 1)
                act.activation(rstd[:], ps[:, 1, 0:NB], ACT.Ln, bias=keep["eps"][:]).then_inc(ln_done, 1)
                act.wait_ge(ln_done, 1)
                act.activation(rstd[:], rstd[:], ACT.Exp, scale=-0.5).then_inc(rstd_done, 1)
                act.wait_ge(a_in, 16)
                act.activation(aneg[:], alog[:], ACT.Exp).then_inc(exp_done, 1)
                act.wait_ge(small_in, 48)
                act.activation(sil[:], cond[:], ACT.Silu).then_inc(sil_done, 1)
                act.wait_ge(split_v, 1)
                act.wait_ge(az_zero, 1)
                for b in range(PAIR):
                    act.copy(az[:, :, 0, b, b, :], aneg[:]).then_inc(split_a, 1)
                act.wait_ge(split_v, 2)
                for b in range(PAIR):
                    act.copy(az[:, :, 1, b, b, :], ares[:]).then_inc(split_a, 1)
                act.wait_ge(hid_mm, 1)
                for m in range(FC):
                    act.activation(hid[:, m, :], ps[:, 0, 64 + m * NB:64 + (m + 1) * NB], ACT.Gelu,
                                   bias=vec[:, VEC["l0b1"][0] + m:VEC["l0b1"][0] + m + 1]).then_inc(hid_done, 1)

            @block.vector
            def _(dve):
                dve.memset(ones[:], 1.0 / D).then_inc(ones_set, 1)
                dve.memset(keep["eps"][:], EPS).then_inc(eps_set, 1)
                dve.memset(az[:], 0.0).then_inc(az_zero, 1)
                dve.wait_ge(small_in, 48)
                dve.wait_ge(mean_mm, 1)
                dve.tensor_tensor(xc[:], cond[:], ps[:, 0, None, 0:NB].to_broadcast([P, FC, NB]),
                                  ALU.subtract).then_inc(xc_done, 1)
                dve.wait_ge(exp_done, 1)
                dve.tensor_scalar(aneg[:], aneg[:], -1.0, None, ALU.mult).then_inc(split_v, 1)
                dve.wait_ge(split_v, 1)
                dve.wait_ge(split_a, 2)
                dve.tensor_tensor(ares[:], aneg[:], az[:, :, 0, 0, 0, :], ALU.subtract).then_inc(split_v, 1)
                dve.wait_ge(split_v, 2)
                dve.wait_ge(split_a, 4)
                for b in range(PAIR):
                    dve.tensor_tensor(az[:, :, 2, b, b, :], ares[:], az[:, :, 1, 0, 0, :],
                                      ALU.subtract).then_inc(split_v, 1)
                dve.wait_ge(rstd_done, 1)
                dve.tensor_tensor(xn[:], xc[:], rstd[:, None, :].to_broadcast([P, FC, NB]),
                                  ALU.mult).then_inc(xn_done, 1)
                dve.wait_ge(xn_done, 1)
                g, b0 = VEC["ln_g"][0], VEC["ln_b"][0]
                for k in range(FC):
                    dve.tensor_scalar(hn[:, k, :], xn[:, k, :], vec[:, g + k:g + k + 1],
                                      vec[:, b0 + k:b0 + k + 1], ALU.mult, ALU.add).then_inc(hn_done, 1)
                dve.wait_ge(mod_mm, 1)
                mb = VEC["mod_b"][0]
                for lo, hi, bank in ((0, 12, 2), (12, NMOD, 3)):
                    dve.tensor_tensor(
                        mod[:, lo:hi, :], ps[:, bank, 0:(hi - lo) * NB].rearrange("p (m b) -> p m b", b=NB),
                        vec[:, mb + lo:mb + hi, None].to_broadcast([P, hi - lo, NB]), ALU.add).then_inc(mod_done, 1)
                dve.wait_ge(mod_done, 2)
                for name in ("m_sc", "p_sc", "a2_sc", "f2_sc", "a3_sc", "f3_sc"):
                    dve.tensor_scalar(mod[:, MOD[name]:MOD[name] + 2, :], mod[:, MOD[name]:MOD[name] + 2, :],
                                      1.0, None, ALU.add).then_inc(one_done, 1)
                dve.wait_ge(one_done, 6)
                k = 0
                for g, be, sc, sh in (("g1", "be1", "a3_sc", "a3_sh"), ("g2", "be2", "f3_sc", "f3_sh")):
                    for ch in range(FC):
                        dve.scalar_tensor_tensor(mod[:, MOD[sh] + ch, :], mod[:, MOD[sc] + ch, :],
                                                 vec[:, VEC[be][0] + ch:VEC[be][0] + ch + 1],
                                                 mod[:, MOD[sh] + ch, :], ALU.mult, ALU.add).then_inc(fold, 1)
                        dve.wait_ge(fold, k + 1)
                        dve.tensor_scalar(mod[:, MOD[sc] + ch, :], mod[:, MOD[sc] + ch, :],
                                          vec[:, VEC[g][0] + ch:VEC[g][0] + ch + 1], None, ALU.mult).then_inc(fold, 1)
                        k += 2
                dve.wait_ge(wa_mm, 1)
                ba = VEC["l0b2a"][0]
                dve.tensor_tensor(wa[:], pw[:, 0, :].rearrange("p (m b) -> p m b", b=NB),
                                  vec[:, ba:ba + 32, None].to_broadcast([P, 32, NB]), ALU.add)
                for m in range(8):
                    dve.wait_ge(bb_mm, m + 1)
                    dve.tensor_tensor(wbb[:, m * 512:(m + 1) * 512], pw[0:NB, 1 + m % 3, :],
                                      b2b[:, m * 512:(m + 1) * 512], ALU.add).then_inc(bb_done, 1)
    release(nc, sems)


def prepare(nc, ctx, io, keep, scratch):
    sems = []
    with ExitStack() as c:
        def sb(name, shape, dt=F32):
            return c.enter_context(nc.sbuf_tensor("p_" + name, shape, dt))

        def sem(name):
            sems.append(nc.alloc_semaphore(name="p_" + name))
            return sems[-1]

        vec, mod, wa = keep["vec"], keep["mod"], keep["wa"]
        ones = sb("ones", [P, P])
        ident = sb("ident", [P, P])
        in_w = [sb(f"in_w{r}", [P, FC, 2 * DI]) for r in range(2)]
        xp_w = [sb(f"xp_w{r}", [P, IC, DI + 2 * S]) for r in range(2)]
        cdup = [sb(f"cdup{r}", [P, IC, 2, S]) for r in range(2)]
        x = sb("x", [P, FC, N])
        bb = sb("bb", [RANK, 2, PAIR, D])
        low = sb("low", [RANK, 2, N])
        g = sb("g", [P, FC, N])
        x1 = sb("x1", [P, FC, N])
        xc = sb("xc", [P, FC, N])
        sq = sb("sq", [P, FC, N])
        rstd = sb("rstd", [P, N])
        h = [sb(f"h{r}", [P, FC, N]) for r in range(2)]
        xs = sb("xs", [P, IC, N])
        sz = sb("sz", [P, IC, N])
        skip = sb("skip", [P, IC, N])
        pre = sb("pre", [P, IC, N])
        sp_ = sb("soft", [P, IC, N])
        dt_ = sb("dt", [P, IC, N])
        u = sb("u", [P, IC, N])
        dp = sb("dp", [P, IC, PARTS, N], BF16)
        up = sb("up", [P, PARTS, 4, DI], BF16)
        bz = sb("bz", [P, PARTS, 4, PAIR, S], BF16)
        bres = sb("bres", [P, 4, S])
        cs = sb("cs", [P, T, PAIR])
        g0 = c.enter_context(nc.psum_tensor("p_g0", [P, 4, 512], F32))
        g1 = c.enter_context(nc.psum_tensor("p_g1", [P, 4, 512], F32))

        names = ("w_in x_in bb_in const z1 z2 low1_mm low1_done up1_mm gelu_done low2_mm low2_done up2_mm "
                 "x1_done x1_out mean_mm xc_done sq_done var_mm ln_done rstd_done xn_done h_done hr_done "
                 "xs_mm xs_done z_mm sz_done skip_done dt_mm pre_done abs_done soft_e soft_done dt_done u_done "
                 "vec_b dp0 dres dp1 dp2 ut_mm up0 ures up1 up2 bc_mm bz0 bres_done bz1 bz2 cs_done "
                 "sz_out skip_out dp_out up_out bz_out cs_out").split()
        s = {n: sem(n) for n in names}

        with nc.Block() as block:
            @block.sync
            def _(sp):
                for r in range(2):
                    sp.dma_start(in_w[r][:], io["in_w"][r].rearrange("(c p) m -> p c m", p=P)).then_inc(s["w_in"], 16)
                    sp.dma_start(xp_w[r][:], io["xproj_w"][r].rearrange("(c p) m -> p c m", p=P)).then_inc(s["w_in"], 16)
                    for e in range(2):
                        sp.dma_start(cdup[r][:, :, e, :],
                                     io["xproj_w"][r][:, DI + S:DI + 2 * S].rearrange("(c p) m -> p c m", p=P)
                                     ).then_inc(s["w_in"], 16)

                def unit(i):
                    wait(sp, s["x1_done"], i)
                    sp.dma_start(x[:], io["xT"][i]).then_inc(s["x_in"], 16)
                    wait(sp, s["up2_mm"], i)
                    sp.dma_start(bb[:], scratch["BB"].rearrange("q r (i b) d -> i r q (b d)", b=PAIR)[i]
                                 ).then_inc(s["bb_in"], 16)
                    wait(sp, s["x1_done"], i + 1)
                    sp.dma_start(scratch["X1"][i], x1[:]).then_inc(s["x1_out"], 16)
                    for r in range(2):
                        k = 2 * i + r
                        wait(sp, s["sz_done"], k + 1)
                        sp.dma_start(scratch["SZ"][r, i], sz[:]).then_inc(s["sz_out"], 16)
                        wait(sp, s["skip_done"], IC * k + IC)
                        sp.dma_start(scratch["SK"][r, i], skip[:]).then_inc(s["skip_out"], 16)
                        wait(sp, s["cs_done"], 2 * k + 2)
                        sp.dma_start(scratch["C2"][r, i], cs[:]).then_inc(s["cs_out"], 16)
                        wait(sp, s["bz2"], 2 * k + 2)
                        wait(sp, s["bz1"], 2 * k + 2)
                        sp.dma_start(scratch["B3"][r, i].rearrange("j b c t f -> t (j b c) f"),
                                     bz[:].rearrange("t j k c s -> t (j k) (c s)")).then_inc(s["bz_out"], 16)
                        wait(sp, s["dp2"], k + 1)
                        for m in range(IC):
                            sp.dma_start(scratch["D3"][r, m, i].rearrange("j b c d t -> d (j b c) t"),
                                         dp[:, m].rearrange("p j (k t) -> p (j k) t", t=P)).then_inc(s["dp_out"], 16)
                        wait(sp, s["up2"], k + 1)
                        for m in range(IC):
                            sp.dma_start(scratch["U3"][r, m, i].rearrange("j b c t d -> t (j b c) d"),
                                         up[:, :, :, m * P:(m + 1) * P].rearrange("p j k d -> p (j k) d")
                                         ).then_inc(s["up_out"], 16)

                over_units(sp, unit)
                sp.wait_ge(s["x1_out"], 16 * UNITS)
                for n in ("sz_out", "skip_out", "cs_out", "bz_out"):
                    sp.wait_ge(s[n], 32 * UNITS)
                for n in ("dp_out", "up_out"):
                    sp.wait_ge(s[n], 32 * IC * UNITS)

            @block.gpsimd
            def _(pool):
                pool.memset(ident[:], 0.0).then_inc(s["z1"], 1)
                pool.wait_ge(s["z1"], 1)
                pool.affine_select(out=ident[:], in_=ident[:], compare_op=ALU.not_equal, fill=1.0, base=0,
                                   pattern=[[-1, P]], channel_multiplier=1).then_inc(s["const"], 1)

                def unit(i):
                    for r in range(2):
                        k = 2 * i + r
                        wait(pool, s["dt_done"], k + 1)
                        wait(pool, s["xs_done"], k + 1)
                        wait(pool, s["ut_mm"], k)
                        pool.tensor_tensor(u[:], dt_[:], xs[:], ALU.mult).then_inc(s["u_done"], 1)

                over_units(pool, unit)

            @block.tensor
            def _(pe):
                pe.wait_ge(s["w_in"], 16 * 8)
                pe.wait_ge(s["const"], 2)

                def unit(i):
                    pe.wait_ge(s["x_in"], 16 * i + 16)
                    wait(pe, s["vec_b"], 2 * i + 2)
                    wait(pe, s["up0"], 2 * i)
                    wait(pe, s["ures"], 2 * i)
                    for b in range(PAIR):
                        for k in range(FC):
                            mm = pe.matmul(g0[0:RANK, 0, b * T:(b + 1) * T], keep["wab"][:, b, 0, :, k],
                                           x[:, k, b * T:(b + 1) * T], start=(k == 0), stop=(k == FC - 1))
                    mm.then_inc(s["low1_mm"], 1)
                    pe.wait_ge(s["bb_in"], 16 * i + 16)
                    wait(pe, s["low1_done"], i + 1)
                    wait(pe, s["cs_done"], 4 * i)
                    wait(pe, s["bres_done"], 2 * i)
                    for m in range(FC):
                        for b in range(PAIR):
                            mm = pe.matmul(g1[:, m, b * T:(b + 1) * T], bb[:, 0, b, m * P:(m + 1) * P],
                                           low[:, 0, b * T:(b + 1) * T], start=True, stop=True)
                    mm.then_inc(s["up1_mm"], 1)
                    wait(pe, s["gelu_done"], i + 1)
                    for b in range(PAIR):
                        for k in range(FC):
                            mm = pe.matmul(g0[0:RANK, 1, b * T:(b + 1) * T], keep["wab"][:, b, 1, :, k],
                                           g[:, k, b * T:(b + 1) * T], start=(k == 0), stop=(k == FC - 1))
                    mm.then_inc(s["low2_mm"], 1)
                    wait(pe, s["low2_done"], i + 1)
                    for m in range(FC):
                        for b in range(PAIR):
                            mm = pe.matmul(g1[:, 2 + m, b * T:(b + 1) * T], bb[:, 1, b, m * P:(m + 1) * P],
                                           low[:, 1, b * T:(b + 1) * T], start=True, stop=True)
                    mm.then_inc(s["up2_mm"], 1)
                    wait(pe, s["x1_done"], i + 1)
                    for k in range(FC):
                        mm = pe.matmul(g0[:, 2, :], ones[:], x1[:, k, :], start=(k == 0), stop=(k == FC - 1))
                    mm.then_inc(s["mean_mm"], 1)
                    wait(pe, s["sq_done"], i + 1)
                    for k in range(FC):
                        mm = pe.matmul(g0[:, 3, :], ones[:], sq[:, k, :], start=(k == 0), stop=(k == FC - 1))
                    mm.then_inc(s["var_mm"], 1)
                    for r in range(2):
                        n = 2 * i + r
                        if r == 0:
                            wait(pe, s["h_done"], 4 * i + 4)
                        else:
                            wait(pe, s["hr_done"], i + 1)
                            wait(pe, s["up0"], n)
                            wait(pe, s["ures"], n)
                        for m in range(IC):
                            for k in range(FC):
                                mm = pe.matmul(g0[:, m, :], in_w[r][:, k, m * P:(m + 1) * P], h[r][:, k, :],
                                               start=(k == 0), stop=(k == FC - 1))
                        mm.then_inc(s["xs_mm"], 1)
                        if r == 1:
                            wait(pe, s["cs_done"], 2 * n)
                            wait(pe, s["bres_done"], n)
                        for m in range(IC):
                            for k in range(FC):
                                mm = pe.matmul(g1[:, m, :], in_w[r][:, k, DI + m * P:DI + (m + 1) * P],
                                               h[r][:, k, :], start=(k == 0), stop=(k == FC - 1))
                        mm.then_inc(s["z_mm"], 1)
                        wait(pe, s["xs_done"], n + 1)
                        for m in range(IC):
                            for k in range(IC):
                                mm = pe.matmul(g0[:, m, :], xp_w[r][:, k, m * P:(m + 1) * P], xs[:, k, :],
                                               start=(k == 0), stop=(k == IC - 1))
                        mm.then_inc(s["dt_mm"], 1)
                        wait(pe, s["sz_done"], n + 1)
                        for k in range(IC):
                            pe.matmul(g1[:, 0, :], cdup[r][:, k, :, :].rearrange("p e s -> p (e s)"), xs[:, k, :],
                                      start=(k == 0), stop=(k == IC - 1))
                        for q in range(4):
                            for k in range(IC):
                                mm = pe.matmul(g1[:, 1, q * S:(q + 1) * S], xs[:, k, q * P:(q + 1) * P],
                                               xp_w[r][:, k, DI:DI + S], start=(k == 0), stop=(k == IC - 1))
                        mm.then_inc(s["bc_mm"], 1)
                        wait(pe, s["pre_done"], IC * n + IC)
                        wait(pe, s["u_done"], n + 1)
                        for q in range(4):
                            for m in range(IC):
                                mm = pe.transpose(g0[:, q, m * P:(m + 1) * P], u[:, m, q * P:(q + 1) * P], ident[:])
                        mm.then_inc(s["ut_mm"], 1)

                over_units(pe, unit)

            @block.scalar
            def _(act):
                def unit(i):
                    wait(act, s["low1_mm"], i + 1)
                    act.copy(low[:, 0, :], g0[0:RANK, 0, :]).then_inc(s["low1_done"], 1)
                    wait(act, s["up1_mm"], i + 1)
                    act.activation(g[:], g1[:, 0:2, :], ACT.Gelu).then_inc(s["gelu_done"], 1)
                    wait(act, s["low2_mm"], i + 1)
                    act.copy(low[:, 1, :], g0[0:RANK, 1, :]).then_inc(s["low2_done"], 1)
                    wait(act, s["xc_done"], i + 1)
                    act.activation(sq[:], xc[:], ACT.Square).then_inc(s["sq_done"], 1)
                    wait(act, s["var_mm"], i + 1)
                    wait(act, s["xn_done"], i)
                    act.activation(rstd[:], g0[:, 3, :], ACT.Ln, bias=keep["eps"][:]).then_inc(s["ln_done"], 1)
                    wait(act, s["ln_done"], i + 1)
                    act.activation(rstd[:], rstd[:], ACT.Exp, scale=-0.5).then_inc(s["rstd_done"], 1)
                    for r in range(2):
                        n = 2 * i + r
                        wait(act, s["xs_mm"], n + 1)
                        wait(act, s["bc_mm"], n)
                        wait(act, s["u_done"], n)
                        wait(act, s["skip_done"], IC * n)
                        act.activation(xs[:], g0[:], ACT.Silu).then_inc(s["xs_done"], 1)
                        wait(act, s["z_mm"], n + 1)
                        wait(act, s["sz_out"], 16 * n)
                        act.activation(sz[:], g1[:], ACT.Silu).then_inc(s["sz_done"], 1)
                        wait(act, s["pre_done"], IC * n + IC)
                        wait(act, s["dt_done"], n)
                        wait(act, s["up2"], n)
                        act.activation(sp_[:], pre[:], ACT.Abs).then_inc(s["abs_done"], 1)
                        wait(act, s["abs_done"], n + 1)
                        act.activation(sp_[:], sp_[:], ACT.Exp, scale=-1.0).then_inc(s["soft_e"], 1)
                        wait(act, s["soft_e"], n + 1)
                        act.activation(sp_[:], sp_[:], ACT.Ln, bias=1.0).then_inc(s["soft_done"], 1)
                        wait(act, s["bc_mm"], n + 1)
                        wait(act, s["bz_out"], 16 * n)
                        if isinstance(i, int) and r == 0:
                            act.wait_ge(s["z2"], 2)
                        for b in range(PAIR):
                            act.copy(bz[:, 0, 2 * b:2 * b + 2, b, :],
                                     g1[:, 1, 2 * b * S:(2 * b + 2) * S].rearrange("p (k s) -> p k s", s=S)
                                     ).then_inc(s["bz0"], 1)
                        wait(act, s["bres_done"], n + 1)
                        for b in range(PAIR):
                            act.copy(bz[:, 1, 2 * b:2 * b + 2, b, :], bres[:, 2 * b:2 * b + 2, :]).then_inc(s["bz1"], 1)
                        wait(act, s["dt_done"], n + 1)
                        wait(act, s["dp_out"], 16 * IC * n)
                        act.copy(dp[:, :, 0, :], dt_[:]).then_inc(s["dp0"], 1)
                        wait(act, s["dres"], n + 1)
                        act.copy(dp[:, :, 1, :], pre[:]).then_inc(s["dp1"], 1)
                        wait(act, s["ut_mm"], n + 1)
                        wait(act, s["up_out"], 16 * IC * n)
                        act.copy(up[:, 0], g0[:]).then_inc(s["up0"], 1)
                        wait(act, s["ures"], n + 1)
                        act.copy(up[:, 1], sp_[:]).then_inc(s["up1"], 1)

                over_units(act, unit)

            @block.vector
            def _(dve):
                dve.memset(ones[:], 1.0 / D).then_inc(s["const"], 1)
                dve.memset(bz[:], 0.0).then_inc(s["z2"], 1)
                dve.memset(cs[:], 0.0).then_inc(s["z2"], 1)
                dve.wait_ge(s["z2"], 2)

                def unit(i):
                    wait(dve, s["low2_mm"], i)
                    wait(dve, s["h_done"], 4 * i)
                    dve.tensor_copy(keep["wab"][:].rearrange("p b q r k -> p b (q r k)"),
                                    wa[:, :, bass.ds(PAIR * i, PAIR)].rearrange("p m b -> p b m")).then_inc(s["vec_b"], 1)
                    dve.tensor_copy(keep["mb"][:], mod[:, :, bass.ds(PAIR * i, PAIR)].rearrange("p m b -> p b m")
                                    ).then_inc(s["vec_b"], 1)
                    wait(dve, s["up2_mm"], i + 1)
                    wait(dve, s["x1_out"], 16 * i)
                    dve.tensor_tensor(x1[:], x[:], g1[:, 2:4, :], ALU.add).then_inc(s["x1_done"], 1)
                    wait(dve, s["mean_mm"], i + 1)
                    wait(dve, s["x1_done"], i + 1)
                    dve.tensor_tensor(xc[:], x1[:], g0[:, 2, None, :].to_broadcast([P, FC, N]),
                                      ALU.subtract).then_inc(s["xc_done"], 1)
                    wait(dve, s["rstd_done"], i + 1)
                    dve.tensor_tensor(xc[:], xc[:], rstd[:, None, :].to_broadcast([P, FC, N]),
                                      ALU.mult).then_inc(s["xn_done"], 1)
                    wait(dve, s["xn_done"], i + 1)
                    wait(dve, s["z_mm"], 2 * i)
                    wait(dve, s["vec_b"], 2 * i + 2)
                    for k in range(FC):
                        for b in range(PAIR):
                            dve.tensor_scalar(h[0][:, k, b * T:(b + 1) * T], xc[:, k, b * T:(b + 1) * T],
                                              keep["mb"][:, b, MOD["m_sc"] + k:MOD["m_sc"] + k + 1],
                                              keep["mb"][:, b, MOD["m_sh"] + k:MOD["m_sh"] + k + 1],
                                              ALU.mult, ALU.add).then_inc(s["h_done"], 1)
                    wait(dve, s["h_done"], 4 * i + 4)
                    dve.tensor_copy(h[1][:].rearrange("p c (b t) -> p (c b) t", t=T)[:, :, ::-1],
                                    h[0][:].rearrange("p c (b t) -> p (c b) t", t=T)).then_inc(s["hr_done"], 1)
                    for r in range(2):
                        n = 2 * i + r
                        wait(dve, s["dt_mm"], n + 1)
                        wait(dve, s["dp1"], n)
                        wait(dve, s["dp2"], n)
                        db = VEC[f"dtb{r}"][0]
                        for m in range(IC):
                            dve.tensor_scalar(pre[:, m, :], g0[:, m, :], vec[:, db + m:db + m + 1], None,
                                              ALU.add).then_inc(s["pre_done"], 1)
                        wait(dve, s["sz_done"], n + 1)
                        wait(dve, s["skip_out"], 16 * n)
                        d0 = VEC[f"D{r}"][0]
                        for m in range(IC):
                            dve.scalar_tensor_tensor(skip[:, m, :], xs[:, m, :], vec[:, d0 + m:d0 + m + 1],
                                                     sz[:, m, :], ALU.mult, ALU.mult).then_inc(s["skip_done"], 1)
                        wait(dve, s["soft_done"], n + 1)
                        wait(dve, s["pre_done"], IC * n + IC)
                        wait(dve, s["u_done"], n)
                        wait(dve, s["dp0"], n)
                        dve.scalar_tensor_tensor(dt_[:], pre[:], 0.0, sp_[:], ALU.max, ALU.add).then_inc(s["dt_done"], 1)
                        wait(dve, s["bc_mm"], n + 1)
                        wait(dve, s["cs_out"], 16 * n)
                        for b in range(PAIR):
                            dve.tensor_copy(cs[b * S:(b + 1) * S, :, b],
                                            g1[b * S:(b + 1) * S, 0, b * T:(b + 1) * T]).then_inc(s["cs_done"], 1)
                        wait(dve, s["bz0"], 2 * n + 2)
                        wait(dve, s["bz1"], 2 * n)
                        wait(dve, s["bz2"], 2 * n)
                        for b in range(PAIR):
                            bres_op = dve.tensor_tensor(
                                bres[:, 2 * b:2 * b + 2, :],
                                g1[:, 1, 2 * b * S:(2 * b + 2) * S].rearrange("p (k s) -> p k s", s=S),
                                bz[:, 0, 2 * b:2 * b + 2, b, :], ALU.subtract)
                        bres_op.then_inc(s["bres_done"], 1)
                        wait(dve, s["bz1"], 2 * n + 2)
                        wait(dve, s["bres_done"], n + 1)
                        for b in range(PAIR):
                            dve.tensor_tensor(bz[:, 2, 2 * b:2 * b + 2, b, :], bres[:, 2 * b:2 * b + 2, :],
                                              bz[:, 1, 2 * b:2 * b + 2, b, :], ALU.subtract).then_inc(s["bz2"], 1)
                        wait(dve, s["dp0"], n + 1)
                        wait(dve, s["dt_done"], n + 1)
                        dve.tensor_tensor(pre[:], dt_[:], dp[:, :, 0, :], ALU.subtract).then_inc(s["dres"], 1)
                        wait(dve, s["dp1"], n + 1)
                        wait(dve, s["dres"], n + 1)
                        dve.tensor_tensor(dp[:, :, 2, :], pre[:], dp[:, :, 1, :], ALU.subtract).then_inc(s["dp2"], 1)
                        wait(dve, s["up0"], n + 1)
                        wait(dve, s["dt_done"], n + 1)
                        dve.tensor_tensor(sp_[:], g0[:], up[:, 0], ALU.subtract).then_inc(s["ures"], 1)
                        wait(dve, s["up1"], n + 1)
                        wait(dve, s["ures"], n + 1)
                        dve.tensor_tensor(up[:, 2], sp_[:], up[:, 1], ALU.subtract).then_inc(s["up2"], 1)

                over_units(dve, unit)
    release(nc, sems)


def scan(nc, ctx, io, keep, scratch):
    STEPS = P // 8
    HALVES = 2 * STEPS
    LAG = 3
    ROW = P + PAIR
    RING = 4
    PAIRS = 2 * IC * UNITS
    W = P + 1

    sems = []
    with ExitStack() as c:
        def sb(name, shape, dt=F32):
            return c.enter_context(nc.sbuf_tensor("s_" + name, shape, dt))

        def sem(name):
            sems.append(nc.alloc_semaphore(name="s_" + name))
            return sems[-1]

        hb = [sb(f"h{e}", [P, P, W]) for e in range(2)]
        decay = [sb(f"decay{e}", [P, 8, W]) for e in range(RING)]
        dl = sb("dl", [P, QR, P], BF16)
        al = sb("al", [P, QR, P], BF16)
        ul = sb("ul", [P, QR, P], BF16)
        bl = sb("bl", [P, QR, P], BF16)
        cl = [sb(f"cl{e}", [P, P, PAIR]) for e in range(2)]
        cz = sb("cz", [P, 2, P // 8 * ROW])
        ytok = sb("ytok", [P, 2, P])
        ys = [sb(f"ys{e}", [P, PAIR, P]) for e in range(2)]
        ident = sb("ident", [P, P])
        one = sb("one", [P, 1])
        pa = [c.enter_context(nc.psum_tensor(f"s_pa{e}", [P, 8, P], F32)) for e in range(2)]
        pb = [c.enter_context(nc.psum_tensor(f"s_pb{e}", [P, 4, P], F32)) for e in range(2)]
        py = c.enter_context(nc.psum_tensor("s_py", [P, 4, P], F32))
        pt = c.enter_context(nc.psum_tensor("s_pt", [P, 4, P], F32))

        dt_in = [sem(f"dt_in{q}") for q in range(Q)]
        a_in = [sem(f"a_in{q}") for q in range(Q)]
        ub_in = [sem(f"ub_in{q}") for q in range(Q)]
        c_in = [sem(f"c_in{e}") for e in range(2)]
        y_out = [sem(f"y_out{e}") for e in range(2)]
        zeroed, adt_mm, exp_done, scanned, bu_mm, bu_done, carried, c_filled, y_mm, ytok_done, yt_mm, y_done, const = (
            sem(n) for n in ("zeroed", "adt_mm", "exp_done", "scanned", "bu_mm", "bu_done", "carried",
                             "c_filled", "y_mm", "ytok_done", "yt_mm", "y_done", "const"))

        def pairs(eng, body):
            body(0, False)
            body(1, False)
            with eng.Fori(2, PAIRS - 1) as n:
                body(n, False)
            body(PAIRS - 1, True)

        with nc.Block() as block:
            @block.sync
            def _(sp):
                def of_unit(n):
                    return (n // (IC * UNITS)) * UNITS + n % UNITS

                def group(tile, q, i=None):
                    lo = QR * q + (0 if i is None else i * PARTS * PAIR)
                    return tile[lo:lo + (ROWS if i is None else PARTS * PAIR), :, :].rearrange("r a b -> r (a b)")

                def moving(table, n, e, q):
                    rows = table[n, :, :, e, QR * q:QR * q + QR, :].rearrange("j b a f -> (j b) (a f)")
                    return rows[None].to_broadcast([PARTS, PARTS * PAIR, QR * P])

                def load_dt(n, e, q):
                    sp.dma_start(group(dl, q), moving(scratch["D3f"], n, e, q)).then_inc(dt_in[q], 16)

                def load_ub(n, e, q):
                    sp.dma_start(group(ul, q), moving(scratch["U3f"], n, e, q)).then_inc(ub_in[q], 16)
                    for i in range(PARTS):
                        rows = scratch["B3f"][of_unit(n), i, :, e, QR * q:QR * q + QR, :].rearrange("b t f -> b (t f)")
                        sp.dma_start(group(bl, q, i), rows[None].to_broadcast([PARTS, PAIR, QR * P])
                                     ).then_inc(ub_in[q], 16)

                def load_a(n, q):
                    for i in range(PARTS):
                        rows = scratch["A3"][n // UNITS, i, :, QR * q:QR * q + QR, :].rearrange("b d f -> b (d f)")
                        sp.dma_start(group(al, q, i), rows[None].to_broadcast([PARTS, PAIR, QR * P])
                                     ).then_inc(a_in[q], 16)

                def load_c(n, e):
                    sp.dma_start(cl[e][:], scratch["C2f"][of_unit(n), :, e * P:(e + 1) * P, :]).then_inc(c_in[e], 16)

                def store_y(n, e):
                    wait(sp, y_done, 2 * n + e + 1)
                    sp.dma_start(scratch["Yf"][n, :, :, e * P:(e + 1) * P], ys[e][:]).then_inc(y_out[e], 16)

                for q in range(Q):
                    load_dt(0, 0, q)
                    load_a(0, q)
                    load_ub(0, 0, q)
                for e in range(2):
                    load_c(0, e)
                for q in range(Q):
                    sp.wait_ge(bu_mm, 8 * q + 8)
                    load_ub(0, 1, q)

                def pair(n, last):
                    for e in range(2):
                        k = 2 * n + e
                        for q in range(Q):
                            if not (last and e):
                                wait(sp, adt_mm, STEPS * k + 4 * q + 4)
                                load_dt(n + e, 1 - e, q)
                                if e:
                                    load_a(n + 1, q)
                            if not last:
                                wait(sp, bu_mm, HALVES * (k + 1) + 8 * q + 8)
                                load_ub(n + 1, e, q)
                        if isinstance(n, int) and n == 0 and e == 0:
                            continue
                        store_y(n - 1 + e, 1 - e)
                        if not (last and e):
                            load_c(n + e, 1 - e)

                pairs(sp, pair)
                store_y(PAIRS - 1, 1)
                for e in range(2):
                    sp.wait_ge(y_out[e], 16 * PAIRS)

            @block.tensor
            def _(pe):
                def adt(k, n, j):
                    q = j // 4
                    if j % 4 == 0:
                        wait(pe, dt_in[q], 16 * (k + 1))
                        wait(pe, a_in[q], 48 * (n + 1))
                    wait(pe, exp_done, STEPS * k + j - 1)
                    for m in range(8):
                        d = 8 * (j % 4) + m
                        mm = pe.matmul(pa[j % 2][:, m, :], al[QR * q:QR * q + ROWS, d, :],
                                       dl[QR * q:QR * q + ROWS, d, :], start=True, stop=True)
                    mm.then_inc(adt_mm, 1)

                def bu(k, h):
                    q = h // 8
                    if h % 8 == 0:
                        wait(pe, ub_in[q], 64 * (k + 1))
                    wait(pe, bu_done, HALVES * k + h - 1)
                    for m in range(4):
                        t = 4 * (h % 8) + m
                        mm = pe.matmul(pb[h % 2][:, m, :], bl[QR * q:QR * q + ROWS, t, :],
                                       ul[QR * q:QR * q + ROWS, t, :], start=True, stop=True)
                    mm.then_inc(bu_mm, 1)

                def ch(k, e, j):
                    if j % 4 == 0:
                        wait(pe, c_filled, 4 * k + j // 4 + 1)
                    for m in range(8):
                        t = 8 * j + m
                        half, row, q = t // (P // 2), t // 4 % 16, t % 4
                        mm = pe.matmul(py[QR * q:QR * q + QR, half, :],
                                       cz[:, half, row * P + QR * q:row * P + QR * q + QR],
                                       hb[e][:, :, 1 + t], start=(row == 0), stop=(row == 15))
                    mm.then_inc(y_mm, 1)

                def turn_y(k):
                    wait(pe, ytok_done, k + 1)
                    wait(pe, y_done, k)
                    for half in range(2):
                        mm = pe.transpose(pt[:, half, :], ytok[:, half, :], ident[:])
                    mm.then_inc(yt_mm, 1)

                pe.wait_ge(const, 3)
                adt(0, 0, 0)
                adt(0, 0, 1)
                for h in range(HALVES):
                    bu(0, h)

                def pair(n, last):
                    first = isinstance(n, int) and n == 0
                    for e in range(2):
                        k = 2 * n + e
                        for j in range(STEPS + LAG - 1):
                            if j + 2 < STEPS:
                                adt(k, n, j + 2)
                            if STEPS <= j < STEPS + 2 and not (last and e):
                                adt(k + 1, n + e, j - STEPS)
                            if j == 1 and not first:
                                turn_y(k - 2)
                            if j == LAG - 1 and not (first and e == 0):
                                wait(pe, scanned, STEPS * k)
                            if j >= LAG - 1:
                                m = j - LAG + 1
                                if not (first and e == 0):
                                    ch(k - 1, 1 - e, m)
                                if not (last and e):
                                    bu(k + 1, 2 * m)
                                    bu(k + 1, 2 * m + 1)

                pairs(pe, pair)
                last = 2 * PAIRS - 1
                turn_y(last - 1)
                pe.wait_ge(scanned, STEPS * (last + 1))
                for j in range(STEPS):
                    ch(last, 1, j)
                turn_y(last)

            @block.scalar
            def _(act):
                def take_bu(k, e, h):
                    wait(act, bu_mm, HALVES * k + h + 1)
                    wait(act, y_mm, STEPS * (k - 2) + h // 2 + 1)
                    act.copy(hb[e][:, :, 1 + 4 * h:5 + 4 * h], pb[h % 2][:].rearrange("p t d -> p d t")
                             ).then_inc(bu_done, 1)

                act.wait_ge(zeroed, 2 + RING)
                for h in range(HALVES):
                    take_bu(0, 0, h)

                def take_y(k):
                    wait(act, y_mm, STEPS * (k + 1))
                    wait(act, yt_mm, k)
                    act.copy(ytok[:], py[:, 0:2, :]).then_inc(ytok_done, 1)

                def pair(n, last):
                    for e in range(2):
                        k = 2 * n + e
                        for j in range(STEPS + LAG):
                            if j < STEPS:
                                wait(act, adt_mm, STEPS * k + j + 1)
                                wait(act, scanned, STEPS * k + j + 1 - RING)
                                act.activation(decay[j % RING][:, :, 1:W], pa[j % 2][:], ACT.Exp).then_inc(exp_done, 1)
                            if j >= LAG and not (last and e):
                                take_bu(k + 1, 1 - e, 2 * (j - LAG))
                                take_bu(k + 1, 1 - e, 2 * (j - LAG) + 1)
                        if not (isinstance(n, int) and n == 0 and e == 0):
                            take_y(k - 1)

                pairs(act, pair)
                take_y(2 * PAIRS - 1)

            @block.gpsimd
            def _(pool):
                pool.memset(cz[:], 0.0).then_inc(const, 1)
                pool.memset(one[:], 1.0).then_inc(const, 1)
                pool.memset(ident[:], 0.0).then_inc(zeroed, 1)
                pool.wait_ge(zeroed, 3 + RING)
                pool.affine_select(out=ident[:], in_=ident[:], compare_op=ALU.not_equal, fill=1.0, base=0,
                                   pattern=[[-1, P]], channel_multiplier=1).then_inc(const, 1)
                pool.wait_ge(const, 3)

                def copy(out, source):
                    return pool.tensor_tensor(out, source, one[:, None, None, 0:1].to_broadcast(list(source.shape)),
                                              ALU.mult)

                def fill(k, n, e):
                    wait(pool, c_in[e], 16 * (n + 1))
                    for g in range(4):
                        wait(pool, y_mm, STEPS * (k - 1) + 4 * g + 4)
                        rows = cz[:, g // 2, :].rearrange("p (l m) -> p l m", m=ROW)[:, 8 * (g % 2):8 * (g % 2) + 8, 0:P]
                        copy(rows.rearrange("p l (q m) -> p l q m", m=QR)[:, :, :, 0:PAIR],
                             cl[e][:, 32 * g:32 * g + 32, :].rearrange("p (l q) b -> p l q b", q=4)
                             ).then_inc(c_filled, 1)

                def pair(n, last):
                    for e in range(2):
                        fill(2 * n + e, n, e)

                pairs(pool, pair)

            @block.vector
            def _(dve):
                for e in range(RING):
                    dve.memset(decay[e][:, :, 0], 0.0).then_inc(zeroed, 1)
                for e in range(2):
                    dve.memset(hb[e][:, :, 0], 0.0).then_inc(zeroed, 1)
                dve.wait_ge(zeroed, 2 + RING)

                def turned_y(k, n, e):
                    wait(dve, yt_mm, k + 1)
                    wait(dve, y_out[e], 16 * n)
                    for half in range(2):
                        out = ys[e][:, :, half * (P // 2):(half + 1) * (P // 2)]
                        op = dve.tensor_copy(out.rearrange("p b (l q) -> p b l q", q=4),
                                             pt[:, half, :].rearrange("p (q l b) -> p b l q", l=16, b=PAIR))
                    op.then_inc(y_done, 1)

                def pair(n, last):
                    for e in range(2):
                        k = 2 * n + e
                        wait(dve, bu_done, HALVES * (k + 1))
                        if e:
                            wait(dve, scanned, STEPS * k)
                            dve.tensor_copy(hb[1][:, :, 0], hb[0][:, :, P]).then_inc(carried, 1)
                            wait(dve, carried, n + 1)
                        for j in range(STEPS):
                            wait(dve, exp_done, STEPS * k + j + 1)
                            seg = hb[e][:, 8 * j:8 * j + 8, :].rearrange("p d w -> p (d w)")
                            dve.tensor_tensor_scan(seg, decay[j % RING][:].rearrange("p d w -> p (d w)"), seg,
                                                    0.0, ALU.mult, ALU.add).then_inc(scanned, 1)
                            if j == 3 and not (isinstance(n, int) and n == 0):
                                turned_y(k - 2, n - 1, e)

                pairs(dve, pair)
                for e in range(2):
                    turned_y(2 * PAIRS - 2 + e, PAIRS - 1, e)
    release(nc, sems)


class Jobs:

    def __init__(self, jobs, ring, base=0):
        self.names = [n for n, _, _ in jobs]
        self.reader = [e for _, e, _ in jobs]
        self.ring, self.base, self.count = ring, base, len(jobs)
        assert self.count % ring == 0
        self.per = {e: sum(n for _, r, n in jobs if r == e) for e in "va"}
        self.upto = [sum(n for _, r, n in jobs[:k + 1] if r == e) for k, (_, e, _) in enumerate(jobs)]

    def bank(self, name):
        return self.base + self.names.index(name) % self.ring

    def made(self, i, name):
        return i * self.count + self.names.index(name) + 1

    def taken(self, i, name):
        k = self.names.index(name)
        return i * self.per[self.reader[k]] + self.upto[k]

    def before(self, i, name):
        k = self.names.index(name) - self.ring
        at = i if k >= 0 else i - 1
        return self.reader[k], at * self.per[self.reader[k]] + self.upto[k]


def finish_scan(nc, ctx, io, keep, scratch):
    sems = []
    with ExitStack() as c:
        def sb(name, shape, dt=F32):
            return c.enter_context(nc.sbuf_tensor("f_" + name, shape, dt))

        def sem(name):
            sems.append(nc.alloc_semaphore(name="f_" + name))
            return sems[-1]

        mod, mb = keep["mod"], keep["mb"]
        HC = 2 * D // P
        ow = sb("ow", [P, 2, IC, D])
        w1, w2 = sb("w1", [P, FC, 2 * D]), sb("w2", [P, FC, 2 * D])
        w3 = sb("w3", [P, HC, D])
        ones = sb("ones", [P, P])
        x = sb("x", [P, FC, N])
        y = [sb(f"y{r}", [P, IC, N]) for r in range(2)]
        sz = [sb(f"sz{r}", [P, IC, N]) for r in range(2)]
        skip = [sb(f"skip{r}", [P, IC, N]) for r in range(2)]
        yg = [sb(f"yg{r}", [P, IC, N]) for r in range(2)]
        x2, xc, sq, h, xo = (sb(n, [P, FC, N]) for n in ("x2", "xc", "sq", "h", "xo"))
        rstd = sb("rstd", [P, N])
        gate, prod = sb("gate", [P, HC, N]), sb("prod", [P, HC, N])
        ps = c.enter_context(nc.psum_tensor("f_ps", [P, 8, 512], F32))
        jobs = Jobs([("po0", "v", 2), ("po1", "v", 2), ("mean", "v", 1), ("var", "a", 1)]
                    + [(f"{w}{m}", e, 1) for m in range(HC) for w, e in (("g", "a"), ("l", "v"))]
                    + [("out0", "v", 2), ("out1", "v", 2)], 7)
        s = {n: sem(n) for n in ("w_in ones x_in y_in0 y_in1 vec_b mul0 mul1 yg0 yg1 mm taken_v taken_a "
                                 "sq_done ln_done rstd_done xn_done h_done x_out").split()}

        def bank_free(pe, i, name):
            e, value = jobs.before(i, name)
            wait(pe, s["taken_" + e], value)

        with nc.Block() as block:
            @block.sync
            def _(sp):
                for r in range(2):
                    sp.dma_start(ow[:, r], io["out_w"][r].rearrange("(c p) m -> p c m", p=P)).then_inc(s["w_in"], 16)
                for dst, name in ((w1, "mlp_w1"), (w2, "mlp_w2"), (w3, "mlp_w3")):
                    sp.dma_start(dst[:], io[name].rearrange("(c p) m -> p c m", p=P)).then_inc(s["w_in"], 16)

                def unit(i):
                    for r in range(2):
                        wait(sp, s[f"yg{r}"], i)
                        for m in range(IC):
                            sp.dma_start(y[r][:, m, :].rearrange("p (b t) -> p b t", b=PAIR), scratch["Y"][r, m, i]
                                         ).then_inc(s[f"y_in{r}"], 16)
                        sp.dma_start(sz[r][:], scratch["SZ"][r, i]).then_inc(s[f"y_in{r}"], 16)
                        sp.dma_start(skip[r][:], scratch["SK"][r, i]).then_inc(s[f"y_in{r}"], 16)
                    wait(sp, s["taken_v"], jobs.taken(i - 1, "po1"))
                    sp.dma_start(x[:], scratch["X1"][i]).then_inc(s["x_in"], 16)
                    if isinstance(i, int):
                        return
                    wait(sp, s["taken_v"], jobs.taken(i - 1, "out1"))
                    sp.dma_start(scratch["X2"][bass.ds(i - 1, 1)].rearrange("o p c n -> (o p) c n"), xo[:]
                                 ).then_inc(s["x_out"], 16)

                over_units(sp, unit)
                sp.wait_ge(s["taken_v"], jobs.taken(UNITS - 1, "out1"))
                sp.dma_start(scratch["X2"][UNITS - 1], xo[:]).then_inc(s["x_out"], 16)
                sp.wait_ge(s["x_out"], 16 * UNITS)

            @block.tensor
            def _(pe):
                pe.wait_ge(s["w_in"], 80)
                pe.wait_ge(s["ones"], 1)

                def unit(i):
                    for m in range(FC):
                        bank_free(pe, i, f"po{m}")
                        for r in range(2):
                            wait(pe, s[f"yg{r}"], i + 1)
                            for k in range(IC):
                                mm = pe.matmul(ps[:, jobs.bank(f"po{m}"), :], ow[:, r, k, m * P:(m + 1) * P],
                                               yg[r][:, k, :], start=(r == 0 and k == 0), stop=(r == 1 and k == IC - 1))
                        mm.then_inc(s["mm"], 1)
                    bank_free(pe, i, "mean")
                    wait(pe, s["taken_v"], jobs.taken(i, "po1"))
                    for k in range(FC):
                        mm = pe.matmul(ps[:, jobs.bank("mean"), :], ones[:], x2[:, k, :], start=(k == 0), stop=(k == FC - 1))
                    mm.then_inc(s["mm"], 1)
                    bank_free(pe, i, "var")
                    wait(pe, s["sq_done"], i + 1)
                    for k in range(FC):
                        mm = pe.matmul(ps[:, jobs.bank("var"), :], ones[:], sq[:, k, :], start=(k == 0), stop=(k == FC - 1))
                    mm.then_inc(s["mm"], 1)
                    wait(pe, s["h_done"], 4 * i + 4)
                    for m in range(HC):
                        for name, w in ((f"g{m}", w1), (f"l{m}", w2)):
                            bank_free(pe, i, name)
                            for k in range(FC):
                                mm = pe.matmul(ps[:, jobs.bank(name), :], w[:, k, m * P:(m + 1) * P], h[:, k, :],
                                               start=(k == 0), stop=(k == FC - 1))
                            mm.then_inc(s["mm"], 1)
                    wait(pe, s["taken_v"], jobs.taken(i, f"l{HC - 1}"))
                    for m in range(FC):
                        bank_free(pe, i, f"out{m}")
                        for k in range(HC):
                            mm = pe.matmul(ps[:, jobs.bank(f"out{m}"), :], w3[:, k, m * P:(m + 1) * P], prod[:, k, :],
                                           start=(k == 0), stop=(k == HC - 1))
                        mm.then_inc(s["mm"], 1)

                over_units(pe, unit)

            @block.scalar
            def _(act):
                def unit(i):
                    wait(act, s["xn_done"], i)
                    wait(act, s["taken_v"], jobs.taken(i, "mean"))
                    act.activation(sq[:], xc[:], ACT.Square).then_inc(s["sq_done"], 1)
                    wait(act, s["mm"], jobs.made(i, "var"))
                    act.activation(rstd[:], ps[:, jobs.bank("var"), :], ACT.Ln, bias=keep["eps"][:]
                                   ).then_inc(s["taken_a"], 1)
                    wait(act, s["taken_a"], jobs.taken(i, "var"))
                    act.activation(rstd[:], rstd[:], ACT.Exp, scale=-0.5).then_inc(s["rstd_done"], 1)
                    for m in range(HC):
                        wait(act, s["mm"], jobs.made(i, f"g{m}"))
                        act.activation(gate[:, m, :], ps[:, jobs.bank(f"g{m}"), :], ACT.Silu).then_inc(s["taken_a"], 1)

                over_units(act, unit)

            @block.vector
            def _(dve):
                dve.memset(ones[:], 1.0 / D).then_inc(s["ones"], 1)

                def unit(i):
                    wait(dve, s["taken_v"], jobs.taken(i - 1, "out1"))
                    dve.tensor_copy(mb[:], mod[:, :, bass.ds(PAIR * i, PAIR)].rearrange("p m b -> p b m")
                                    ).then_inc(s["vec_b"], 1)
                    for r in range(2):
                        wait(dve, s[f"y_in{r}"], 16 * (IC + 2) * (i + 1))
                        dve.tensor_tensor(y[r][:], y[r][:], sz[r][:], ALU.mult).then_inc(s[f"mul{r}"], 1)
                        wait(dve, s[f"mul{r}"], i + 1)
                        wait(dve, s["mm"], jobs.made(i, "po1") - jobs.count)
                        out = yg[r][:].rearrange("p c (b t) -> p (c b) t", t=T)
                        dve.tensor_tensor(out[:, :, ::-1] if r else out, y[r][:].rearrange("p c (b t) -> p (c b) t", t=T),
                                          skip[r][:].rearrange("p c (b t) -> p (c b) t", t=T), ALU.add
                                          ).then_inc(s[f"yg{r}"], 1)
                    wait(dve, s["x_in"], 16 * (i + 1))
                    wait(dve, s["vec_b"], i + 1)
                    for m in range(FC):
                        wait(dve, s["mm"], jobs.made(i, f"po{m}"))
                        for b in range(PAIR):
                            cols = slice(b * T, (b + 1) * T)
                            ch = MOD["m_g"] + m
                            dve.scalar_tensor_tensor(x2[:, m, cols], ps[:, jobs.bank(f"po{m}"), cols],
                                                     mb[:, b, ch:ch + 1], x[:, m, cols], ALU.mult, ALU.add
                                                     ).then_inc(s["taken_v"], 1)
                    wait(dve, s["mm"], jobs.made(i, "mean"))
                    wait(dve, s["taken_v"], jobs.taken(i, "po1"))
                    dve.tensor_tensor(xc[:], x2[:], ps[:, jobs.bank("mean"), None, :].to_broadcast([P, FC, N]),
                                      ALU.subtract).then_inc(s["taken_v"], 1)
                    wait(dve, s["rstd_done"], i + 1)
                    dve.tensor_tensor(xc[:], xc[:], rstd[:, None, :].to_broadcast([P, FC, N]), ALU.mult
                                      ).then_inc(s["xn_done"], 1)
                    wait(dve, s["xn_done"], i + 1)
                    for m in range(FC):
                        for b in range(PAIR):
                            cols = slice(b * T, (b + 1) * T)
                            sc, sh = MOD["p_sc"] + m, MOD["p_sh"] + m
                            dve.tensor_scalar(h[:, m, cols], xc[:, m, cols], mb[:, b, sc:sc + 1], mb[:, b, sh:sh + 1],
                                              ALU.mult, ALU.add).then_inc(s["h_done"], 1)
                    for m in range(HC):
                        wait(dve, s["mm"], jobs.made(i, f"l{m}"))
                        wait(dve, s["taken_a"], jobs.taken(i, f"g{m}"))
                        dve.tensor_tensor(prod[:, m, :], ps[:, jobs.bank(f"l{m}"), :], gate[:, m, :], ALU.mult
                                          ).then_inc(s["taken_v"], 1)
                    wait(dve, s["x_out"], 16 * i)
                    for m in range(FC):
                        wait(dve, s["mm"], jobs.made(i, f"out{m}"))
                        for b in range(PAIR):
                            cols = slice(b * T, (b + 1) * T)
                            ch = MOD["p_g"] + m
                            dve.scalar_tensor_tensor(xo[:, m, cols], ps[:, jobs.bank(f"out{m}"), cols],
                                                     mb[:, b, ch:ch + 1], x2[:, m, cols], ALU.mult, ALU.add
                                                     ).then_inc(s["taken_v"], 1)

                over_units(dve, unit)
    release(nc, sems)


def transformer(nc, ctx, io, keep, scratch, layer, x_from, x_to):
    HR, dh = (DH2, DH2) if layer == 2 else (PADH, DH3)
    HT = P // HR
    MT = H // HT
    VW = H * HR
    VB = VW // 512
    HEADS = PAIR * H
    TILES = PAIR * MT
    MC = MLP // P
    SCALE = dh ** -0.5

    sems = []
    with ExitStack() as c:
        def sb(name, shape, dt=F32):
            return c.enter_context(nc.sbuf_tensor(f"t{layer}_" + name, shape, dt))

        def sem(name):
            sems.append(nc.alloc_semaphore(name=f"t{layer}_" + name))
            return sems[-1]

        vec, mod, mb = keep["vec"], keep["mod"], keep["mb"]
        wqkv = sb("wqkv", [P, FC, 3 * VW])
        wo = sb("wo", [P, MT, D])
        w1 = sb("w1", [P, FC, MLP])
        w2 = sb("w2", [P, MC, D])
        ones, ident = sb("ones", [P, P]), sb("ident", [P, P])
        x, x2, xc, h, xo = (sb(n, [P, FC, N]) for n in ("x", "x2", "xc", "h", "xo"))
        sq = h
        tmp = sb("tmp", [P, N])
        rstd = sb("rstd", [P, N])
        qf, kf = sb("q", [P, MT, N]), sb("k", [P, MT, N])
        vt = sb("v", [P, N // P, VW])
        o = sb("o", [P, MT, N])
        hid = qf if MT == MC else sb("hid", [P, MC, N])
        prob = [sb(f"prob{e}", [P, 2, T]) for e in range(2)]
        probt = [sb(f"probt{e}", [P, 2, T]) for e in range(2)]
        nmax = [sb(f"nmax{e}", [P, 2]) for e in range(2)]
        rsum = [sb(f"rsum{e}", [P, 2]) for e in range(2)]
        rinv = [sb(f"rinv{e}", [P, 2]) for e in range(2)]
        ps = c.enter_context(nc.psum_tensor(f"t{layer}_ps", [P, 8, 512], F32))

        jobs = Jobs([("mean1", "v", 1), ("var1", "a", 1)]
                    + [(f"{w}{m}", "v", 1) for w in "qk" for m in range(MT)]
                    + [(f"v{t}_{m}", "a", 1) for t in range(N // P) for m in range(VB)]
                    + [("proj0", "v", 2), ("proj1", "v", 2), ("mean2", "v", 1), ("var2", "a", 1)]
                    + [(f"f{m}", "a", 1) for m in range(MC)]
                    + [("out0", "v", 2), ("out1", "v", 2)], 2, base=6)
        s = {n: sem(n) for n in ("w_in ones ident x_in vec_b mm taken_v taken_a sq ln rstd xn h s_mm max exp recip "
                                 "norm t_mm pt pv o_done x2_done xo_done x_out").split()}
        steps = {1: ("mean1", "var1", f"a{layer}"), 2: ("mean2", "var2", f"f{layer}")}
        bo, b1, b2 = (VEC[f"{n}{layer}"][0] for n in ("bo", "b1", "b2"))

        def bank(name):
            return ps[:, jobs.bank(name), :]

        with nc.Block() as block:
            @block.sync
            def _(sp):
                for dst, name in ((wqkv, f"Wqkv{layer}"), (wo, f"Wo{layer}"), (w1, f"W1{layer}"), (w2, f"W2{layer}")):
                    sp.dma_start(dst[:], io[name].rearrange("(c p) m -> p c m", p=P)).then_inc(s["w_in"], 16)

                def unit(i):
                    wait(sp, s["x2_done"], 2 * i)
                    sp.dma_start(x[:], x_from[i]).then_inc(s["x_in"], 16)
                    if isinstance(i, int):
                        return
                    wait(sp, s["xo_done"], 2 * i)
                    sp.dma_start(x_to[bass.ds(i - 1, 1)].rearrange("o p c n -> (o p) c n"), xo[:]
                                 ).then_inc(s["x_out"], 16)

                over_units(sp, unit)
                sp.wait_ge(s["xo_done"], 2 * UNITS)
                sp.dma_start(x_to[UNITS - 1], xo[:]).then_inc(s["x_out"], 16)
                sp.wait_ge(s["x_out"], 16 * UNITS)

            @block.gpsimd
            def _(pool):
                pool.memset(ident[:], 0.0).then_inc(s["ident"], 1)
                pool.wait_ge(s["ident"], 1)
                pool.affine_select(out=ident[:], in_=ident[:], compare_op=ALU.not_equal, fill=1.0, base=0,
                                   pattern=[[-1, P]], channel_multiplier=1).then_inc(s["ident"], 1)

            @block.tensor
            def _(pe):
                def linear(i, name, pairs):
                    e, value = jobs.before(i, name)
                    wait(pe, s["taken_" + e], value)
                    for k, (w, v) in enumerate(pairs):
                        mm = pe.matmul(bank(name), w, v, start=(k == 0), stop=(k == len(pairs) - 1))
                    mm.then_inc(s["mm"], 1)

                def scores(i, n):
                    wait(pe, s["exp"], i * HEADS + n - 1)
                    b, tile, lo = n // H, (n % H) // HT, HR * (n % HT)
                    for e in range(2):
                        mm = pe.matmul(ps[:, n % 2, e * T:(e + 1) * T],
                                       qf[lo:lo + HR, tile, b * T + e * P:b * T + (e + 1) * P],
                                       kf[lo:lo + HR, tile, b * T:(b + 1) * T], start=True, stop=True)
                    mm.then_inc(s["s_mm"], 1)

                def turn(i, n):
                    wait(pe, s["norm"], i * HEADS + n + 1)
                    wait(pe, s["pt"], i * HEADS + n - 1)
                    for e in range(2):
                        for kb in range(2):
                            mm = pe.transpose(ps[:, 2 + n % 2, kb * T + e * P:kb * T + (e + 1) * P],
                                              prob[n % 2][:, e, kb * P:(kb + 1) * P], ident[:])
                    mm.then_inc(s["t_mm"], 1)

                def values(i, n):
                    wait(pe, s["pt"], i * HEADS + n + 1)
                    b, tile, lo = n // H, n // HT, HR * (n % HT)
                    if n % HT == 0:
                        wait(pe, s["o_done"], i * TILES + tile - 1)
                    for kb in range(2):
                        mm = pe.matmul(ps[lo:lo + HR, 4 + tile % 2, 0:T],
                                       vt[:, 2 * b + kb, (n % H) * HR:(n % H + 1) * HR],
                                       probt[n % 2][:, kb, :], start=(kb == 0), stop=(kb == 1))
                    mm.then_inc(s["pv"], 1)

                pe.wait_ge(s["w_in"], 64)
                pe.wait_ge(s["ones"], 1)
                pe.wait_ge(s["ident"], 2)

                def unit(i):
                    wait(pe, s["x_in"], 16 * (i + 1))
                    linear(i, "mean1", [(ones[:], x[:, k, :]) for k in range(FC)])
                    wait(pe, s["sq"], 2 * i + 1)
                    linear(i, "var1", [(ones[:], sq[:, k, :]) for k in range(FC)])
                    wait(pe, s["h"], 8 * i + 4)
                    for w in range(2):
                        for m in range(MT):
                            linear(i, f"{'qk'[w]}{m}", [(wqkv[:, k, w * VW + m * P:w * VW + (m + 1) * P], h[:, k, :])
                                                        for k in range(FC)])
                    for t in range(N // P):
                        for m in range(VB):
                            linear(i, f"v{t}_{m}", [(h[:, k, t * P:(t + 1) * P],
                                                     wqkv[:, k, 2 * VW + m * 512:2 * VW + (m + 1) * 512])
                                                    for k in range(FC)])
                    wait(pe, s["taken_v"], jobs.taken(i, f"k{MT - 1}"))
                    wait(pe, s["taken_a"], jobs.taken(i, f"v{N // P - 1}_{VB - 1}"))
                    for n in range(HEADS + 2):
                        if n < HEADS:
                            scores(i, n)
                        if 1 <= n <= HEADS:
                            turn(i, n - 1)
                        if n >= 2:
                            values(i, n - 2)
                    wait(pe, s["o_done"], TILES * (i + 1))
                    for m in range(FC):
                        linear(i, f"proj{m}", [(wo[:, k, m * P:(m + 1) * P], o[:, k, :]) for k in range(MT)])
                    wait(pe, s["x2_done"], 2 * i + 2)
                    linear(i, "mean2", [(ones[:], x2[:, k, :]) for k in range(FC)])
                    wait(pe, s["sq"], 2 * i + 2)
                    linear(i, "var2", [(ones[:], sq[:, k, :]) for k in range(FC)])
                    wait(pe, s["h"], 8 * i + 8)
                    for m in range(MC):
                        linear(i, f"f{m}", [(w1[:, k, m * P:(m + 1) * P], h[:, k, :]) for k in range(FC)])
                    wait(pe, s["taken_a"], jobs.taken(i, f"f{MC - 1}"))
                    for m in range(FC):
                        linear(i, f"out{m}", [(w2[:, k, m * P:(m + 1) * P], hid[:, k, :]) for k in range(MC)])

                over_units(pe, unit)

            @block.scalar
            def _(act):
                def norm(i, g):
                    mean, var, _ = steps[g]
                    wait(act, s["taken_v"], jobs.taken(i, mean))
                    wait(act, s["mm"], jobs.made(i, mean))
                    act.activation(sq[:], xc[:], ACT.Square).then_inc(s["sq"], 1)
                    wait(act, s["mm"], jobs.made(i, var))
                    act.activation(rstd[:], bank(var), ACT.Ln, bias=keep["eps"][:]).then_inc(s["taken_a"], 1)
                    wait(act, s["taken_a"], jobs.taken(i, var))
                    act.activation(rstd[:], rstd[:], ACT.Exp, scale=-0.5).then_inc(s["rstd"], 1)

                def unit(i):
                    norm(i, 1)
                    for t in range(N // P):
                        for m in range(VB):
                            wait(act, s["mm"], jobs.made(i, f"v{t}_{m}"))
                            act.copy(vt[:, t, m * 512:(m + 1) * 512], bank(f"v{t}_{m}")).then_inc(s["taken_a"], 1)
                    for n in range(HEADS + 1):
                        if n < HEADS:
                            wait(act, s["max"], i * HEADS + n + 1)
                            wait(act, s["t_mm"], i * HEADS + n - 1)
                            for e in range(2):
                                op = act.activation(prob[n % 2][:, e, :], ps[:, n % 2, e * T:(e + 1) * T], ACT.Exp,
                                                    bias=nmax[n % 2][:, e:e + 1], accum_out=rsum[n % 2][:, e:e + 1])
                            op.then_inc(s["exp"], 1)
                        if n >= 1:
                            m = n - 1
                            wait(act, s["t_mm"], i * HEADS + m + 1)
                            wait(act, s["pv"], i * HEADS + m - 1)
                            act.copy(probt[m % 2][:], ps[:, 2 + m % 2, :].rearrange("p (a t) -> p a t", t=T)
                                     ).then_inc(s["pt"], 1)
                    norm(i, 2)
                    for m in range(MC):
                        wait(act, s["mm"], jobs.made(i, f"f{m}"))
                        act.activation(hid[:, m, :], bank(f"f{m}"), ACT.Gelu, bias=vec[:, b1 + m:b1 + m + 1]
                                       ).then_inc(s["taken_a"], 1)

                over_units(act, unit)

            @block.vector
            def _(dve):
                def norm(i, g, source):
                    mean, _, name = steps[g]
                    wait(dve, s["mm"], jobs.made(i, mean))
                    dve.tensor_tensor(xc[:], source[:], ps[:, jobs.bank(mean), None, :].to_broadcast([P, FC, N]),
                                      ALU.subtract).then_inc(s["taken_v"], 1)
                    wait(dve, s["rstd"], 2 * i + g)
                    wait(dve, s["taken_v"], jobs.taken(i, mean))
                    dve.tensor_tensor(xc[:], xc[:], rstd[:, None, :].to_broadcast([P, FC, N]), ALU.mult
                                      ).then_inc(s["xn"], 1)
                    wait(dve, s["xn"], 2 * i + g)
                    for m in range(FC):
                        for b in range(PAIR):
                            cols = slice(b * T, (b + 1) * T)
                            sc, sh = MOD[name + "_sc"] + m, MOD[name + "_sh"] + m
                            dve.tensor_scalar(h[:, m, cols], xc[:, m, cols], mb[:, b, sc:sc + 1], mb[:, b, sh:sh + 1],
                                              ALU.mult, ALU.add).then_inc(s["h"], 1)

                def residual(i, g, what, bias, dst, source, done):
                    for m in range(FC):
                        wait(dve, s["mm"], jobs.made(i, f"{what}{m}"))
                        wait(dve, s[done], 2 * i + m)
                        for b in range(PAIR):
                            cols = slice(b * T, (b + 1) * T)
                            ch = MOD[steps[g][2] + "_g"] + m
                            dve.tensor_scalar(tmp[:, cols], ps[:, jobs.bank(f"{what}{m}"), cols],
                                              vec[:, bias + m:bias + m + 1], mb[:, b, ch:ch + 1],
                                              ALU.add, ALU.mult).then_inc(s["taken_v"], 1)
                        wait(dve, s["taken_v"], jobs.taken(i, f"{what}{m}"))
                        dve.tensor_tensor(dst[:, m, :], tmp[:], source[:, m, :], ALU.add).then_inc(s[done], 1)

                dve.memset(ones[:], 1.0 / D).then_inc(s["ones"], 1)

                def unit(i):
                    wait(dve, s["xo_done"], 2 * i)
                    dve.tensor_copy(mb[:], mod[:, :, bass.ds(PAIR * i, PAIR)].rearrange("p m b -> p b m")
                                    ).then_inc(s["vec_b"], 1)
                    wait(dve, s["x_in"], 16 * (i + 1))
                    wait(dve, s["vec_b"], i + 1)
                    norm(i, 1, x)
                    for w, dst in (("q", qf), ("k", kf)):
                        for m in range(MT):
                            name = f"{w}{m}"
                            wait(dve, s["mm"], jobs.made(i, name))
                            scale = SCALE if w == "q" else 1.0
                            if layer == 3:
                                at = VEC[f"b{w}3"][0] + m
                                op = dve.tensor_scalar(dst[:, m, :], bank(name), vec[:, at:at + 1], scale,
                                                       ALU.add, ALU.mult)
                            else:
                                op = dve.tensor_scalar(dst[:, m, :], bank(name), scale, None, ALU.mult)
                            op.then_inc(s["taken_v"], 1)
                    for n in range(HEADS + 4):
                        if n < HEADS:
                            wait(dve, s["s_mm"], i * HEADS + n + 1)
                            wait(dve, s["exp"], i * HEADS + n - 1)
                            dve.tensor_reduce(nmax[n % 2][:], ps[:, n % 2, :].rearrange("p (a t) -> p a t", t=T),
                                              axis=AX.X, op=ALU.max, negate=True).then_inc(s["max"], 1)
                        if 1 <= n <= HEADS:
                            m = n - 1
                            wait(dve, s["exp"], i * HEADS + m + 1)
                            dve.reciprocal(rinv[m % 2][:], rsum[m % 2][:]).then_inc(s["recip"], 1)
                            wait(dve, s["recip"], i * HEADS + m + 1)
                            for e in range(2):
                                op = dve.tensor_scalar(prob[m % 2][:, e, :], prob[m % 2][:, e, :],
                                                       rinv[m % 2][:, e:e + 1], None, ALU.mult)
                            op.then_inc(s["norm"], 1)
                        m = n - 3
                        if 0 <= m < HEADS and m % HT == HT - 1:
                            tile = m // HT
                            wait(dve, s["pv"], i * HEADS + m + 1)
                            wait(dve, s["mm"], jobs.made(i, "proj1") - jobs.count)
                            b, col = tile // MT, tile % MT
                            out, src = o[:, col, b * T:(b + 1) * T], ps[:, 4 + tile % 2, 0:T]
                            if layer == 3:
                                at = VEC["bv3"][0] + col
                                op = dve.tensor_scalar(out, src, vec[:, at:at + 1], None, ALU.add)
                            else:
                                op = dve.tensor_copy(out, src)
                            op.then_inc(s["o_done"], 1)
                    residual(i, 1, "proj", bo, x2, x, "x2_done")
                    wait(dve, s["x2_done"], 2 * i + 2)
                    norm(i, 2, x2)
                    wait(dve, s["x_out"], 16 * i)
                    residual(i, 2, "out", b2, xo, x2, "xo_done")

                over_units(dve, unit)
    release(nc, sems)


def finish(nc, ctx, io, keep, scratch, out):
    finish_scan(nc, ctx, io, keep, scratch)
    transformer(nc, ctx, io, keep, scratch, 2, scratch["X2"], scratch["X4"])
    transformer(nc, ctx, io, keep, scratch, 3, scratch["X4"], out)


def program(nc, io, out):
    def dram(name, shape, dt=F32):
        return nc.dram_tensor(name, shape, dt, kind="Internal").ap()

    d3 = dram("D3", [2, IC, UNITS, PARTS, PAIR, TC, P, P], BF16)
    u3 = dram("U3", [2, IC, UNITS, PARTS, PAIR, TC, P, P], BF16)
    b3 = dram("B3", [2, UNITS, PARTS, PAIR, TC, P, PAIR * S], BF16)
    c2 = dram("C2", [2, UNITS, P, T, PAIR])
    y = dram("Y", [2, IC, UNITS, P, PAIR, T])
    scratch = {
        "A3": dram("A3", [2 * IC, PARTS, PAIR, P, PAIR * S], BF16),
        "BB": dram("BB", [2, RANK, NB, D]),
        "X1": dram("X1", [UNITS, P, FC, N]), "X2": dram("X2", [UNITS, P, FC, N]),
        "X4": dram("X4", [UNITS, P, FC, N]),
        "SZ": dram("SZ", [2, UNITS, P, IC, N]), "SK": dram("SK", [2, UNITS, P, IC, N]),
        "D3": d3, "U3": u3, "B3": b3, "C2": c2, "Y": y,
        "D3f": d3.rearrange("r m i j b c d t -> (r m i) j b c d t"),
        "U3f": u3.rearrange("r m i j b c t d -> (r m i) j b c t d"),
        "B3f": b3.rearrange("r i j b c t f -> (r i) j b c t f"),
        "C2f": c2.rearrange("r i p t b -> (r i) p t b"),
        "Yf": y.rearrange("r m i p b t -> (r m i) p b t"),
    }
    with ExitStack() as ctx:
        def sb(name, shape, dt=F32):
            return ctx.enter_context(nc.sbuf_tensor(name, shape, dt))

        keep = {"vec": sb("vec", [P, NVEC]), "mod": sb("mod", [P, NMOD, NB]), "wa": sb("wa", [P, 32, NB]),
                "eps": sb("eps", [P, 1]), "mb": sb("mb", [P, PAIR, NMOD]),
                "wab": sb("wab", [P, PAIR, 2, RANK, FC])}
        conditioning(nc, ctx, io, keep, scratch)
        prepare(nc, ctx, io, keep, scratch)
        scan(nc, ctx, io, keep, scratch)
        finish(nc, ctx, io, keep, scratch, out)


def columns(v):
    return v.reshape(-1, P).T


def padded(v):
    v = v.reshape(v.shape[:-1] + (H, DH3))
    out = np.zeros(v.shape[:-1] + (PADH,), v.dtype)
    out[..., :DH3] = v
    return out.reshape(v.shape[:-2] + (H * PADH,))


def layout(a):
    def b2(q):
        w = q.reshape(q.shape[:-1] + (4, D, RANK))
        w = np.swapaxes(w, -1, -2)
        return (np.ascontiguousarray(w[..., 0::2, :, :]).reshape(q.shape[:-1] + (4096,)),
                np.ascontiguousarray(w[..., 1::2, :, :]).reshape(q.shape[:-1] + (4096,)))

    w2a, w2b = b2(a["L0_cond_W2"])
    b2a, b2b = b2(a["L0_cond_b2"])
    bq, bk, bv = (padded(v) for v in np.split(a["L3_cond_bqkv"], 3))
    wq, wk, wv = (padded(v) for v in np.split(a["L3_cond_Wqkv"], 3, axis=1))
    vecs = {"ln_g": a["L0_cond_ln_g"], "ln_b": a["L0_cond_ln_b"], "l0b1": a["L0_cond_b1"], "l0b2a": b2a,
            "mod_b": np.concatenate([a["L1_cond_adaln_mamba_b"], a["L1_cond_adaln_mlp_b"],
                                     a["L2_cond_b_mod"], a["L3_cond_bt"]]),
            "g1": a["L3_cond_g1"], "be1": a["L3_cond_be1"], "g2": a["L3_cond_g2"], "be2": a["L3_cond_be2"],
            "dtb0": a["L1_cond_fwd_dt_bias"], "dtb1": a["L1_cond_bwd_dt_bias"],
            "D0": a["L1_cond_fwd_D"], "D1": a["L1_cond_bwd_D"],
            "bo2": a["L2_cond_b_out"], "b12": a["L2_cond_b1"], "b22": a["L2_cond_b2"],
            "bq3": bq, "bk3": bk, "bv3": bv, "bo3": a["L3_cond_bproj"], "b13": a["L3_cond_b1"],
            "b23": a["L3_cond_b2"]}
    return {
        "vecs": np.concatenate([columns(vecs[n]) for n in VEC], axis=1),
        "condT": a["cond_1024"].reshape(NB, FC, P).transpose(2, 1, 0),
        "xT": a["x"].reshape(UNITS, PAIR, T, FC, P).transpose(0, 4, 3, 1, 2).reshape(UNITS, P, FC, N),
        "l0W1": a["L0_cond_W1"], "l0W2a": w2a, "l0W2b": w2b, "l0b2b": b2b.reshape(1, 4096),
        "mamba_w": a["L1_cond_adaln_mamba_w"], "mlp_w": a["L1_cond_adaln_mlp_w"],
        "W_mod": a["L2_cond_W_mod"], "Wt": a["L3_cond_Wt"],
        "A_log": np.concatenate([a["L1_cond_fwd_A_log"], a["L1_cond_bwd_A_log"]]),
        "in_w": np.stack([a["L1_cond_fwd_in_w"], a["L1_cond_bwd_in_w"]]),
        "xproj_w": np.stack([a["L1_cond_fwd_xproj_w"], a["L1_cond_bwd_xproj_w"]]),
        "out_w": np.stack([a["L1_cond_fwd_out_w"], a["L1_cond_bwd_out_w"]]),
        "mlp_w1": a["L1_cond_mlp_w1"], "mlp_w2": a["L1_cond_mlp_w2"], "mlp_w3": a["L1_cond_mlp_w3"],
        "Wqkv2": a["L2_cond_W_qkv"], "Wo2": a["L2_cond_W_out"], "W12": a["L2_cond_W1"], "W22": a["L2_cond_W2"],
        "Wqkv3": np.concatenate([wq, wk, wv], axis=1), "Wo3": padded(a["L3_cond_Wproj"].T).T,
        "W13": a["L3_cond_W1"], "W23": a["L3_cond_W2"],
    }


def kernel(**inputs):
    import concourse.bacc as bacc
    from concourse.bass_utils import run_bass_kernel_spmd

    nc = bacc.Bacc("TRN2", target_bir_lowering=False, num_devices=1)
    arrays = {"in_" + n: np.ascontiguousarray(v)
              for n, v in layout({n: np.asarray(v) for n, v in inputs.items()}).items()}
    io = {n[3:]: nc.dram_tensor(n, v.shape, mybir.dt.from_np(v.dtype), kind="ExternalInput").ap()
          for n, v in arrays.items()}
    out = nc.dram_tensor("out", [UNITS, P, FC, N], F32, kind="ExternalOutput").ap()
    program(nc, io, out)
    got = run_bass_kernel_spmd(nc, [arrays], core_ids=[0]).results[0]["out"]
    return np.ascontiguousarray(
        got.reshape(UNITS, P, FC, PAIR, T).transpose(0, 3, 4, 2, 1)).reshape(NB, T, D)
```

```python
import numpy as np
from contextlib import ExitStack

import concourse.bass as bass
from concourse import mybir

F32 = mybir.dt.float32
BF16 = mybir.dt.bfloat16
ALU = mybir.AluOpType
ACT = mybir.ActivationFunctionType
AX = mybir.AxisListType

P = 128
NB, T, D = 16, 256, 256
PAIR = 2
UNITS = NB // PAIR
N = PAIR * T
FC = D // P
RANK = 8
DI = 2 * D
IC = DI // P
S = 64
PARTS = 3
ROWS = PARTS * PARTS * PAIR
TC = T // P
TS = 64
Q = 4
QR = P // Q
EPS = 1e-5
H = 16
DH2, DH3 = 64, 16
PADH = 32
MLP = 1024

VEC = {}


def _columns():
    at = 0
    for name, n in (("ln_g", 2), ("ln_b", 2), ("l0b1", 2), ("l0b2a", 32), ("mod_b", 36),
                    ("g1", 2), ("be1", 2), ("g2", 2), ("be2", 2),
                    ("dtb0", 4), ("dtb1", 4), ("D0", 4), ("D1", 4),
                    ("bo2", 2), ("b12", 8), ("b22", 2),
                    ("bq3", 4), ("bk3", 4), ("bv3", 4), ("bo3", 2), ("b13", 8), ("b23", 2)):
        VEC[name] = (at, at + n)
        at += n
    return at


NVEC = _columns()

MOD = {n: 2 * k for k, n in enumerate(
    ("m_sh", "m_sc", "m_g", "p_sh", "p_sc", "p_g",
     "a2_sh", "a2_sc", "a2_g", "f2_sh", "f2_sc", "f2_g",
     "a3_sh", "a3_sc", "a3_g", "f3_sh", "f3_sc", "f3_g"))}
NMOD = 36


def wait(eng, sem, value):
    if isinstance(value, int) and value <= 0:
        return
    eng.wait_ge(sem, value)


def release(nc, sems):
    nc.clear_and_free_semaphores(sems)
    nc.all_engine_barrier()


def over_units(eng, body, count=UNITS):
    body(0)
    with eng.Fori(1, count) as i:
        body(i)


def conditioning(nc, ctx, io, keep, scratch):
    sems = []
    with ExitStack() as c:
        def sb(name, shape, dt=F32):
            return c.enter_context(nc.sbuf_tensor(name, shape, dt))

        def sem(name):
            sems.append(nc.alloc_semaphore(name="c_" + name))
            return sems[-1]

        vec, mod, wa = keep["vec"], keep["mod"], keep["wa"]
        cond = sb("cond", [P, FC, NB])
        ones = sb("c_ones", [P, P])
        w1 = sb("w1", [P, FC, D])
        w2a = sb("w2a", [P, FC, 4096])
        w2b = sb("w2b", [P, FC, 4096])
        b2b = sb("b2b", [NB, 4096])
        wm = sb("wm", [P, FC, NMOD * P])
        xc = sb("c_xc", [P, FC, NB])
        sq = sb("c_sq", [P, FC, NB])
        rstd = sb("c_rstd", [P, NB])
        xn = sb("c_xn", [P, FC, NB])
        hn = sb("c_hn", [P, FC, NB])
        hid = sb("c_hid", [P, FC, NB])
        sil = sb("c_sil", [P, FC, NB])
        wbb = sb("c_wbb", [NB, 4096])
        alog = sb("c_alog", [P, 2 * IC, S])
        aneg = sb("c_aneg", [P, 2 * IC, S])
        ares = sb("c_ares", [P, 2 * IC, S])
        az = sb("c_az", [P, 2 * IC, PARTS, PAIR, PAIR, S], BF16)
        gsc = sb("c_gsc", [P, 4, NB])
        ps = c.enter_context(nc.psum_tensor("c_ps", [P, 4, 512], F32))
        pw = c.enter_context(nc.psum_tensor("c_pw", [P, 4, 512], F32))

        small_in, w1_in, w2_in, wm_in, a_in = (sem(n) for n in ("small_in", "w1_in", "w2_in", "wm_in", "a_in"))
        ones_set, mean_mm, xc_done, sq_done, var_mm, rstd_done, xn_done, hn_done = (
            sem(n) for n in ("ones", "mean", "xc", "sq", "var", "rstd", "xn", "hn"))
        ln_done, hid_mm, hid_done, sil_done, wa_mm, bb_mm, bb_done, mod_mm, mod_done = (
            sem(n) for n in ("ln", "hidmm", "hid", "sil", "wamm", "bbmm", "bb", "modmm", "mod"))
        bb_out, a_out, exp_done, az_zero, split_v, split_a, one_done, fold, eps_set = (
            sem(n) for n in ("bbout", "aout", "exp", "azz", "splitv", "splita", "one", "fold", "eps"))

        with nc.Block() as block:
            @block.sync
            def _(sp):
                sp.dma_start(vec[:], io["vecs"]).then_inc(small_in, 16)
                sp.dma_start(cond[:], io["condT"]).then_inc(small_in, 16)
                sp.dma_start(b2b[:], io["l0b2b"].to_broadcast([NB, 4096])).then_inc(small_in, 16)
                sp.dma_start(w1[:], io["l0W1"].rearrange("(c p) m -> p c m", p=P)).then_inc(w1_in, 16)
                sp.dma_start(alog[:], io["A_log"].rearrange("(n p) s -> p n s", p=P)).then_inc(a_in, 16)
                at = 0
                for name in ("mamba_w", "mlp_w", "W_mod", "Wt"):
                    n = io[name].shape[1]
                    sp.dma_start(wm[:, :, at:at + n], io[name].rearrange("(c p) m -> p c m", p=P)).then_inc(wm_in, 16)
                    at += n
                sp.dma_start(w2a[:], io["l0W2a"].rearrange("(c p) m -> p c m", p=P)).then_inc(w2_in, 16)
                sp.dma_start(w2b[:], io["l0W2b"].rearrange("(c p) m -> p c m", p=P)).then_inc(w2_in, 16)
                sp.wait_ge(split_v, 4)
                sp.wait_ge(split_a, 4)
                for j in range(PARTS):
                    for i in range(PARTS):
                        for b in range(PAIR):
                            sp.dma_start(scratch["A3"][:, i, j, b].rearrange("n d f -> d n f"),
                                         az[:, :, i, b].rearrange("p n c s -> p n (c s)")).then_inc(a_out, 16)
                sp.wait_ge(bb_done, 8)
                sp.dma_start(scratch["BB"].rearrange("q r b d -> b (q r) d"),
                             wbb[:].rearrange("b (m d) -> b m d", d=D)).then_inc(bb_out, 16)
                sp.wait_ge(a_out, 16 * PARTS * PARTS * PAIR)
                sp.wait_ge(bb_out, 16)

            @block.tensor
            def _(pe):
                pe.wait_ge(ones_set, 1)
                pe.wait_ge(small_in, 48)
                for k in range(FC):
                    mm = pe.matmul(ps[:, 0, 0:NB], ones[:], cond[:, k, :], start=(k == 0), stop=(k == FC - 1))
                mm.then_inc(mean_mm, 1)
                pe.wait_ge(sq_done, 1)
                for k in range(FC):
                    mm = pe.matmul(ps[:, 1, 0:NB], ones[:], sq[:, k, :], start=(k == 0), stop=(k == FC - 1))
                mm.then_inc(var_mm, 1)
                pe.wait_ge(wm_in, 64)
                for m in range(NMOD):
                    if m == 12:
                        pe.wait_ge(sil_done, 1)
                    src = cond if m < 12 else sil
                    out = ps[:, 2, m * NB:(m + 1) * NB] if m < 12 else ps[:, 3, (m - 12) * NB:(m - 11) * NB]
                    for k in range(FC):
                        mm = pe.matmul(out, wm[:, k, m * P:(m + 1) * P], src[:, k, :],
                                       start=(k == 0), stop=(k == FC - 1))
                mm.then_inc(mod_mm, 1)
                pe.wait_ge(w1_in, 16)
                pe.wait_ge(hn_done, 2)
                for m in range(FC):
                    for k in range(FC):
                        mm = pe.matmul(ps[:, 0, 64 + m * NB:64 + (m + 1) * NB], w1[:, k, m * P:(m + 1) * P],
                                       hn[:, k, :], start=(k == 0), stop=(k == FC - 1))
                mm.then_inc(hid_mm, 1)
                pe.wait_ge(w2_in, 32)
                pe.wait_ge(hid_done, 2)
                for m in range(32):
                    for k in range(FC):
                        mm = pe.matmul(pw[:, 0, m * NB:(m + 1) * NB], w2a[:, k, m * P:(m + 1) * P],
                                       hid[:, k, :], start=(k == 0), stop=(k == FC - 1))
                mm.then_inc(wa_mm, 1)
                for m in range(8):
                    if m >= 3:
                        pe.wait_ge(bb_done, m - 2)
                    for k in range(FC):
                        mm = pe.matmul(pw[0:NB, 1 + m % 3, :], hid[:, k, :], w2b[:, k, m * 512:(m + 1) * 512],
                                       start=(k == 0), stop=(k == FC - 1))
                    mm.then_inc(bb_mm, 1)

            @block.scalar
            def _(act):
                act.wait_ge(xc_done, 1)
                act.activation(sq[:], xc[:], ACT.Square).then_inc(sq_done, 1)
                act.wait_ge(var_mm, 1)
                act.wait_ge(eps_set, 1)
                act.activation(rstd[:], ps[:, 1, 0:NB], ACT.Ln, bias=keep["eps"][:]).then_inc(ln_done, 1)
                act.wait_ge(ln_done, 1)
                act.activation(rstd[:], rstd[:], ACT.Exp, scale=-0.5).then_inc(rstd_done, 1)
                act.wait_ge(a_in, 16)
                act.activation(aneg[:], alog[:], ACT.Exp).then_inc(exp_done, 1)
                act.wait_ge(small_in, 48)
                act.activation(sil[:], cond[:], ACT.Silu).then_inc(sil_done, 1)
                act.wait_ge(split_v, 1)
                act.wait_ge(az_zero, 1)
                for b in range(PAIR):
                    act.copy(az[:, :, 0, b, b, :], aneg[:]).then_inc(split_a, 1)
                act.wait_ge(split_v, 2)
                for b in range(PAIR):
                    act.copy(az[:, :, 1, b, b, :], ares[:]).then_inc(split_a, 1)
                act.wait_ge(hid_mm, 1)
                for m in range(FC):
                    act.activation(hid[:, m, :], ps[:, 0, 64 + m * NB:64 + (m + 1) * NB], ACT.Gelu,
                                   bias=vec[:, VEC["l0b1"][0] + m:VEC["l0b1"][0] + m + 1]).then_inc(hid_done, 1)

            @block.vector
            def _(dve):
                dve.memset(ones[:], 1.0 / D).then_inc(ones_set, 1)
                dve.memset(keep["eps"][:], EPS).then_inc(eps_set, 1)
                dve.memset(az[:], 0.0).then_inc(az_zero, 1)
                dve.wait_ge(small_in, 48)
                dve.wait_ge(mean_mm, 1)
                dve.tensor_tensor(xc[:], cond[:], ps[:, 0, None, 0:NB].to_broadcast([P, FC, NB]),
                                  ALU.subtract).then_inc(xc_done, 1)
                dve.wait_ge(exp_done, 1)
                dve.tensor_scalar(aneg[:], aneg[:], -1.0, None, ALU.mult).then_inc(split_v, 1)
                dve.wait_ge(split_v, 1)
                dve.wait_ge(split_a, 2)
                dve.tensor_tensor(ares[:], aneg[:], az[:, :, 0, 0, 0, :], ALU.subtract).then_inc(split_v, 1)
                dve.wait_ge(split_v, 2)
                dve.wait_ge(split_a, 4)
                for b in range(PAIR):
                    dve.tensor_tensor(az[:, :, 2, b, b, :], ares[:], az[:, :, 1, 0, 0, :],
                                      ALU.subtract).then_inc(split_v, 1)
                dve.wait_ge(rstd_done, 1)
                dve.tensor_tensor(xn[:], xc[:], rstd[:, None, :].to_broadcast([P, FC, NB]),
                                  ALU.mult).then_inc(xn_done, 1)
                dve.wait_ge(xn_done, 1)
                g, b0 = VEC["ln_g"][0], VEC["ln_b"][0]
                for k in range(FC):
                    dve.tensor_scalar(hn[:, k, :], xn[:, k, :], vec[:, g + k:g + k + 1],
                                      vec[:, b0 + k:b0 + k + 1], ALU.mult, ALU.add).then_inc(hn_done, 1)
                dve.wait_ge(mod_mm, 1)
                mb = VEC["mod_b"][0]
                for lo, hi, bank in ((0, 12, 2), (12, NMOD, 3)):
                    dve.tensor_tensor(
                        mod[:, lo:hi, :], ps[:, bank, 0:(hi - lo) * NB].rearrange("p (m b) -> p m b", b=NB),
                        vec[:, mb + lo:mb + hi, None].to_broadcast([P, hi - lo, NB]), ALU.add).then_inc(mod_done, 1)
                dve.wait_ge(mod_done, 2)
                for name in ("m_sc", "p_sc", "a2_sc", "f2_sc", "a3_sc", "f3_sc"):
                    dve.tensor_scalar(mod[:, MOD[name]:MOD[name] + 2, :], mod[:, MOD[name]:MOD[name] + 2, :],
                                      1.0, None, ALU.add).then_inc(one_done, 1)
                dve.wait_ge(one_done, 6)
                k = 0
                for g, be, sc, sh in (("g1", "be1", "a3_sc", "a3_sh"), ("g2", "be2", "f3_sc", "f3_sh")):
                    for ch in range(FC):
                        dve.scalar_tensor_tensor(mod[:, MOD[sh] + ch, :], mod[:, MOD[sc] + ch, :],
                                                 vec[:, VEC[be][0] + ch:VEC[be][0] + ch + 1],
                                                 mod[:, MOD[sh] + ch, :], ALU.mult, ALU.add).then_inc(fold, 1)
                        dve.wait_ge(fold, k + 1)
                        dve.tensor_scalar(mod[:, MOD[sc] + ch, :], mod[:, MOD[sc] + ch, :],
                                          vec[:, VEC[g][0] + ch:VEC[g][0] + ch + 1], None, ALU.mult).then_inc(fold, 1)
                        k += 2
                dve.wait_ge(wa_mm, 1)
                ba = VEC["l0b2a"][0]
                dve.tensor_tensor(wa[:], pw[:, 0, :].rearrange("p (m b) -> p m b", b=NB),
                                  vec[:, ba:ba + 32, None].to_broadcast([P, 32, NB]), ALU.add)
                for m in range(8):
                    dve.wait_ge(bb_mm, m + 1)
                    dve.tensor_tensor(wbb[:, m * 512:(m + 1) * 512], pw[0:NB, 1 + m % 3, :],
                                      b2b[:, m * 512:(m + 1) * 512], ALU.add).then_inc(bb_done, 1)
    release(nc, sems)


def prepare(nc, ctx, io, keep, scratch):
    sems = []
    with ExitStack() as c:
        def sb(name, shape, dt=F32):
            return c.enter_context(nc.sbuf_tensor("p_" + name, shape, dt))

        def sem(name):
            sems.append(nc.alloc_semaphore(name="p_" + name))
            return sems[-1]

        vec, mod, wa = keep["vec"], keep["mod"], keep["wa"]
        ones = sb("ones", [P, P])
        ident = sb("ident", [P, P])
        in_w = [sb(f"in_w{r}", [P, FC, 2 * DI]) for r in range(2)]
        xp_w = [sb(f"xp_w{r}", [P, IC, DI + 2 * S]) for r in range(2)]
        cdup = [sb(f"cdup{r}", [P, IC, 2, S]) for r in range(2)]
        x = sb("x", [P, FC, N])
        bb = sb("bb", [RANK, 2, PAIR, D])
        low = sb("low", [RANK, 2, N])
        g = sb("g", [P, FC, N])
        x1 = sb("x1", [P, FC, N])
        xc = sb("xc", [P, FC, N])
        sq = sb("sq", [P, FC, N])
        rstd = sb("rstd", [P, N])
        h = [sb(f"h{r}", [P, FC, N]) for r in range(2)]
        xs = sb("xs", [P, IC, N])
        sz = sb("sz", [P, IC, N])
        skip = sb("skip", [P, IC, N])
        pre = sb("pre", [P, IC, N])
        sp_ = sb("soft", [P, IC, N])
        dt_ = sb("dt", [P, IC, N])
        u = sb("u", [P, IC, N])
        dp = sb("dp", [P, IC, PARTS, N], BF16)
        up = sb("up", [P, PARTS, 4, DI], BF16)
        bz = sb("bz", [P, PARTS, 4, PAIR, S], BF16)
        bres = sb("bres", [P, 4, S])
        cs = sb("cs", [P, T, PAIR])
        g0 = c.enter_context(nc.psum_tensor("p_g0", [P, 4, 512], F32))
        g1 = c.enter_context(nc.psum_tensor("p_g1", [P, 4, 512], F32))

        names = ("w_in x_in bb_in const z1 z2 low1_mm low1_done up1_mm gelu_done low2_mm low2_done up2_mm "
                 "x1_done x1_out mean_mm xc_done sq_done var_mm ln_done rstd_done xn_done h_done hr_done "
                 "xs_mm xs_done z_mm sz_done skip_done dt_mm pre_done abs_done soft_e soft_done dt_done u_done "
                 "vec_b dp0 dres dp1 dp2 ut_mm up0 ures up1 up2 bc_mm bz0 bres_done bz1 bz2 cs_done "
                 "sz_out skip_out dp_out up_out bz_out cs_out").split()
        s = {n: sem(n) for n in names}

        with nc.Block() as block:
            @block.sync
            def _(sp):
                for r in range(2):
                    sp.dma_start(in_w[r][:], io["in_w"][r].rearrange("(c p) m -> p c m", p=P)).then_inc(s["w_in"], 16)
                    sp.dma_start(xp_w[r][:], io["xproj_w"][r].rearrange("(c p) m -> p c m", p=P)).then_inc(s["w_in"], 16)
                    for e in range(2):
                        sp.dma_start(cdup[r][:, :, e, :],
                                     io["xproj_w"][r][:, DI + S:DI + 2 * S].rearrange("(c p) m -> p c m", p=P)
                                     ).then_inc(s["w_in"], 16)

                def unit(i):
                    wait(sp, s["x1_done"], i)
                    sp.dma_start(x[:], io["xT"][i]).then_inc(s["x_in"], 16)
                    wait(sp, s["up2_mm"], i)
                    sp.dma_start(bb[:], scratch["BB"].rearrange("q r (i b) d -> i r q (b d)", b=PAIR)[i]
                                 ).then_inc(s["bb_in"], 16)
                    wait(sp, s["x1_done"], i + 1)
                    sp.dma_start(scratch["X1"][i], x1[:]).then_inc(s["x1_out"], 16)
                    for r in range(2):
                        k = 2 * i + r
                        wait(sp, s["sz_done"], k + 1)
                        sp.dma_start(scratch["SZ"][r, i], sz[:]).then_inc(s["sz_out"], 16)
                        wait(sp, s["skip_done"], IC * k + IC)
                        sp.dma_start(scratch["SK"][r, i], skip[:]).then_inc(s["skip_out"], 16)
                        wait(sp, s["cs_done"], 2 * k + 2)
                        sp.dma_start(scratch["C2"][r, i], cs[:]).then_inc(s["cs_out"], 16)
                        wait(sp, s["bz2"], 2 * k + 2)
                        wait(sp, s["bz1"], 2 * k + 2)
                        for j in range(PARTS):
                            for m in range(PARTS):
                                sp.dma_start(scratch["B3"][r, i, m, j].rearrange("b c t f -> t (b c) f"),
                                             bz[:, m].rearrange("t k c s -> t k (c s)")).then_inc(s["bz_out"], 16)
                        wait(sp, s["dp2"], k + 1)
                        for m in range(IC):
                            sp.dma_start(scratch["D3"][r, m, i].rearrange("j b c d t -> d (j b c) t"),
                                         dp[:, m].rearrange("p j (k t) -> p (j k) t", t=TS)).then_inc(s["dp_out"], 16)
                        wait(sp, s["up2"], k + 1)
                        for m in range(IC):
                            sp.dma_start(scratch["U3"][r, m, i].rearrange("j b c t d -> t (j b c) d"),
                                         up[:, :, :, m * P:(m + 1) * P].rearrange("p j k d -> p (j k) d")
                                         ).then_inc(s["up_out"], 16)

                over_units(sp, unit)
                sp.wait_ge(s["x1_out"], 16 * UNITS)
                for n in ("sz_out", "skip_out", "cs_out"):
                    sp.wait_ge(s[n], 32 * UNITS)
                sp.wait_ge(s["bz_out"], 32 * PARTS * PARTS * UNITS)
                for n in ("dp_out", "up_out"):
                    sp.wait_ge(s[n], 32 * IC * UNITS)

            @block.gpsimd
            def _(pool):
                pool.memset(ident[:], 0.0).then_inc(s["z1"], 1)
                pool.wait_ge(s["z1"], 1)
                pool.affine_select(out=ident[:], in_=ident[:], compare_op=ALU.not_equal, fill=1.0, base=0,
                                   pattern=[[-1, P]], channel_multiplier=1).then_inc(s["const"], 1)

                def unit(i):
                    for r in range(2):
                        k = 2 * i + r
                        wait(pool, s["dt_done"], k + 1)
                        wait(pool, s["xs_done"], k + 1)
                        wait(pool, s["ut_mm"], k)
                        pool.tensor_tensor(u[:], dt_[:], xs[:], ALU.mult).then_inc(s["u_done"], 1)

                over_units(pool, unit)

            @block.tensor
            def _(pe):
                pe.wait_ge(s["w_in"], 16 * 8)
                pe.wait_ge(s["const"], 2)

                def unit(i):
                    pe.wait_ge(s["x_in"], 16 * i + 16)
                    wait(pe, s["vec_b"], 2 * i + 2)
                    wait(pe, s["up0"], 2 * i)
                    wait(pe, s["ures"], 2 * i)
                    for b in range(PAIR):
                        for k in range(FC):
                            mm = pe.matmul(g0[0:RANK, 0, b * T:(b + 1) * T], keep["wab"][:, b, 0, :, k],
                                           x[:, k, b * T:(b + 1) * T], start=(k == 0), stop=(k == FC - 1))
                    mm.then_inc(s["low1_mm"], 1)
                    pe.wait_ge(s["bb_in"], 16 * i + 16)
                    wait(pe, s["low1_done"], i + 1)
                    wait(pe, s["cs_done"], 4 * i)
                    wait(pe, s["bres_done"], 2 * i)
                    for m in range(FC):
                        for b in range(PAIR):
                            mm = pe.matmul(g1[:, m, b * T:(b + 1) * T], bb[:, 0, b, m * P:(m + 1) * P],
                                           low[:, 0, b * T:(b + 1) * T], start=True, stop=True)
                    mm.then_inc(s["up1_mm"], 1)
                    wait(pe, s["gelu_done"], i + 1)
                    for b in range(PAIR):
                        for k in range(FC):
                            mm = pe.matmul(g0[0:RANK, 1, b * T:(b + 1) * T], keep["wab"][:, b, 1, :, k],
                                           g[:, k, b * T:(b + 1) * T], start=(k == 0), stop=(k == FC - 1))
                    mm.then_inc(s["low2_mm"], 1)
                    wait(pe, s["low2_done"], i + 1)
                    for m in range(FC):
                        for b in range(PAIR):
                            mm = pe.matmul(g1[:, 2 + m, b * T:(b + 1) * T], bb[:, 1, b, m * P:(m + 1) * P],
                                           low[:, 1, b * T:(b + 1) * T], start=True, stop=True)
                    mm.then_inc(s["up2_mm"], 1)
                    wait(pe, s["x1_done"], i + 1)
                    for k in range(FC):
                        mm = pe.matmul(g0[:, 2, :], ones[:], x1[:, k, :], start=(k == 0), stop=(k == FC - 1))
                    mm.then_inc(s["mean_mm"], 1)
                    wait(pe, s["sq_done"], i + 1)
                    for k in range(FC):
                        mm = pe.matmul(g0[:, 3, :], ones[:], sq[:, k, :], start=(k == 0), stop=(k == FC - 1))
                    mm.then_inc(s["var_mm"], 1)
                    for r in range(2):
                        n = 2 * i + r
                        if r == 0:
                            wait(pe, s["h_done"], 4 * i + 4)
                        else:
                            wait(pe, s["hr_done"], i + 1)
                            wait(pe, s["up0"], n)
                            wait(pe, s["ures"], n)
                        for m in range(IC):
                            for k in range(FC):
                                mm = pe.matmul(g0[:, m, :], in_w[r][:, k, m * P:(m + 1) * P], h[r][:, k, :],
                                               start=(k == 0), stop=(k == FC - 1))
                        mm.then_inc(s["xs_mm"], 1)
                        if r == 1:
                            wait(pe, s["cs_done"], 2 * n)
                            wait(pe, s["bres_done"], n)
                        for m in range(IC):
                            for k in range(FC):
                                mm = pe.matmul(g1[:, m, :], in_w[r][:, k, DI + m * P:DI + (m + 1) * P],
                                               h[r][:, k, :], start=(k == 0), stop=(k == FC - 1))
                        mm.then_inc(s["z_mm"], 1)
                        wait(pe, s["xs_done"], n + 1)
                        for m in range(IC):
                            for k in range(IC):
                                mm = pe.matmul(g0[:, m, :], xp_w[r][:, k, m * P:(m + 1) * P], xs[:, k, :],
                                               start=(k == 0), stop=(k == IC - 1))
                        mm.then_inc(s["dt_mm"], 1)
                        wait(pe, s["sz_done"], n + 1)
                        for k in range(IC):
                            pe.matmul(g1[:, 0, :], cdup[r][:, k, :, :].rearrange("p e s -> p (e s)"), xs[:, k, :],
                                      start=(k == 0), stop=(k == IC - 1))
                        for q in range(4):
                            for k in range(IC):
                                mm = pe.matmul(g1[:, 1, q * S:(q + 1) * S], xs[:, k, q * P:(q + 1) * P],
                                               xp_w[r][:, k, DI:DI + S], start=(k == 0), stop=(k == IC - 1))
                        mm.then_inc(s["bc_mm"], 1)
                        wait(pe, s["pre_done"], IC * n + IC)
                        wait(pe, s["u_done"], n + 1)
                        for q in range(4):
                            for m in range(IC):
                                mm = pe.transpose(g0[:, q, m * P:(m + 1) * P], u[:, m, q * P:(q + 1) * P], ident[:])
                        mm.then_inc(s["ut_mm"], 1)

                over_units(pe, unit)

            @block.scalar
            def _(act):
                def unit(i):
                    wait(act, s["low1_mm"], i + 1)
                    act.copy(low[:, 0, :], g0[0:RANK, 0, :]).then_inc(s["low1_done"], 1)
                    wait(act, s["up1_mm"], i + 1)
                    act.activation(g[:], g1[:, 0:2, :], ACT.Gelu).then_inc(s["gelu_done"], 1)
                    wait(act, s["low2_mm"], i + 1)
                    act.copy(low[:, 1, :], g0[0:RANK, 1, :]).then_inc(s["low2_done"], 1)
                    wait(act, s["xc_done"], i + 1)
                    act.activation(sq[:], xc[:], ACT.Square).then_inc(s["sq_done"], 1)
                    wait(act, s["var_mm"], i + 1)
                    wait(act, s["xn_done"], i)
                    act.activation(rstd[:], g0[:, 3, :], ACT.Ln, bias=keep["eps"][:]).then_inc(s["ln_done"], 1)
                    wait(act, s["ln_done"], i + 1)
                    act.activation(rstd[:], rstd[:], ACT.Exp, scale=-0.5).then_inc(s["rstd_done"], 1)
                    for r in range(2):
                        n = 2 * i + r
                        wait(act, s["xs_mm"], n + 1)
                        wait(act, s["bc_mm"], n)
                        wait(act, s["u_done"], n)
                        wait(act, s["skip_done"], IC * n)
                        act.activation(xs[:], g0[:], ACT.Silu).then_inc(s["xs_done"], 1)
                        wait(act, s["z_mm"], n + 1)
                        wait(act, s["sz_out"], 16 * n)
                        act.activation(sz[:], g1[:], ACT.Silu).then_inc(s["sz_done"], 1)
                        wait(act, s["pre_done"], IC * n + IC)
                        wait(act, s["dt_done"], n)
                        wait(act, s["up2"], n)
                        act.activation(sp_[:], pre[:], ACT.Abs).then_inc(s["abs_done"], 1)
                        wait(act, s["abs_done"], n + 1)
                        act.activation(sp_[:], sp_[:], ACT.Exp, scale=-1.0).then_inc(s["soft_e"], 1)
                        wait(act, s["soft_e"], n + 1)
                        act.activation(sp_[:], sp_[:], ACT.Ln, bias=1.0).then_inc(s["soft_done"], 1)
                        wait(act, s["bc_mm"], n + 1)
                        wait(act, s["bz_out"], 16 * PARTS * PARTS * n)
                        if isinstance(i, int) and r == 0:
                            act.wait_ge(s["z2"], 2)
                        for b in range(PAIR):
                            act.copy(bz[:, 0, 2 * b:2 * b + 2, b, :],
                                     g1[:, 1, 2 * b * S:(2 * b + 2) * S].rearrange("p (k s) -> p k s", s=S)
                                     ).then_inc(s["bz0"], 1)
                        wait(act, s["bres_done"], n + 1)
                        for b in range(PAIR):
                            act.copy(bz[:, 1, 2 * b:2 * b + 2, b, :], bres[:, 2 * b:2 * b + 2, :]).then_inc(s["bz1"], 1)
                        wait(act, s["dt_done"], n + 1)
                        wait(act, s["dp_out"], 16 * IC * n)
                        act.copy(dp[:, :, 0, :], dt_[:]).then_inc(s["dp0"], 1)
                        wait(act, s["dres"], n + 1)
                        act.copy(dp[:, :, 1, :], pre[:]).then_inc(s["dp1"], 1)
                        wait(act, s["ut_mm"], n + 1)
                        wait(act, s["up_out"], 16 * IC * n)
                        act.copy(up[:, 0], g0[:]).then_inc(s["up0"], 1)
                        wait(act, s["ures"], n + 1)
                        act.copy(up[:, 1], sp_[:]).then_inc(s["up1"], 1)

                over_units(act, unit)

            @block.vector
            def _(dve):
                dve.memset(ones[:], 1.0 / D).then_inc(s["const"], 1)
                dve.memset(bz[:], 0.0).then_inc(s["z2"], 1)
                dve.memset(cs[:], 0.0).then_inc(s["z2"], 1)
                dve.wait_ge(s["z2"], 2)

                def unit(i):
                    wait(dve, s["low2_mm"], i)
                    wait(dve, s["h_done"], 4 * i)
                    dve.tensor_copy(keep["wab"][:].rearrange("p b q r k -> p b (q r k)"),
                                    wa[:, :, bass.ds(PAIR * i, PAIR)].rearrange("p m b -> p b m")).then_inc(s["vec_b"], 1)
                    dve.tensor_copy(keep["mb"][:], mod[:, :, bass.ds(PAIR * i, PAIR)].rearrange("p m b -> p b m")
                                    ).then_inc(s["vec_b"], 1)
                    wait(dve, s["up2_mm"], i + 1)
                    wait(dve, s["x1_out"], 16 * i)
                    dve.tensor_tensor(x1[:], x[:], g1[:, 2:4, :], ALU.add).then_inc(s["x1_done"], 1)
                    wait(dve, s["mean_mm"], i + 1)
                    wait(dve, s["x1_done"], i + 1)
                    dve.tensor_tensor(xc[:], x1[:], g0[:, 2, None, :].to_broadcast([P, FC, N]),
                                      ALU.subtract).then_inc(s["xc_done"], 1)
                    wait(dve, s["rstd_done"], i + 1)
                    dve.tensor_tensor(xc[:], xc[:], rstd[:, None, :].to_broadcast([P, FC, N]),
                                      ALU.mult).then_inc(s["xn_done"], 1)
                    wait(dve, s["xn_done"], i + 1)
                    wait(dve, s["z_mm"], 2 * i)
                    wait(dve, s["vec_b"], 2 * i + 2)
                    for k in range(FC):
                        for b in range(PAIR):
                            dve.tensor_scalar(h[0][:, k, b * T:(b + 1) * T], xc[:, k, b * T:(b + 1) * T],
                                              keep["mb"][:, b, MOD["m_sc"] + k:MOD["m_sc"] + k + 1],
                                              keep["mb"][:, b, MOD["m_sh"] + k:MOD["m_sh"] + k + 1],
                                              ALU.mult, ALU.add).then_inc(s["h_done"], 1)
                    wait(dve, s["h_done"], 4 * i + 4)
                    dve.tensor_copy(h[1][:].rearrange("p c (b t) -> p (c b) t", t=T)[:, :, ::-1],
                                    h[0][:].rearrange("p c (b t) -> p (c b) t", t=T)).then_inc(s["hr_done"], 1)
                    for r in range(2):
                        n = 2 * i + r
                        wait(dve, s["dt_mm"], n + 1)
                        wait(dve, s["dp1"], n)
                        wait(dve, s["dp2"], n)
                        db = VEC[f"dtb{r}"][0]
                        for m in range(IC):
                            dve.tensor_scalar(pre[:, m, :], g0[:, m, :], vec[:, db + m:db + m + 1], None,
                                              ALU.add).then_inc(s["pre_done"], 1)
                        wait(dve, s["sz_done"], n + 1)
                        wait(dve, s["skip_out"], 16 * n)
                        d0 = VEC[f"D{r}"][0]
                        for m in range(IC):
                            dve.scalar_tensor_tensor(skip[:, m, :], xs[:, m, :], vec[:, d0 + m:d0 + m + 1],
                                                     sz[:, m, :], ALU.mult, ALU.mult).then_inc(s["skip_done"], 1)
                        wait(dve, s["soft_done"], n + 1)
                        wait(dve, s["pre_done"], IC * n + IC)
                        wait(dve, s["u_done"], n)
                        wait(dve, s["dp0"], n)
                        dve.scalar_tensor_tensor(dt_[:], pre[:], 0.0, sp_[:], ALU.max, ALU.add).then_inc(s["dt_done"], 1)
                        wait(dve, s["bc_mm"], n + 1)
                        wait(dve, s["cs_out"], 16 * n)
                        for b in range(PAIR):
                            dve.tensor_copy(cs[b * S:(b + 1) * S, :, b],
                                            g1[b * S:(b + 1) * S, 0, b * T:(b + 1) * T]).then_inc(s["cs_done"], 1)
                        wait(dve, s["bz0"], 2 * n + 2)
                        wait(dve, s["bz1"], 2 * n)
                        wait(dve, s["bz2"], 2 * n)
                        for b in range(PAIR):
                            bres_op = dve.tensor_tensor(
                                bres[:, 2 * b:2 * b + 2, :],
                                g1[:, 1, 2 * b * S:(2 * b + 2) * S].rearrange("p (k s) -> p k s", s=S),
                                bz[:, 0, 2 * b:2 * b + 2, b, :], ALU.subtract)
                        bres_op.then_inc(s["bres_done"], 1)
                        wait(dve, s["bz1"], 2 * n + 2)
                        wait(dve, s["bres_done"], n + 1)
                        for b in range(PAIR):
                            dve.tensor_tensor(bz[:, 2, 2 * b:2 * b + 2, b, :], bres[:, 2 * b:2 * b + 2, :],
                                              bz[:, 1, 2 * b:2 * b + 2, b, :], ALU.subtract).then_inc(s["bz2"], 1)
                        wait(dve, s["dp0"], n + 1)
                        wait(dve, s["dt_done"], n + 1)
                        dve.tensor_tensor(pre[:], dt_[:], dp[:, :, 0, :], ALU.subtract).then_inc(s["dres"], 1)
                        wait(dve, s["dp1"], n + 1)
                        wait(dve, s["dres"], n + 1)
                        dve.tensor_tensor(dp[:, :, 2, :], pre[:], dp[:, :, 1, :], ALU.subtract).then_inc(s["dp2"], 1)
                        wait(dve, s["up0"], n + 1)
                        wait(dve, s["dt_done"], n + 1)
                        dve.tensor_tensor(sp_[:], g0[:], up[:, 0], ALU.subtract).then_inc(s["ures"], 1)
                        wait(dve, s["up1"], n + 1)
                        wait(dve, s["ures"], n + 1)
                        dve.tensor_tensor(up[:, 2], sp_[:], up[:, 1], ALU.subtract).then_inc(s["up2"], 1)

                over_units(dve, unit)
    release(nc, sems)


def scan(nc, ctx, io, keep, scratch):
    TB = TS
    NT = T // TB
    FG = 1024 // TB
    STEPS = P // FG
    HALVES = TB // 4
    TQ = TB // Q
    RING = 8
    SEQS = 2 * IC * UNITS
    W = TB + 1
    LAG = 3
    AHEAD = LAG - 1
    ROW = P + PAIR

    sems = []
    with ExitStack() as c:
        def sb(name, shape, dt=F32):
            return c.enter_context(nc.sbuf_tensor("s_" + name, shape, dt))

        def sem(name):
            sems.append(nc.alloc_semaphore(name="s_" + name))
            return sems[-1]

        hb = [sb(f"h{e}", [P, P, W]) for e in range(2)]
        decay = [sb(f"decay{e}", [P, FG, W]) for e in range(RING)]
        dl = [sb(f"dl{e}", [P, QR, TB], BF16) for e in range(2)]
        ul = [sb(f"ul{e}", [P, TQ, P], BF16) for e in range(2)]
        al = sb("al", [P, P, P], BF16)
        bl = sb("bl", [P, TB, P], BF16)
        cl = [sb(f"cl{e}", [P, TB, PAIR]) for e in range(2)]
        cz = sb("cz", [P, TB // 4 * ROW])
        ytok = sb("ytok", [P, P])
        ys = [sb(f"ys{e}", [P, PAIR, TB]) for e in range(2)]
        ident = sb("ident", [P, P])
        one = sb("one", [P, 1])
        zcol = sb("zcol", [P, P])
        pa = [c.enter_context(nc.psum_tensor(f"s_pa{e}", [P, FG, TB], F32)) for e in range(2)]
        pb = [c.enter_context(nc.psum_tensor(f"s_pb{e}", [P, 4, P], F32)) for e in range(2)]
        py = c.enter_context(nc.psum_tensor("s_py", [P, 512], F32))
        pt = c.enter_context(nc.psum_tensor("s_pt", [P, 512], F32))

        dt_in = [sem(f"dt_in{e}") for e in range(2)]
        u_in = [sem(f"u_in{e}") for e in range(2)]
        a_in = [sem(f"a_in{q}") for q in range(Q)]
        b_in = [sem(f"b_in{q}") for q in range(Q)]
        c_in = [sem(f"c_in{e}") for e in range(2)]
        y_out = [sem(f"y_out{e}") for e in range(2)]
        zeroed, adt_mm, exp_done, scanned, bu_mm, bu_done, carried, c_filled, y_mm, ytok_done, yt_mm, y_done, const = (
            sem(n) for n in ("zeroed", "adt_mm", "exp_done", "scanned", "bu_mm", "bu_done", "carried",
                             "c_filled", "y_mm", "ytok_done", "yt_mm", "y_done", "const"))
        ZEROED = 1 + RING + 6

        def sequences(eng, body):
            body(0, True, False)
            with eng.Fori(1, SEQS - 1) as n:
                body(n, False, False)
            body(SEQS - 1, False, True)

        def ahead(n, e, m):
            return n + (e + m) // NT, (e + m) % NT

        def before(n, e):
            return (n, e - 2) if e >= 2 else (n - 1, e + NT - 2)

        def uses(n, e):
            return NT // 2 * n + e // 2 + 1

        with nc.Block() as block:
            @block.sync
            def _(sp):
                def of_unit(n):
                    return (n // (IC * UNITS)) * UNITS + n % UNITS

                def rows(tile, q, lo, hi):
                    return tile[QR * q:QR * q + ROWS, lo:hi, :].rearrange("r a b -> r (a b)")

                def moving(source):
                    s = source.rearrange("j b a f -> (j b) (a f)")
                    return s[None].to_broadcast([PARTS, PARTS * PAIR, s.shape[1]])

                def load_dt(n, e):
                    for q in range(Q):
                        sp.dma_start(rows(dl[e % 2], q, 0, QR), moving(scratch["D3f"][n, :, :, e, QR * q:QR * q + QR, :])
                                     ).then_inc(dt_in[e % 2], 16)

                def load_u(n, e):
                    for q in range(Q):
                        t = e * TB % P + TQ * q
                        sp.dma_start(rows(ul[e % 2], q, 0, TQ),
                                     moving(scratch["U3f"][n, :, :, e * TB // P, t:t + TQ, :])
                                     ).then_inc(u_in[e % 2], 16)

                def load_b(n, e, q):
                    t = e * TB % P + TQ * q
                    sp.dma_start(rows(bl, q, TQ * q, TQ * q + TQ),
                                 scratch["B3f"][of_unit(n), :, :, :, e * TB // P, t:t + TQ, :].rearrange(
                                     "i j b t f -> (i j b) (t f)")).then_inc(b_in[q], 16)

                def load_a(n, q):
                    sp.dma_start(rows(al, q, QR * q, QR * q + QR),
                                 scratch["A3"][n // UNITS, :, :, :, QR * q:QR * q + QR, :].rearrange(
                                     "i j b d f -> (i j b) (d f)")).then_inc(a_in[q], 16)

                def load_c(n, e):
                    sp.dma_start(cl[e % 2][:], scratch["C2f"][of_unit(n), :, e * TB:(e + 1) * TB, :]
                                 ).then_inc(c_in[e % 2], 16)

                def store_y(n, e):
                    wait(sp, y_done, NT * n + e + 1)
                    sp.dma_start(scratch["Yf"][n, :, :, e * TB:(e + 1) * TB], ys[e % 2][:]).then_inc(y_out[e % 2], 16)

                sp.wait_ge(zeroed, ZEROED)
                for q in range(Q):
                    load_a(0, q)
                    load_b(0, 0, q)
                for e in range(2):
                    load_dt(0, e)
                    load_u(0, e)
                    load_c(0, e)
                for q in range(Q):
                    sp.wait_ge(bu_mm, 4 * q + 4)
                    load_b(0, 1, q)
                load_u(0, 2)

                def sequence(n, first, last):
                    for e in range(NT):
                        k = NT * n + e
                        if e == NT - 1 and not last:
                            for q in range(Q):
                                wait(sp, adt_mm, STEPS * k + 2 * q + 2)
                                load_a(n + 1, q)
                        if not (last and e + 2 >= NT):
                            for q in range(Q):
                                wait(sp, bu_mm, HALVES * (k + 1) + 4 * q + 4)
                                load_b(*ahead(n, e, 2), q)
                            if not (last and e + 3 >= NT):
                                load_u(*ahead(n, e, 3))
                            wait(sp, adt_mm, STEPS * k + STEPS)
                            load_dt(*ahead(n, e, 2))
                        if not (first and e < 2):
                            store_y(*before(n, e))
                        if last:
                            wait(sp, c_filled, 2 * k)
                        if not (first and e == 0) and not (last and e + 1 >= NT):
                            load_c(*ahead(n, e, 1))

                sequences(sp, sequence)
                for e in range(2):
                    store_y(SEQS - 1, NT - 2 + e)
                for e in range(2):
                    sp.wait_ge(y_out[e], 16 * SEQS * NT // 2)

            @block.tensor
            def _(pe):
                def adt(n, e, j):
                    if j == 0:
                        wait(pe, dt_in[e % 2], 64 * uses(n, e))
                    if j % 2 == 0:
                        wait(pe, a_in[j // 2], 16 * (n + 1))
                    wait(pe, exp_done, STEPS * (NT * n + e) + j - 1)
                    for m in range(FG):
                        d = FG * j + m
                        mm = pe.matmul(pa[j % 2][:, m, :], al[:, d, :], dl[e % 2][:, d % QR, :], start=True, stop=True)
                    mm.then_inc(adt_mm, 1)

                def bu(n, e, h):
                    k = NT * n + e
                    if h == 0:
                        wait(pe, u_in[e % 2], 64 * uses(n, e))
                    if h % 4 == 0:
                        wait(pe, b_in[h // 4], 16 * (k + 1))
                    wait(pe, bu_done, HALVES * k + h - 1)
                    for m in range(4):
                        t = 4 * h + m
                        mm = pe.matmul(pb[h % 2][:, m, :], bl[:, t, :], ul[e % 2][:, t % TQ, :], start=True, stop=True)
                    mm.then_inc(bu_mm, 1)

                def ch(k, e, j):
                    if j == 0:
                        wait(pe, scanned, STEPS * (k + 1))
                        wait(pe, ytok_done, k)
                    if j % 4 == 0:
                        wait(pe, c_filled, 2 * k + j // 4 + 1)
                    for m in range(8):
                        t = 8 * j + m
                        row, q = t // 4, t % 4
                        mm = pe.matmul(py[QR * q:QR * q + QR, 0:P], cz[:, row * P + QR * q:row * P + QR * q + QR],
                                       hb[e % 2][:, :, 1 + t], start=(row == 0), stop=(row == TB // 4 - 1))
                    mm.then_inc(y_mm, 1)

                def turn_y(k):
                    wait(pe, ytok_done, k + 1)
                    wait(pe, y_done, k)
                    pe.transpose(pt[:, 0:P], ytok[:], ident[:]).then_inc(yt_mm, 1)

                pe.wait_ge(const, 3)
                pe.wait_ge(zeroed, ZEROED)
                adt(0, 0, 0)
                adt(0, 0, 1)
                for h in range(HALVES):
                    bu(0, 0, h)

                def sequence(n, first, last):
                    for e in range(NT):
                        k = NT * n + e
                        more = not (last and e == NT - 1)
                        for j in range(STEPS):
                            if j + 2 < STEPS:
                                adt(n, e, j + 2)
                            elif more:
                                adt(*ahead(n, e, 1), j + 2 - STEPS)
                            if j == LAG + 1 and not (first and e < 2):
                                turn_y(k - 2)
                            m = j - AHEAD
                            if m < 0:
                                if not (first and e < 2):
                                    ch(k - 2, e, m + STEPS)
                                if not (first and e == 0):
                                    bu(n, e, 2 * (m + STEPS))
                                    bu(n, e, 2 * (m + STEPS) + 1)
                            else:
                                if not (first and e == 0):
                                    ch(k - 1, e + 1, m)
                                if more:
                                    bu(*ahead(n, e, 1), 2 * m)
                                    bu(*ahead(n, e, 1), 2 * m + 1)

                sequences(pe, sequence)
                final = NT * SEQS - 1
                for j in range(STEPS - AHEAD, STEPS):
                    ch(final - 1, 0, j)
                turn_y(final - 1)
                for j in range(STEPS):
                    ch(final, 1, j)
                turn_y(final)

            @block.scalar
            def _(act):
                def take_bu(n, e, h):
                    k = NT * n + e
                    wait(act, bu_mm, HALVES * k + h + 1)
                    wait(act, y_mm, STEPS * (k - 2) + h // 2 + 1)
                    act.copy(hb[e % 2][:, :, 1 + 4 * h:5 + 4 * h], pb[h % 2][:].rearrange("p t d -> p d t")
                             ).then_inc(bu_done, 1)

                def take_y(k):
                    wait(act, y_mm, STEPS * (k + 1))
                    wait(act, yt_mm, k)
                    act.copy(ytok[:], py[:, 0:P]).then_inc(ytok_done, 1)

                act.wait_ge(zeroed, ZEROED)
                for h in range(HALVES):
                    take_bu(0, 0, h)

                def sequence(n, first, last):
                    for e in range(NT):
                        k = NT * n + e
                        for j in range(STEPS):
                            if j == LAG - 1 and not (first and e < 2):
                                take_y(k - 2)
                            wait(act, adt_mm, STEPS * k + j + 1)
                            wait(act, scanned, STEPS * k + j + 1 - RING)
                            act.activation(decay[j % RING][:, :, 1:W], pa[j % 2][:], ACT.Exp).then_inc(exp_done, 1)
                            m = j - LAG
                            if m < 0:
                                if not (first and e == 0):
                                    take_bu(n, e, 2 * (m + STEPS))
                                    take_bu(n, e, 2 * (m + STEPS) + 1)
                            elif not (last and e == NT - 1):
                                take_bu(*ahead(n, e, 1), 2 * m)
                                take_bu(*ahead(n, e, 1), 2 * m + 1)

                sequences(act, sequence)
                for e in range(2):
                    take_y(NT * SEQS - 2 + e)

            @block.gpsimd
            def _(pool):
                pool.memset(cz[:], 0.0).then_inc(const, 1)
                pool.memset(one[:], 1.0).then_inc(const, 1)
                pool.memset(ident[:], 0.0).then_inc(zeroed, 1)
                pool.wait_ge(zeroed, ZEROED)
                pool.affine_select(out=ident[:], in_=ident[:], compare_op=ALU.not_equal, fill=1.0, base=0,
                                   pattern=[[-1, P]], channel_multiplier=1).then_inc(const, 1)
                pool.wait_ge(const, 3)

                def fill(n, e):
                    k = NT * n + e
                    wait(pool, c_in[e % 2], 16 * uses(n, e))
                    for g in range(2):
                        wait(pool, y_mm, STEPS * (k - 1) + 4 * g + 4)
                        out = cz[:].rearrange("p (l m) -> p l m", m=ROW)[:, 8 * g:8 * g + 8, 0:P].rearrange(
                            "p l (q m) -> p l q m", m=QR)[:, :, :, 0:PAIR]
                        pool.tensor_tensor(out, cl[e % 2][:, 32 * g:32 * g + 32, :].rearrange("p (l q) b -> p l q b", q=4),
                                           one[:, None, None, 0:1].to_broadcast([P, 8, 4, PAIR]), ALU.mult
                                           ).then_inc(c_filled, 1)

                def sequence(n, first, last):
                    for e in range(NT):
                        fill(n, e)

                sequences(pool, sequence)

            @block.vector
            def _(dve):
                for e in range(RING):
                    dve.memset(decay[e][:, :, 0], 0.0).then_inc(zeroed, 1)
                dve.memset(zcol[:], 0.0).then_inc(zeroed, 1)
                dve.memset(al[:], 0.0)
                dve.memset(bl[:], 0.0).then_inc(zeroed, 1)
                for e in range(2):
                    dve.memset(dl[e][:], 0.0).then_inc(zeroed, 1)
                    dve.memset(ul[e][:], 0.0).then_inc(zeroed, 1)
                dve.wait_ge(zeroed, ZEROED)

                def turned_y(k, n, e):
                    wait(dve, yt_mm, k + 1)
                    wait(dve, y_out[e % 2], 16 * (uses(n, e) - 1))
                    dve.tensor_copy(ys[e % 2][:].rearrange("p b (l q) -> p b l q", q=4),
                                    pt[:, 0:P].rearrange("p (q l b) -> p b l q", q=4, b=PAIR)).then_inc(y_done, 1)

                def sequence(n, first, last):
                    for e in range(NT):
                        k = NT * n + e
                        wait(dve, bu_done, HALVES * (k + 1))
                        wait(dve, scanned, STEPS * k)
                        start = hb[(e + 1) % 2][:, :, TB] if e else zcol[:]
                        dve.tensor_copy(hb[e % 2][:, :, 0], start).then_inc(carried, 1)
                        wait(dve, carried, k + 1)
                        for j in range(STEPS):
                            wait(dve, exp_done, STEPS * k + j + 1)
                            seg = hb[e % 2][:, FG * j:FG * j + FG, :].rearrange("p d w -> p (d w)")
                            dve.tensor_tensor_scan(seg, decay[j % RING][:].rearrange("p d w -> p (d w)"), seg,
                                                   0.0, ALU.mult, ALU.add).then_inc(scanned, 1)
                            if j == LAG + 1 and not (first and e < 2):
                                turned_y(k - 2, *before(n, e))

                sequences(dve, sequence)
                for e in range(2):
                    turned_y(NT * SEQS - 2 + e, SEQS - 1, NT - 2 + e)

    release(nc, sems)


class Jobs:

    def __init__(self, jobs, ring, base=0):
        self.names = [n for n, _, _ in jobs]
        self.reader = [e for _, e, _ in jobs]
        self.ring, self.base, self.count = ring, base, len(jobs)
        assert self.count % ring == 0
        self.per = {e: sum(n for _, r, n in jobs if r == e) for e in "va"}
        self.upto = [sum(n for _, r, n in jobs[:k + 1] if r == e) for k, (_, e, _) in enumerate(jobs)]

    def bank(self, name):
        return self.base + self.names.index(name) % self.ring

    def made(self, i, name):
        return i * self.count + self.names.index(name) + 1

    def taken(self, i, name):
        k = self.names.index(name)
        return i * self.per[self.reader[k]] + self.upto[k]

    def before(self, i, name):
        k = self.names.index(name) - self.ring
        at = i if k >= 0 else i - 1
        return self.reader[k], at * self.per[self.reader[k]] + self.upto[k]


def finish_scan(nc, ctx, io, keep, scratch):
    sems = []
    with ExitStack() as c:
        def sb(name, shape, dt=F32):
            return c.enter_context(nc.sbuf_tensor("f_" + name, shape, dt))

        def sem(name):
            sems.append(nc.alloc_semaphore(name="f_" + name))
            return sems[-1]

        mod, mb = keep["mod"], keep["mb"]
        HC = 2 * D // P
        ow = sb("ow", [P, 2, IC, D])
        w1, w2 = sb("w1", [P, FC, 2 * D]), sb("w2", [P, FC, 2 * D])
        w3 = sb("w3", [P, HC, D])
        ones = sb("ones", [P, P])
        x = sb("x", [P, FC, N])
        y = [sb(f"y{r}", [P, IC, N]) for r in range(2)]
        sz = [sb(f"sz{r}", [P, IC, N]) for r in range(2)]
        skip = [sb(f"skip{r}", [P, IC, N]) for r in range(2)]
        yg = [sb(f"yg{r}", [P, IC, N]) for r in range(2)]
        x2, xc, sq, h, xo = (sb(n, [P, FC, N]) for n in ("x2", "xc", "sq", "h", "xo"))
        rstd = sb("rstd", [P, N])
        gate, prod = sb("gate", [P, HC, N]), sb("prod", [P, HC, N])
        ps = c.enter_context(nc.psum_tensor("f_ps", [P, 8, 512], F32))
        jobs = Jobs([("po0", "v", 2), ("po1", "v", 2), ("mean", "v", 1), ("var", "a", 1)]
                    + [(f"{w}{m}", e, 1) for m in range(HC) for w, e in (("g", "a"), ("l", "v"))]
                    + [("out0", "v", 2), ("out1", "v", 2)], 7)
        s = {n: sem(n) for n in ("w_in ones x_in y_in0 y_in1 vec_b mul0 mul1 yg0 yg1 mm taken_v taken_a "
                                 "sq_done ln_done rstd_done xn_done h_done x_out").split()}

        def bank_free(pe, i, name):
            e, value = jobs.before(i, name)
            wait(pe, s["taken_" + e], value)

        with nc.Block() as block:
            @block.sync
            def _(sp):
                for r in range(2):
                    sp.dma_start(ow[:, r], io["out_w"][r].rearrange("(c p) m -> p c m", p=P)).then_inc(s["w_in"], 16)
                for dst, name in ((w1, "mlp_w1"), (w2, "mlp_w2"), (w3, "mlp_w3")):
                    sp.dma_start(dst[:], io[name].rearrange("(c p) m -> p c m", p=P)).then_inc(s["w_in"], 16)

                def unit(i):
                    for r in range(2):
                        wait(sp, s[f"yg{r}"], i)
                        for m in range(IC):
                            sp.dma_start(y[r][:, m, :].rearrange("p (b t) -> p b t", b=PAIR), scratch["Y"][r, m, i]
                                         ).then_inc(s[f"y_in{r}"], 16)
                        sp.dma_start(sz[r][:], scratch["SZ"][r, i]).then_inc(s[f"y_in{r}"], 16)
                        sp.dma_start(skip[r][:], scratch["SK"][r, i]).then_inc(s[f"y_in{r}"], 16)
                    wait(sp, s["taken_v"], jobs.taken(i - 1, "po1"))
                    sp.dma_start(x[:], scratch["X1"][i]).then_inc(s["x_in"], 16)
                    if isinstance(i, int):
                        return
                    wait(sp, s["taken_v"], jobs.taken(i - 1, "out1"))
                    sp.dma_start(scratch["X2"][bass.ds(i - 1, 1)].rearrange("o p c n -> (o p) c n"), xo[:]
                                 ).then_inc(s["x_out"], 16)

                over_units(sp, unit)
                sp.wait_ge(s["taken_v"], jobs.taken(UNITS - 1, "out1"))
                sp.dma_start(scratch["X2"][UNITS - 1], xo[:]).then_inc(s["x_out"], 16)
                sp.wait_ge(s["x_out"], 16 * UNITS)

            @block.tensor
            def _(pe):
                pe.wait_ge(s["w_in"], 80)
                pe.wait_ge(s["ones"], 1)

                def unit(i):
                    for m in range(FC):
                        bank_free(pe, i, f"po{m}")
                        for r in range(2):
                            wait(pe, s[f"yg{r}"], i + 1)
                            for k in range(IC):
                                mm = pe.matmul(ps[:, jobs.bank(f"po{m}"), :], ow[:, r, k, m * P:(m + 1) * P],
                                               yg[r][:, k, :], start=(r == 0 and k == 0), stop=(r == 1 and k == IC - 1))
                        mm.then_inc(s["mm"], 1)
                    bank_free(pe, i, "mean")
                    wait(pe, s["taken_v"], jobs.taken(i, "po1"))
                    for k in range(FC):
                        mm = pe.matmul(ps[:, jobs.bank("mean"), :], ones[:], x2[:, k, :], start=(k == 0), stop=(k == FC - 1))
                    mm.then_inc(s["mm"], 1)
                    bank_free(pe, i, "var")
                    wait(pe, s["sq_done"], i + 1)
                    for k in range(FC):
                        mm = pe.matmul(ps[:, jobs.bank("var"), :], ones[:], sq[:, k, :], start=(k == 0), stop=(k == FC - 1))
                    mm.then_inc(s["mm"], 1)
                    wait(pe, s["h_done"], 4 * i + 4)
                    for m in range(HC):
                        for name, w in ((f"g{m}", w1), (f"l{m}", w2)):
                            bank_free(pe, i, name)
                            for k in range(FC):
                                mm = pe.matmul(ps[:, jobs.bank(name), :], w[:, k, m * P:(m + 1) * P], h[:, k, :],
                                               start=(k == 0), stop=(k == FC - 1))
                            mm.then_inc(s["mm"], 1)
                    wait(pe, s["taken_v"], jobs.taken(i, f"l{HC - 1}"))
                    for m in range(FC):
                        bank_free(pe, i, f"out{m}")
                        for k in range(HC):
                            mm = pe.matmul(ps[:, jobs.bank(f"out{m}"), :], w3[:, k, m * P:(m + 1) * P], prod[:, k, :],
                                           start=(k == 0), stop=(k == HC - 1))
                        mm.then_inc(s["mm"], 1)

                over_units(pe, unit)

            @block.scalar
            def _(act):
                def unit(i):
                    wait(act, s["xn_done"], i)
                    wait(act, s["taken_v"], jobs.taken(i, "mean"))
                    act.activation(sq[:], xc[:], ACT.Square).then_inc(s["sq_done"], 1)
                    wait(act, s["mm"], jobs.made(i, "var"))
                    act.activation(rstd[:], ps[:, jobs.bank("var"), :], ACT.Ln, bias=keep["eps"][:]
                                   ).then_inc(s["taken_a"], 1)
                    wait(act, s["taken_a"], jobs.taken(i, "var"))
                    act.activation(rstd[:], rstd[:], ACT.Exp, scale=-0.5).then_inc(s["rstd_done"], 1)
                    for m in range(HC):
                        wait(act, s["mm"], jobs.made(i, f"g{m}"))
                        act.activation(gate[:, m, :], ps[:, jobs.bank(f"g{m}"), :], ACT.Silu).then_inc(s["taken_a"], 1)

                over_units(act, unit)

            @block.vector
            def _(dve):
                dve.memset(ones[:], 1.0 / D).then_inc(s["ones"], 1)

                def unit(i):
                    wait(dve, s["taken_v"], jobs.taken(i - 1, "out1"))
                    dve.tensor_copy(mb[:], mod[:, :, bass.ds(PAIR * i, PAIR)].rearrange("p m b -> p b m")
                                    ).then_inc(s["vec_b"], 1)
                    for r in range(2):
                        wait(dve, s[f"y_in{r}"], 16 * (IC + 2) * (i + 1))
                        dve.tensor_tensor(y[r][:], y[r][:], sz[r][:], ALU.mult).then_inc(s[f"mul{r}"], 1)
                        wait(dve, s[f"mul{r}"], i + 1)
                        wait(dve, s["mm"], jobs.made(i, "po1") - jobs.count)
                        out = yg[r][:].rearrange("p c (b t) -> p (c b) t", t=T)
                        dve.tensor_tensor(out[:, :, ::-1] if r else out, y[r][:].rearrange("p c (b t) -> p (c b) t", t=T),
                                          skip[r][:].rearrange("p c (b t) -> p (c b) t", t=T), ALU.add
                                          ).then_inc(s[f"yg{r}"], 1)
                    wait(dve, s["x_in"], 16 * (i + 1))
                    wait(dve, s["vec_b"], i + 1)
                    for m in range(FC):
                        wait(dve, s["mm"], jobs.made(i, f"po{m}"))
                        for b in range(PAIR):
                            cols = slice(b * T, (b + 1) * T)
                            ch = MOD["m_g"] + m
                            dve.scalar_tensor_tensor(x2[:, m, cols], ps[:, jobs.bank(f"po{m}"), cols],
                                                     mb[:, b, ch:ch + 1], x[:, m, cols], ALU.mult, ALU.add
                                                     ).then_inc(s["taken_v"], 1)
                    wait(dve, s["mm"], jobs.made(i, "mean"))
                    wait(dve, s["taken_v"], jobs.taken(i, "po1"))
                    dve.tensor_tensor(xc[:], x2[:], ps[:, jobs.bank("mean"), None, :].to_broadcast([P, FC, N]),
                                      ALU.subtract).then_inc(s["taken_v"], 1)
                    wait(dve, s["rstd_done"], i + 1)
                    dve.tensor_tensor(xc[:], xc[:], rstd[:, None, :].to_broadcast([P, FC, N]), ALU.mult
                                      ).then_inc(s["xn_done"], 1)
                    wait(dve, s["xn_done"], i + 1)
                    for m in range(FC):
                        for b in range(PAIR):
                            cols = slice(b * T, (b + 1) * T)
                            sc, sh = MOD["p_sc"] + m, MOD["p_sh"] + m
                            dve.tensor_scalar(h[:, m, cols], xc[:, m, cols], mb[:, b, sc:sc + 1], mb[:, b, sh:sh + 1],
                                              ALU.mult, ALU.add).then_inc(s["h_done"], 1)
                    for m in range(HC):
                        wait(dve, s["mm"], jobs.made(i, f"l{m}"))
                        wait(dve, s["taken_a"], jobs.taken(i, f"g{m}"))
                        dve.tensor_tensor(prod[:, m, :], ps[:, jobs.bank(f"l{m}"), :], gate[:, m, :], ALU.mult
                                          ).then_inc(s["taken_v"], 1)
                    wait(dve, s["x_out"], 16 * i)
                    for m in range(FC):
                        wait(dve, s["mm"], jobs.made(i, f"out{m}"))
                        for b in range(PAIR):
                            cols = slice(b * T, (b + 1) * T)
                            ch = MOD["p_g"] + m
                            dve.scalar_tensor_tensor(xo[:, m, cols], ps[:, jobs.bank(f"out{m}"), cols],
                                                     mb[:, b, ch:ch + 1], x2[:, m, cols], ALU.mult, ALU.add
                                                     ).then_inc(s["taken_v"], 1)

                over_units(dve, unit)
    release(nc, sems)


def transformer(nc, ctx, io, keep, scratch, layer, x_from, x_to):
    HR, dh = (DH2, DH2) if layer == 2 else (PADH, DH3)
    HT = P // HR
    MT = H // HT
    VW = H * HR
    VB = VW // 512
    HEADS = PAIR * H
    TILES = PAIR * MT
    MC = MLP // P
    SCALE = dh ** -0.5

    sems = []
    with ExitStack() as c:
        def sb(name, shape, dt=F32):
            return c.enter_context(nc.sbuf_tensor(f"t{layer}_" + name, shape, dt))

        def sem(name):
            sems.append(nc.alloc_semaphore(name=f"t{layer}_" + name))
            return sems[-1]

        vec, mod, mb = keep["vec"], keep["mod"], keep["mb"]
        wqkv = sb("wqkv", [P, FC, 3 * VW])
        wo = sb("wo", [P, MT, D])
        w1 = sb("w1", [P, FC, MLP])
        w2 = sb("w2", [P, MC, D])
        ones, ident = sb("ones", [P, P]), sb("ident", [P, P])
        x, x2, xc, h, xo = (sb(n, [P, FC, N]) for n in ("x", "x2", "xc", "h", "xo"))
        sq = h
        tmp = sb("tmp", [P, N])
        rstd = sb("rstd", [P, N])
        kf = sb("k", [P, MT, N])
        qf = sb("q", [P, MT, N]) if layer == 2 else sb("q", [P, MT, HT, N])
        vt = sb("v", [P, N // P, VW])
        o = sb("o", [P, MT, N])
        hid = qf if MT == MC else sb("hid", [P, MC, N])
        prob = [sb(f"prob{e}", [P, 2, T]) for e in range(2)]
        probt = [sb(f"probt{e}", [P, 2, T]) for e in range(2)]
        nmax = [sb(f"nmax{e}", [P, 2]) for e in range(2)]
        rsum = [sb(f"rsum{e}", [P, 2]) for e in range(2)]
        rinv = [sb(f"rinv{e}", [P, 2]) for e in range(2)]
        ps = c.enter_context(nc.psum_tensor(f"t{layer}_ps", [P, 8, 512], F32))

        jobs = Jobs([("mean1", "v", 1), ("var1", "a", 1)]
                    + [(f"{w}{m}", "v", 1) for w in "qk" for m in range(MT)]
                    + [(f"v{t}_{m}", "a", 1) for t in range(N // P) for m in range(VB)]
                    + [("proj0", "v", 2), ("proj1", "v", 2), ("mean2", "v", 1), ("var2", "a", 1)]
                    + [(f"f{m}", "a", 1) for m in range(MC)]
                    + [("out0", "v", 2), ("out1", "v", 2)], 2, base=6)
        s = {n: sem(n) for n in ("w_in ones ident zero x_in vec_b mm taken_v taken_a sq ln rstd xn h s_mm max exp recip "
                                 "norm t_mm pt pv o_done x2_done xo_done x_out").split()}
        steps = {1: ("mean1", "var1", f"a{layer}"), 2: ("mean2", "var2", f"f{layer}")}
        bo, b1, b2 = (VEC[f"{n}{layer}"][0] for n in ("bo", "b1", "b2"))

        def bank(name):
            return ps[:, jobs.bank(name), :]

        with nc.Block() as block:
            @block.sync
            def _(sp):
                for dst, name in ((wqkv, f"Wqkv{layer}"), (wo, f"Wo{layer}"), (w1, f"W1{layer}"), (w2, f"W2{layer}")):
                    sp.dma_start(dst[:], io[name].rearrange("(c p) m -> p c m", p=P)).then_inc(s["w_in"], 16)

                def unit(i):
                    wait(sp, s["x2_done"], 2 * i)
                    sp.dma_start(x[:], x_from[i]).then_inc(s["x_in"], 16)
                    if isinstance(i, int):
                        return
                    wait(sp, s["xo_done"], 2 * i)
                    sp.dma_start(x_to[bass.ds(i - 1, 1)].rearrange("o p c n -> (o p) c n"), xo[:]
                                 ).then_inc(s["x_out"], 16)

                over_units(sp, unit)
                sp.wait_ge(s["xo_done"], 2 * UNITS)
                sp.dma_start(x_to[UNITS - 1], xo[:]).then_inc(s["x_out"], 16)
                sp.wait_ge(s["x_out"], 16 * UNITS)

            @block.gpsimd
            def _(pool):
                pool.memset(ident[:], 0.0).then_inc(s["ident"], 1)
                pool.wait_ge(s["ident"], 1)
                pool.affine_select(out=ident[:], in_=ident[:], compare_op=ALU.not_equal, fill=1.0, base=0,
                                   pattern=[[-1, P]], channel_multiplier=1).then_inc(s["ident"], 1)

            @block.tensor
            def _(pe):
                def linear(i, name, pairs):
                    e, value = jobs.before(i, name)
                    wait(pe, s["taken_" + e], value)
                    for k, (w, v) in enumerate(pairs):
                        mm = pe.matmul(bank(name), w, v, start=(k == 0), stop=(k == len(pairs) - 1))
                    mm.then_inc(s["mm"], 1)

                def scores(i, n):
                    wait(pe, s["exp"], i * HEADS + n - 1)
                    b, tile, lo = n // H, (n % H) // HT, HR * (n % HT)
                    for e in range(2):
                        cols = slice(b * T + e * P, b * T + (e + 1) * P)
                        if layer == 2:
                            q, k = qf[lo:lo + HR, tile, cols], kf[lo:lo + HR, tile, b * T:(b + 1) * T]
                        else:
                            q, k = qf[:, tile, n % HT, cols], kf[:, tile, b * T:(b + 1) * T]
                        mm = pe.matmul(ps[:, n % 2, e * T:(e + 1) * T], q, k, start=True, stop=True)
                    mm.then_inc(s["s_mm"], 1)

                def turn(i, n):
                    wait(pe, s["norm"], i * HEADS + n + 1)
                    wait(pe, s["pt"], i * HEADS + n - 1)
                    for e in range(2):
                        for kb in range(2):
                            mm = pe.transpose(ps[:, 2 + n % 2, kb * T + e * P:kb * T + (e + 1) * P],
                                              prob[n % 2][:, e, kb * P:(kb + 1) * P], ident[:])
                    mm.then_inc(s["t_mm"], 1)

                def values(i, n):
                    wait(pe, s["pt"], i * HEADS + n + 1)
                    b, tile, lo = n // H, n // HT, HR * (n % HT)
                    if n % HT == 0:
                        wait(pe, s["o_done"], i * TILES + tile - 1)
                    for kb in range(2):
                        mm = pe.matmul(ps[lo:lo + HR, 4 + tile % 2, 0:T],
                                       vt[:, 2 * b + kb, (n % H) * HR:(n % H + 1) * HR],
                                       probt[n % 2][:, kb, :], start=(kb == 0), stop=(kb == 1))
                    mm.then_inc(s["pv"], 1)

                pe.wait_ge(s["w_in"], 64)
                pe.wait_ge(s["ones"], 1)
                pe.wait_ge(s["ident"], 2)

                def unit(i):
                    wait(pe, s["x_in"], 16 * (i + 1))
                    linear(i, "mean1", [(ones[:], x[:, k, :]) for k in range(FC)])
                    wait(pe, s["sq"], 2 * i + 1)
                    linear(i, "var1", [(ones[:], sq[:, k, :]) for k in range(FC)])
                    wait(pe, s["h"], 8 * i + 4)
                    for w in range(2):
                        for m in range(MT):
                            linear(i, f"{'qk'[w]}{m}", [(wqkv[:, k, w * VW + m * P:w * VW + (m + 1) * P], h[:, k, :])
                                                        for k in range(FC)])
                    for t in range(N // P):
                        for m in range(VB):
                            linear(i, f"v{t}_{m}", [(h[:, k, t * P:(t + 1) * P],
                                                     wqkv[:, k, 2 * VW + m * 512:2 * VW + (m + 1) * 512])
                                                    for k in range(FC)])
                    wait(pe, s["taken_v"], jobs.taken(i, f"k{MT - 1}"))
                    wait(pe, s["taken_a"], jobs.taken(i, f"v{N // P - 1}_{VB - 1}"))
                    for n in range(HEADS + 2):
                        if n < HEADS:
                            scores(i, n)
                        if 1 <= n <= HEADS:
                            turn(i, n - 1)
                        if n >= 2:
                            values(i, n - 2)
                    wait(pe, s["o_done"], TILES * (i + 1))
                    for m in range(FC):
                        linear(i, f"proj{m}", [(wo[:, k, m * P:(m + 1) * P], o[:, k, :]) for k in range(MT)])
                    wait(pe, s["x2_done"], 2 * i + 2)
                    linear(i, "mean2", [(ones[:], x2[:, k, :]) for k in range(FC)])
                    wait(pe, s["sq"], 2 * i + 2)
                    linear(i, "var2", [(ones[:], sq[:, k, :]) for k in range(FC)])
                    wait(pe, s["h"], 8 * i + 8)
                    for m in range(MC):
                        linear(i, f"f{m}", [(w1[:, k, m * P:(m + 1) * P], h[:, k, :]) for k in range(FC)])
                    wait(pe, s["taken_a"], jobs.taken(i, f"f{MC - 1}"))
                    for m in range(FC):
                        linear(i, f"out{m}", [(w2[:, k, m * P:(m + 1) * P], hid[:, k, :]) for k in range(MC)])

                over_units(pe, unit)

            @block.scalar
            def _(act):
                def norm(i, g):
                    mean, var, _ = steps[g]
                    wait(act, s["taken_v"], jobs.taken(i, mean))
                    wait(act, s["mm"], jobs.made(i, mean))
                    act.activation(sq[:], xc[:], ACT.Square).then_inc(s["sq"], 1)
                    wait(act, s["mm"], jobs.made(i, var))
                    act.activation(rstd[:], bank(var), ACT.Ln, bias=keep["eps"][:]).then_inc(s["taken_a"], 1)
                    wait(act, s["taken_a"], jobs.taken(i, var))
                    act.activation(rstd[:], rstd[:], ACT.Exp, scale=-0.5).then_inc(s["rstd"], 1)

                def unit(i):
                    norm(i, 1)
                    for t in range(N // P):
                        for m in range(VB):
                            wait(act, s["mm"], jobs.made(i, f"v{t}_{m}"))
                            act.copy(vt[:, t, m * 512:(m + 1) * 512], bank(f"v{t}_{m}")).then_inc(s["taken_a"], 1)
                    for n in range(HEADS + 1):
                        if n < HEADS:
                            wait(act, s["max"], i * HEADS + n + 1)
                            wait(act, s["t_mm"], i * HEADS + n - 1)
                            for e in range(2):
                                op = act.activation(prob[n % 2][:, e, :], ps[:, n % 2, e * T:(e + 1) * T], ACT.Exp,
                                                    bias=nmax[n % 2][:, e:e + 1], accum_out=rsum[n % 2][:, e:e + 1])
                            op.then_inc(s["exp"], 1)
                        if n >= 1:
                            m = n - 1
                            wait(act, s["t_mm"], i * HEADS + m + 1)
                            wait(act, s["pv"], i * HEADS + m - 1)
                            act.copy(probt[m % 2][:], ps[:, 2 + m % 2, :].rearrange("p (a t) -> p a t", t=T)
                                     ).then_inc(s["pt"], 1)
                    norm(i, 2)
                    for m in range(MC):
                        wait(act, s["mm"], jobs.made(i, f"f{m}"))
                        act.activation(hid[:, m, :], bank(f"f{m}"), ACT.Gelu, bias=vec[:, b1 + m:b1 + m + 1]
                                       ).then_inc(s["taken_a"], 1)

                over_units(act, unit)

            @block.vector
            def _(dve):
                def norm(i, g, source):
                    mean, _, name = steps[g]
                    wait(dve, s["mm"], jobs.made(i, mean))
                    dve.tensor_tensor(xc[:], source[:], ps[:, jobs.bank(mean), None, :].to_broadcast([P, FC, N]),
                                      ALU.subtract).then_inc(s["taken_v"], 1)
                    wait(dve, s["rstd"], 2 * i + g)
                    wait(dve, s["taken_v"], jobs.taken(i, mean))
                    dve.tensor_tensor(xc[:], xc[:], rstd[:, None, :].to_broadcast([P, FC, N]), ALU.mult
                                      ).then_inc(s["xn"], 1)
                    wait(dve, s["xn"], 2 * i + g)
                    for m in range(FC):
                        for b in range(PAIR):
                            cols = slice(b * T, (b + 1) * T)
                            sc, sh = MOD[name + "_sc"] + m, MOD[name + "_sh"] + m
                            dve.tensor_scalar(h[:, m, cols], xc[:, m, cols], mb[:, b, sc:sc + 1], mb[:, b, sh:sh + 1],
                                              ALU.mult, ALU.add).then_inc(s["h"], 1)

                def residual(i, g, what, bias, dst, source, done):
                    for m in range(FC):
                        wait(dve, s["mm"], jobs.made(i, f"{what}{m}"))
                        wait(dve, s[done], 2 * i + m)
                        for b in range(PAIR):
                            cols = slice(b * T, (b + 1) * T)
                            ch = MOD[steps[g][2] + "_g"] + m
                            dve.tensor_scalar(tmp[:, cols], ps[:, jobs.bank(f"{what}{m}"), cols],
                                              vec[:, bias + m:bias + m + 1], mb[:, b, ch:ch + 1],
                                              ALU.add, ALU.mult).then_inc(s["taken_v"], 1)
                        wait(dve, s["taken_v"], jobs.taken(i, f"{what}{m}"))
                        dve.tensor_tensor(dst[:, m, :], tmp[:], source[:, m, :], ALU.add).then_inc(s[done], 1)

                if layer == 3:
                    dve.memset(qf[:], 0.0).then_inc(s["zero"], 1)
                    dve.wait_ge(s["zero"], 1)
                dve.memset(ones[:], 1.0 / D).then_inc(s["ones"], 1)

                def unit(i):
                    wait(dve, s["xo_done"], 2 * i)
                    dve.tensor_copy(mb[:], mod[:, :, bass.ds(PAIR * i, PAIR)].rearrange("p m b -> p b m")
                                    ).then_inc(s["vec_b"], 1)
                    wait(dve, s["x_in"], 16 * (i + 1))
                    wait(dve, s["vec_b"], i + 1)
                    norm(i, 1, x)
                    for w, dst in (("q", qf), ("k", kf)):
                        for m in range(MT):
                            name = f"{w}{m}"
                            wait(dve, s["mm"], jobs.made(i, name))
                            scale = SCALE if w == "q" else 1.0
                            at = VEC[f"b{w}3"][0] + m
                            if layer == 3 and w == "q":
                                for g in range(HT):
                                    lo, hi = HR * g, HR * (g + 1)
                                    op = dve.tensor_scalar(dst[lo:hi, m, g, :], ps[lo:hi, jobs.bank(name), :],
                                                           vec[lo:hi, at:at + 1], scale, ALU.add, ALU.mult)
                            elif layer == 3:
                                op = dve.tensor_scalar(dst[:, m, :], bank(name), vec[:, at:at + 1], scale,
                                                       ALU.add, ALU.mult)
                            else:
                                op = dve.tensor_scalar(dst[:, m, :], bank(name), scale, None, ALU.mult)
                            op.then_inc(s["taken_v"], 1)
                    for n in range(HEADS + 4):
                        if 1 <= n <= HEADS:
                            m = n - 1
                            wait(dve, s["exp"], i * HEADS + m + 1)
                            dve.reciprocal(rinv[m % 2][:], rsum[m % 2][:]).then_inc(s["recip"], 1)
                            wait(dve, s["recip"], i * HEADS + m + 1)
                            for e in range(2):
                                op = dve.tensor_scalar(prob[m % 2][:, e, :], prob[m % 2][:, e, :],
                                                       rinv[m % 2][:, e:e + 1], None, ALU.mult)
                            op.then_inc(s["norm"], 1)
                        if n < HEADS:
                            wait(dve, s["s_mm"], i * HEADS + n + 1)
                            wait(dve, s["exp"], i * HEADS + n - 1)
                            dve.tensor_reduce(nmax[n % 2][:], ps[:, n % 2, :].rearrange("p (a t) -> p a t", t=T),
                                              axis=AX.X, op=ALU.max, negate=True).then_inc(s["max"], 1)
                        m = n - 3
                        if 0 <= m < HEADS and m % HT == HT - 1:
                            tile = m // HT
                            wait(dve, s["pv"], i * HEADS + m + 1)
                            wait(dve, s["mm"], jobs.made(i, "proj1") - jobs.count)
                            b, col = tile // MT, tile % MT
                            out, src = o[:, col, b * T:(b + 1) * T], ps[:, 4 + tile % 2, 0:T]
                            if layer == 3:
                                at = VEC["bv3"][0] + col
                                op = dve.tensor_scalar(out, src, vec[:, at:at + 1], None, ALU.add)
                            else:
                                op = dve.tensor_copy(out, src)
                            op.then_inc(s["o_done"], 1)
                    residual(i, 1, "proj", bo, x2, x, "x2_done")
                    wait(dve, s["x2_done"], 2 * i + 2)
                    norm(i, 2, x2)
                    wait(dve, s["x_out"], 16 * i)
                    residual(i, 2, "out", b2, xo, x2, "xo_done")

                over_units(dve, unit)
    release(nc, sems)


def finish(nc, ctx, io, keep, scratch, out):
    finish_scan(nc, ctx, io, keep, scratch)
    transformer(nc, ctx, io, keep, scratch, 2, scratch["X2"], scratch["X4"])
    transformer(nc, ctx, io, keep, scratch, 3, scratch["X4"], out)


def program(nc, io, out):
    def dram(name, shape, dt=F32):
        return nc.dram_tensor(name, shape, dt, kind="Internal").ap()

    d3 = dram("D3", [2, IC, UNITS, PARTS, PAIR, T // TS, P, TS], BF16)
    u3 = dram("U3", [2, IC, UNITS, PARTS, PAIR, TC, P, P], BF16)
    b3 = dram("B3", [2, UNITS, PARTS, PARTS, PAIR, TC, P, PAIR * S], BF16)
    c2 = dram("C2", [2, UNITS, P, T, PAIR])
    y = dram("Y", [2, IC, UNITS, P, PAIR, T])
    scratch = {
        "A3": dram("A3", [2 * IC, PARTS, PARTS, PAIR, P, PAIR * S], BF16),
        "BB": dram("BB", [2, RANK, NB, D]),
        "X1": dram("X1", [UNITS, P, FC, N]), "X2": dram("X2", [UNITS, P, FC, N]),
        "X4": dram("X4", [UNITS, P, FC, N]),
        "SZ": dram("SZ", [2, UNITS, P, IC, N]), "SK": dram("SK", [2, UNITS, P, IC, N]),
        "D3": d3, "U3": u3, "B3": b3, "C2": c2, "Y": y,
        "D3f": d3.rearrange("r m i j b c d t -> (r m i) j b c d t"),
        "U3f": u3.rearrange("r m i j b c t d -> (r m i) j b c t d"),
        "B3f": b3.rearrange("r n i j b c t f -> (r n) i j b c t f"),
        "C2f": c2.rearrange("r i p t b -> (r i) p t b"),
        "Yf": y.rearrange("r m i p b t -> (r m i) p b t"),
    }
    with ExitStack() as ctx:
        def sb(name, shape, dt=F32):
            return ctx.enter_context(nc.sbuf_tensor(name, shape, dt))

        keep = {"vec": sb("vec", [P, NVEC]), "mod": sb("mod", [P, NMOD, NB]), "wa": sb("wa", [P, 32, NB]),
                "eps": sb("eps", [P, 1]), "mb": sb("mb", [P, PAIR, NMOD]),
                "wab": sb("wab", [P, PAIR, 2, RANK, FC])}
        conditioning(nc, ctx, io, keep, scratch)
        prepare(nc, ctx, io, keep, scratch)
        scan(nc, ctx, io, keep, scratch)
        finish(nc, ctx, io, keep, scratch, out)


def columns(v):
    return v.reshape(-1, P).T


def padded(v):
    v = v.reshape(v.shape[:-1] + (H, DH3))
    out = np.zeros(v.shape[:-1] + (PADH,), v.dtype)
    out[..., :DH3] = v
    return out.reshape(v.shape[:-2] + (H * PADH,))


def layout(a):
    def b2(q):
        w = q.reshape(q.shape[:-1] + (4, D, RANK))
        w = np.swapaxes(w, -1, -2)
        return (np.ascontiguousarray(w[..., 0::2, :, :]).reshape(q.shape[:-1] + (4096,)),
                np.ascontiguousarray(w[..., 1::2, :, :]).reshape(q.shape[:-1] + (4096,)))

    w2a, w2b = b2(a["L0_cond_W2"])
    b2a, b2b = b2(a["L0_cond_b2"])
    bq, bk, bv = (padded(v) for v in np.split(a["L3_cond_bqkv"], 3))
    wq, wk, wv = (padded(v) for v in np.split(a["L3_cond_Wqkv"], 3, axis=1))
    vecs = {"ln_g": a["L0_cond_ln_g"], "ln_b": a["L0_cond_ln_b"], "l0b1": a["L0_cond_b1"], "l0b2a": b2a,
            "mod_b": np.concatenate([a["L1_cond_adaln_mamba_b"], a["L1_cond_adaln_mlp_b"],
                                     a["L2_cond_b_mod"], a["L3_cond_bt"]]),
            "g1": a["L3_cond_g1"], "be1": a["L3_cond_be1"], "g2": a["L3_cond_g2"], "be2": a["L3_cond_be2"],
            "dtb0": a["L1_cond_fwd_dt_bias"], "dtb1": a["L1_cond_bwd_dt_bias"],
            "D0": a["L1_cond_fwd_D"], "D1": a["L1_cond_bwd_D"],
            "bo2": a["L2_cond_b_out"], "b12": a["L2_cond_b1"], "b22": a["L2_cond_b2"],
            "bq3": bq, "bk3": bk, "bv3": bv, "bo3": a["L3_cond_bproj"], "b13": a["L3_cond_b1"],
            "b23": a["L3_cond_b2"]}
    return {
        "vecs": np.concatenate([columns(vecs[n]) for n in VEC], axis=1),
        "condT": a["cond_1024"].reshape(NB, FC, P).transpose(2, 1, 0),
        "xT": a["x"].reshape(UNITS, PAIR, T, FC, P).transpose(0, 4, 3, 1, 2).reshape(UNITS, P, FC, N),
        "l0W1": a["L0_cond_W1"], "l0W2a": w2a, "l0W2b": w2b, "l0b2b": b2b.reshape(1, 4096),
        "mamba_w": a["L1_cond_adaln_mamba_w"], "mlp_w": a["L1_cond_adaln_mlp_w"],
        "W_mod": a["L2_cond_W_mod"], "Wt": a["L3_cond_Wt"],
        "A_log": np.concatenate([a["L1_cond_fwd_A_log"], a["L1_cond_bwd_A_log"]]),
        "in_w": np.stack([a["L1_cond_fwd_in_w"], a["L1_cond_bwd_in_w"]]),
        "xproj_w": np.stack([a["L1_cond_fwd_xproj_w"], a["L1_cond_bwd_xproj_w"]]),
        "out_w": np.stack([a["L1_cond_fwd_out_w"], a["L1_cond_bwd_out_w"]]),
        "mlp_w1": a["L1_cond_mlp_w1"], "mlp_w2": a["L1_cond_mlp_w2"], "mlp_w3": a["L1_cond_mlp_w3"],
        "Wqkv2": a["L2_cond_W_qkv"], "Wo2": a["L2_cond_W_out"], "W12": a["L2_cond_W1"], "W22": a["L2_cond_W2"],
        "Wqkv3": np.concatenate([wq, wk, wv], axis=1), "Wo3": padded(a["L3_cond_Wproj"].T).T,
        "W13": a["L3_cond_W1"], "W23": a["L3_cond_W2"],
    }


def kernel(**inputs):
    import concourse.bacc as bacc
    from concourse.bass_utils import run_bass_kernel_spmd

    nc = bacc.Bacc("TRN2", target_bir_lowering=False, num_devices=1)
    arrays = {"in_" + n: np.ascontiguousarray(v)
              for n, v in layout({n: np.asarray(v) for n, v in inputs.items()}).items()}
    io = {n[3:]: nc.dram_tensor(n, v.shape, mybir.dt.from_np(v.dtype), kind="ExternalInput").ap()
          for n, v in arrays.items()}
    out = nc.dram_tensor("out", [UNITS, P, FC, N], F32, kind="ExternalOutput").ap()
    program(nc, io, out)
    got = run_bass_kernel_spmd(nc, [arrays], core_ids=[0]).results[0]["out"]
    return np.ascontiguousarray(
        got.reshape(UNITS, P, FC, PAIR, T).transpose(0, 3, 4, 2, 1)).reshape(NB, T, D)
```
